# Optimizing a Trainium2 kernel written in Bass

```python
import numpy as np
import jax
import jax.numpy as jnp

def _softmax(x, axis=-1):
    return jax.nn.softmax(x, axis=axis)

def _gelu(x):
    return jax.nn.gelu(x, approximate=True)

def _silu(x):
    return jax.nn.silu(x)

def _sigmoid(x):
    return jax.nn.sigmoid(x)

def _layernorm(x, axis=-1, eps=1e-05):
    m = jnp.mean(x, axis=axis, keepdims=True)
    v = jnp.var(x, axis=axis, keepdims=True)
    return (x - m) / jnp.sqrt(v + eps)

def _scatter_add(tgt, idx, src, axis=0):
    return tgt.at[idx].add(src)

def _segment_sum(src, seg, n):
    return jax.ops.segment_sum(src, seg, n)
kernel_name = 'mk_adaln_d2_jaxref_r4_0eeb25'

def setup_inputs(seed: int=0):
    np.random.seed(seed)
    _w = jnp.asarray

    def _L0_attn_setup():
        import jax, jax.numpy as jnp
        import numpy as np
        H = 256
        F = 1024
        B, S = (4, 1024)
        EPS = 1e-05

        def _layernorm(x, scale, bias):
            mu = jnp.mean(x, axis=-1, keepdims=True)
            var = jnp.var(x, axis=-1, keepdims=True)
            return (x - mu) * jax.lax.rsqrt(var + EPS) * scale + bias
        key = jax.random.key(seed)
        ks = jax.random.split(key, 4)
        x = jax.random.normal(ks[0], (B, S, H), dtype=jnp.float32)
        W_ret = jax.random.normal(ks[1], (H, H), dtype=jnp.float32) * 0.02
        b_ret = jnp.zeros((H,), dtype=jnp.float32)
        ln1_scale = jnp.ones((H,), dtype=jnp.float32)
        ln1_bias = jnp.zeros((H,), dtype=jnp.float32)
        W1 = jax.random.normal(ks[2], (H, F), dtype=jnp.float32) * 0.02
        b1 = jnp.zeros((F,), dtype=jnp.float32)
        W2 = jax.random.normal(ks[3], (F, H), dtype=jnp.float32) * 0.02
        b2 = jnp.zeros((H,), dtype=jnp.float32)
        ln2_scale = jnp.ones((H,), dtype=jnp.float32)
        ln2_bias = jnp.zeros((H,), dtype=jnp.float32)
        return {'x': x, 'W_ret': W_ret, 'b_ret': b_ret, 'ln1_scale': ln1_scale, 'ln1_bias': ln1_bias, 'W1': W1, 'b1': b1, 'W2': W2, 'b2': b2, 'ln2_scale': ln2_scale, 'ln2_bias': ln2_bias}
    _L0_attn_in = _L0_attn_setup()

    def _L0_ffn_setup():
        import jax, jax.numpy as jnp
        import numpy as np
        import math
        B, L, D = (4, 1024, 256)
        F = 1024
        E = 16
        CAP_FACTOR = 1.0
        EPS = 1e-05
        key = jax.random.key(seed)
        ks = jax.random.split(key, 8)
        std = 0.02
        return {'x': jax.random.normal(ks[0], (B, L, D), dtype=jnp.float32), 'norm_weight': jnp.ones((D,), dtype=jnp.float32), 'router_weight': jax.random.normal(ks[1], (E, D), dtype=jnp.float32) * std, 'router_bias': jnp.zeros((E,), dtype=jnp.float32), 'fc1_weight': jax.random.normal(ks[2], (E, F, D), dtype=jnp.float32) * std, 'fc1_bias': jnp.zeros((E, F), dtype=jnp.float32), 'fc2_weight': jax.random.normal(ks[3], (E, D, F), dtype=jnp.float32) * std, 'fc2_bias': jnp.zeros((E, D), dtype=jnp.float32)}
    _L0_ffn_in = _L0_ffn_setup()
    _L0_c = _w((lambda *s: np.random.randn(*s).astype(np.float32) * 0.05)(16, 256))
    _L0_wmod = _w((lambda *s: np.random.randn(*s).astype(np.float32) * 0.05)(256, 6 * 256) * 256 ** (-0.5))

    def _L1_attn_setup():
        import jax, jax.numpy as jnp
        import numpy as np
        B, L, D, H, K = (8, 512, 256, 16, 31)
        D_CONV = D // H
        EPS = 1e-06
        key = jax.random.key(seed)
        ks = jax.random.split(key, 5)
        return {'x': jax.random.normal(ks[0], (B, L, D), dtype=jnp.float32), 'W_pe': jax.random.normal(ks[1], (D_CONV, 2 * K), dtype=jnp.float32) * 0.1, 'b_pe': jnp.zeros((2 * K,), dtype=jnp.float32), 'stt_energy': jnp.ones((1, H, 1, K), dtype=jnp.float32) + 0.02 * jax.random.normal(ks[2], (1, H, 1, K), dtype=jnp.float32), 'W_fc': jax.random.normal(ks[3], (D, D), dtype=jnp.float32) / jnp.sqrt(jnp.float32(D)), 'gamma': jnp.ones((D,), dtype=jnp.float32), 'beta': jnp.zeros((D,), dtype=jnp.float32)}
    _L1_attn_in = _L1_attn_setup()

    def _L1_ffn_setup():
        import jax, jax.numpy as jnp
        import numpy as np
        HIDDEN = 256
        INTER = 1024
        key = jax.random.key(seed)
        k1, k2, k3, k4, k5 = jax.random.split(key, 5)
        hidden_states = jax.random.normal(k1, (4, 512, HIDDEN), dtype=jnp.float32)
        W1 = jax.random.normal(k2, (HIDDEN, INTER), dtype=jnp.float32) * (1.0 / np.sqrt(HIDDEN))
        b1 = jax.random.normal(k3, (INTER,), dtype=jnp.float32) * 0.02
        W2 = jax.random.normal(k4, (INTER, HIDDEN), dtype=jnp.float32) * (1.0 / np.sqrt(INTER))
        b2 = jax.random.normal(k5, (HIDDEN,), dtype=jnp.float32) * 0.02
        return {'hidden_states': hidden_states, 'W1': W1, 'b1': b1, 'W2': W2, 'b2': b2}
    _L1_ffn_in = _L1_ffn_setup()
    _L1_c = _w((lambda *s: np.random.randn(*s).astype(np.float32) * 0.05)(16, 256))
    _L1_wmod = _w((lambda *s: np.random.randn(*s).astype(np.float32) * 0.05)(256, 6 * 256) * 256 ** (-0.5))
    _d = {'L0_attn_x': _L0_attn_in['x'], 'L0_attn_W_ret': _L0_attn_in['W_ret'], 'L0_attn_b_ret': _L0_attn_in['b_ret'], 'L0_attn_ln1_scale': _L0_attn_in['ln1_scale'], 'L0_attn_ln1_bias': _L0_attn_in['ln1_bias'], 'L0_attn_W1': _L0_attn_in['W1'], 'L0_attn_b1': _L0_attn_in['b1'], 'L0_attn_W2': _L0_attn_in['W2'], 'L0_attn_b2': _L0_attn_in['b2'], 'L0_attn_ln2_scale': _L0_attn_in['ln2_scale'], 'L0_attn_ln2_bias': _L0_attn_in['ln2_bias'], 'L0_ffn_norm_weight': _L0_ffn_in['norm_weight'], 'L0_ffn_router_weight': _L0_ffn_in['router_weight'], 'L0_ffn_router_bias': _L0_ffn_in['router_bias'], 'L0_ffn_fc1_weight': _L0_ffn_in['fc1_weight'], 'L0_ffn_fc1_bias': _L0_ffn_in['fc1_bias'], 'L0_ffn_fc2_weight': _L0_ffn_in['fc2_weight'], 'L0_ffn_fc2_bias': _L0_ffn_in['fc2_bias'], 'L0_c': _L0_c, 'L0_wmod': _L0_wmod, 'L1_attn_W_pe': _L1_attn_in['W_pe'], 'L1_attn_b_pe': _L1_attn_in['b_pe'], 'L1_attn_stt_energy': _L1_attn_in['stt_energy'], 'L1_attn_W_fc': _L1_attn_in['W_fc'], 'L1_attn_gamma': _L1_attn_in['gamma'], 'L1_attn_beta': _L1_attn_in['beta'], 'L1_ffn_W1': _L1_ffn_in['W1'], 'L1_ffn_b1': _L1_ffn_in['b1'], 'L1_ffn_W2': _L1_ffn_in['W2'], 'L1_ffn_b2': _L1_ffn_in['b2'], 'L1_c': _L1_c, 'L1_wmod': _L1_wmod}
    _x0 = _d['L0_attn_x']
    _d['L0_attn_x'] = jax.random.normal(jax.random.fold_in(jax.random.key(seed), 1), (16, 1024, 256), dtype=_x0.dtype)
    del _x0
    return _d

def reference(L0_attn_x, L0_attn_W_ret, L0_attn_b_ret, L0_attn_ln1_scale, L0_attn_ln1_bias, L0_attn_W1, L0_attn_b1, L0_attn_W2, L0_attn_b2, L0_attn_ln2_scale, L0_attn_ln2_bias, L0_ffn_norm_weight, L0_ffn_router_weight, L0_ffn_router_bias, L0_ffn_fc1_weight, L0_ffn_fc1_bias, L0_ffn_fc2_weight, L0_ffn_fc2_bias, L0_c, L0_wmod, L1_attn_W_pe, L1_attn_b_pe, L1_attn_stt_energy, L1_attn_W_fc, L1_attn_gamma, L1_attn_beta, L1_ffn_W1, L1_ffn_b1, L1_ffn_W2, L1_ffn_b2, L1_c, L1_wmod):

    def _L0_attn_ref(x, W_ret, b_ret, ln1_scale, ln1_bias, W1, b1, W2, b2, ln2_scale, ln2_bias):
        import jax, jax.numpy as jnp
        import numpy as np
        H = 256
        F = 1024
        B, S = (4, 1024)
        EPS = 1e-05

        def _layernorm(x, scale, bias):
            mu = jnp.mean(x, axis=-1, keepdims=True)
            var = jnp.var(x, axis=-1, keepdims=True)
            return (x - mu) * jax.lax.rsqrt(var + EPS) * scale + bias
        sig = jax.nn.sigmoid(jnp.einsum('bsh,hk->bsk', x, W_ret) + b_ret)

        def ema_step(carry, s_t):
            xi = 0.5 * s_t + 0.5 * carry
            return (xi, xi)
        _, ret = jax.lax.scan(ema_step, jnp.zeros((x.shape[0], x.shape[2]), x.dtype), jnp.transpose(sig, (1, 0, 2)))
        retention_output = jnp.transpose(ret, (1, 0, 2))
        h = _layernorm(x + retention_output, ln1_scale, ln1_bias)
        ffn = jnp.einsum('bsf,fh->bsh', jax.nn.gelu(jnp.einsum('bsh,hf->bsf', h, W1) + b1), W2) + b2
        out = _layernorm(h + ffn, ln2_scale, ln2_bias)
        return out

    def _L0_ffn_ref(x, norm_weight, router_weight, router_bias, fc1_weight, fc1_bias, fc2_weight, fc2_bias):
        import jax, jax.numpy as jnp
        import numpy as np
        import math
        B, L, D = (4, 1024, 256)
        F = 1024
        E = 16
        CAP_FACTOR = 1.0
        EPS = 1e-05
        b, l, d = x.shape
        n_tokens = b * l
        n_experts = router_weight.shape[0]
        capacity = max(1, math.ceil(CAP_FACTOR * n_tokens / n_experts))
        top_k = min(capacity, n_tokens)
        xf = x.reshape(n_tokens, d)
        rms = jnp.sqrt(jnp.mean(xf * xf, axis=-1, keepdims=True) + EPS)
        xn = xf / rms * norm_weight
        logits = xn @ router_weight.T + router_bias
        probs = jax.nn.softmax(logits, axis=-1)
        _, idx = jax.lax.top_k(logits.T, top_k)
        xe = xn[idx]
        h = jnp.einsum('ecd,efd->ecf', xe, fc1_weight) + fc1_bias[:, None, :]
        h = jax.nn.gelu(h, approximate=False)
        y = jnp.einsum('ecf,edf->ecd', h, fc2_weight) + fc2_bias[:, None, :]
        gates = jnp.take_along_axis(probs.T, idx, axis=1)
        flat_idx = idx.reshape(-1)
        contrib = (y * gates[:, :, None]).reshape(-1, d)
        output = jnp.zeros((n_tokens, d), dtype=x.dtype).at[flat_idx].add(contrib)
        gate_sums = jnp.zeros((n_tokens, 1), dtype=x.dtype).at[flat_idx].add(gates.reshape(-1, 1))
        assigned = gate_sums > 0
        output = jnp.where(assigned, output / jnp.where(assigned, gate_sums, 1.0), output)
        return output.reshape(b, l, d)

    def _L1_attn_ref(x, W_pe, b_pe, stt_energy, W_fc, gamma, beta):
        import jax, jax.numpy as jnp
        import numpy as np
        B, L, D, H, K = (8, 512, 256, 16, 31)
        D_CONV = D // H
        EPS = 1e-06
        b, l, d_model = x.shape
        d = d_model // H
        residual = x
        avg = jnp.cumsum(x, axis=1) / jnp.arange(1, l + 1, dtype=x.dtype)[None, :, None]
        ci = avg.reshape(b, l, H, d).transpose(0, 2, 1, 3).reshape(b * H, l, d)
        pc = ci @ W_pe + b_pe
        dyn, gate = (pc[..., :K], pc[..., K:])
        stt = jnp.broadcast_to(stt_energy, (b, H, 1, K)).reshape(b * H, 1, K)
        energy = stt + jax.nn.sigmoid(gate) * dyn
        w = jax.nn.softmax(energy, axis=-1)
        t_idx = jnp.arange(l)[:, None]
        k_idx = jnp.arange(K)[None, :]
        w = jnp.where(t_idx + k_idx - (K - 1) >= 0, w, jnp.zeros((), x.dtype))
        padded = jnp.pad(ci, ((0, 0), (K - 1, 0), (0, 0)))
        out = jnp.zeros((b * H, l, d), dtype=x.dtype)
        for kk in range(K):
            out = out + w[:, :, kk:kk + 1] * padded[:, kk:kk + l, :]
        conv_loc = out.reshape(b, H, l, d).transpose(0, 2, 1, 3).reshape(b, l, d_model)
        v = conv_loc @ W_fc.T + residual
        mu = jnp.mean(v, axis=-1, keepdims=True)
        var = jnp.var(v, axis=-1, keepdims=True)
        v = (v - mu) / jnp.sqrt(var + EPS) * gamma + beta
        return v

    def _L1_ffn_ref(hidden_states, W1, b1, W2, b2):
        import jax, jax.numpy as jnp
        import numpy as np
        HIDDEN = 256
        INTER = 1024
        h = jax.nn.relu(jnp.einsum('bsh,hi->bsi', hidden_states, W1) + b1)
        return jnp.einsum('bsi,ih->bsh', h, W2) + b2
    x = L0_attn_x
    mod = (_silu(L0_c) @ L0_wmod).reshape(L0_c.shape[0], 6, 1, -1)
    sa, ca, ga, sb, cb, gb = (mod[:, 0], mod[:, 1], mod[:, 2], mod[:, 3], mod[:, 4], mod[:, 5])
    ga = (2 * (ga >= 0) - 1) * jnp.maximum(jnp.abs(ga), 0.25)
    gb = (2 * (gb >= 0) - 1) * jnp.maximum(jnp.abs(gb), 0.25)
    h = _layernorm(x, axis=-1) * (1 + ca) + sa
    x = x + ga * _L0_attn_ref(h, L0_attn_W_ret, L0_attn_b_ret, L0_attn_ln1_scale, L0_attn_ln1_bias, L0_attn_W1, L0_attn_b1, L0_attn_W2, L0_attn_b2, L0_attn_ln2_scale, L0_attn_ln2_bias)
    h = _layernorm(x, axis=-1) * (1 + cb) + sb
    x = x + gb * _L0_ffn_ref(h, L0_ffn_norm_weight, L0_ffn_router_weight, L0_ffn_router_bias, L0_ffn_fc1_weight, L0_ffn_fc1_bias, L0_ffn_fc2_weight, L0_ffn_fc2_bias)
    mod = (_silu(L1_c) @ L1_wmod).reshape(L1_c.shape[0], 6, 1, -1)
    sa, ca, ga, sb, cb, gb = (mod[:, 0], mod[:, 1], mod[:, 2], mod[:, 3], mod[:, 4], mod[:, 5])
    ga = (2 * (ga >= 0) - 1) * jnp.maximum(jnp.abs(ga), 0.25)
    gb = (2 * (gb >= 0) - 1) * jnp.maximum(jnp.abs(gb), 0.25)
    h = _layernorm(x, axis=-1) * (1 + ca) + sa
    x = x + ga * _L1_attn_ref(h, L1_attn_W_pe, L1_attn_b_pe, L1_attn_stt_energy, L1_attn_W_fc, L1_attn_gamma, L1_attn_beta)
    h = _layernorm(x, axis=-1) * (1 + cb) + sb
    x = x + gb * _L1_ffn_ref(h, L1_ffn_W1, L1_ffn_b1, L1_ffn_W2, L1_ffn_b2)
    return x

_drawn_inputs = setup_inputs


def setup_inputs(seed=0):
    import zlib

    import numpy as np

    out = dict(_drawn_inputs(seed))
    spreads = {'L0_attn_b_ret': (0.0, 0.8),
     'L0_attn_ln1_scale': (1.0, 0.2),
     'L0_attn_ln1_bias': (0.0, 0.316),
     'L0_attn_b1': (0.0, 0.8),
     'L0_attn_b2': (0.0, 0.297),
     'L0_attn_ln2_scale': (1.0, 0.2),
     'L0_attn_ln2_bias': (0.0, 0.323),
     'L0_ffn_norm_weight': (1.0, 0.6),
     'L0_ffn_router_bias': (0.0, 0.8),
     'L0_ffn_fc1_bias': (0.0, 0.8),
     'L0_ffn_fc2_bias': (0.0, 0.463),
     'L1_attn_b_pe': (0.0, 2.0),
     'L1_attn_gamma': (1.0, 0.2),
     'L1_attn_beta': (0.0, 0.337)}
    factors = {'L0_attn_W_ret': 4.918,
     'L0_ffn_fc1_weight': 2.908,
     'L0_ffn_fc2_weight': 2.71,
     'L1_attn_W_pe': 171.882,
     'L1_attn_stt_energy': 200.0,
     'L1_attn_W_fc': 2.791,
     'L1_ffn_b1': 8.0,
     'L1_ffn_b2': 8.0}
    for name, (base, spread) in spreads.items():
        noise = np.random.default_rng([zlib.crc32(name.encode()), seed]).standard_normal(out[name].shape)
        drawn = base * np.exp(spread * noise) if base else spread * noise
        out[name] = jnp.asarray(drawn.astype(out[name].dtype))
    for name, factor in factors.items():
        out[name] = (out[name] * factor).astype(out[name].dtype)
    return out
```

```python
from contextlib import ExitStack

import concourse.bass as bass
from concourse import mybir

F32 = mybir.dt.float32
BF16 = mybir.dt.bfloat16
I32 = mybir.dt.int32
U32 = mybir.dt.uint32
ALU = mybir.AluOpType
ACT = mybir.ActivationFunctionType
AX_X = mybir.AxisListType.X

P = 128
BANK = 512


class Engine:

    def __init__(self, name, sem):
        self.name, self.sem, self.count, self.queue, self.reached = name, sem, 0, [], {}

    def wait(self, *tokens):
        for token in tokens:
            if token is None:
                continue
            if isinstance(token, list):
                self.wait(*token)
                continue
            sem, value, key = token
            if self.reached.get(key, 0) < value:
                self.reached[key] = value
                self.queue.append(lambda e, s=sem, v=value: e.wait_ge(s, v))

    def quiet(self, instruction, *tokens):
        self.wait(*tokens)
        self.queue.append(instruction)

    def do(self, instruction, *tokens):
        self.wait(*tokens)
        self.count += 1
        self.queue.append(lambda e: instruction(e).then_inc(self.sem, 1))
        return (self.sem, self.count, self.name)

    def last(self):
        return (self.sem, self.count, self.name) if self.count else None

    def replay(self, e):
        for instruction in self.queue:
            instruction(e)


class Lane:

    def __init__(self, name, sem):
        self.name, self.sem, self.count = name, sem, 0

    def send(self, engine, instruction, *tokens):
        engine.wait(*tokens)
        self.count += 16
        engine.queue.append(lambda e: instruction(e).then_inc(self.sem, 16))
        return (self.sem, self.count, self.name)

    def last(self):
        return (self.sem, self.count, self.name) if self.count else None


class Ring:

    def __init__(self, buffers):
        self.buffers, self.free = buffers, [[] for _ in buffers]

    def __getitem__(self, i):
        return self.buffers[i % len(self.buffers)]

    def idle(self, i):
        return self.free[i % len(self.buffers)]

    def used(self, i, *tokens):
        self.free[i % len(self.buffers)] = list(tokens)


class Core:

    def __init__(self, nc, ctx):
        self.nc, self.ctx, self.lanes, self.names = nc, ctx, {}, {}
        self.pe, self.act, self.dve, self.pool, self.sp = (
            Engine(n, ctx.enter_context(nc.semaphore("done_" + n))) for n in ("pe", "act", "dve", "pool", "sp"))
        self.engines = [self.pe, self.act, self.dve, self.pool, self.sp]
        self.banks = Ring([ctx.enter_context(nc.psum_tensor(f"bank{i}", [P, BANK], F32)) for i in range(8)])

    def lane(self, name):
        if name not in self.lanes:
            self.lanes[name] = Lane(name, self.ctx.enter_context(self.nc.semaphore("dma_" + name)))
        return self.lanes[name]

    def tile(self, ctx, name, shape, dt=F32):
        self.names[name] = self.names.get(name, 0) + 1
        if self.names[name] > 1:
            name = f"{name}_v{self.names[name]}"
        return ctx.enter_context(self.nc.sbuf_tensor(name, shape, dt))

    def ring(self, ctx, name, n, shape, dt=F32):
        return Ring([self.tile(ctx, f"{name}{i}", shape, dt) for i in range(n)])

    def everyone_waits_for_everyone(self):
        ends = [e.last() for e in self.engines] + [lane.last() for lane in self.lanes.values()]
        for e in self.engines:
            e.wait(*[t for t in ends if t is not None])


def pipeline(count, schedule):
    for step in range(count + max(lag for _, lag in schedule)):
        for stage, lag in schedule:
            if 0 <= step - lag < count:
                stage(step - lag)


def inverse_root(core, scratch, variance, eps, *tokens):
    dve = core.dve
    v, half, t, y = (scratch[:, i, :] for i in range(4))
    a = dve.do(lambda e: e.tensor_scalar(v, variance, eps, None, ALU.add), *tokens)
    dve.quiet(lambda e: e.tensor_scalar(half, variance, -0.5, -0.5 * eps, ALU.mult, ALU.add))
    a = dve.do(lambda e: e.tensor_scalar(t.bitcast(I32), v.bitcast(I32), 1, None, ALU.logical_shift_right), a)
    a = dve.do(lambda e: e.tensor_scalar(y.bitcast(I32), t.bitcast(I32), -1.0, float(0x5F3759DF), ALU.mult, ALU.add), a)
    for _ in range(3):
        a = dve.do(lambda e: e.tensor_tensor(t, y, y, ALU.mult), a)
        a = dve.do(lambda e: e.tensor_tensor(t, t, half, ALU.mult), a)
        a = dve.do(lambda e: e.scalar_tensor_tensor(out=y, in0=t, scalar=1.5, in1=y, op0=ALU.add, op1=ALU.mult), a)
    return y, a


def statistics(core, stats, moments, source, n, eps, scratch, *tokens):
    dve = core.dve
    for i in range(n):
        a = dve.do(lambda e, i=i: e.bn_stats(stats[:, i, :], source(i)), *(tokens if i == 0 else ()))
    for i in range(n):
        a = dve.do(lambda e, i=i: e.bn_aggr(moments[:, i, :], stats[:, i, :]), a)
    return inverse_root(core, scratch, moments[:, 0:n, 1], eps, a)


def transpose_into(core, bank, columns, source, ident, wait, rows=P):
    for i in range(columns):
        core.pe.wait(*wait)
        wait = ()
        step = (lambda e, i=i: e.transpose(bank[:, i * rows:(i + 1) * rows], source(i), ident[0:rows, 0:rows]))
        token = core.pe.do(step) if i == columns - 1 else core.pe.quiet(step)
    return token


def build(nc, A, out, debug=None):
    B, S, D = A["L0_attn_x"].shape
    T = B * S
    F = A["L0_attn_W1"].shape[1]
    E = A["L0_ffn_router_weight"].shape[0]
    CAP = T // E
    KD, KF = D // P, F // P
    NM = 6 * D
    HEADS, KW = A["L1_attn_stt_energy"].shape[1], A["L1_attn_stt_energy"].shape[3]
    assert D == 2 * P and S == 1024 and CAP == 1024 and E == 16

    ctx = ExitStack()
    with ctx:
        core = Core(nc, ctx)
        pe, act, dve, pool, sp = core.engines
        banks = core.banks

        x1_dram = nc.dram_tensor("x_after_retention", [T, D], F32, kind="Internal").ap()
        xn_dram = nc.dram_tensor("moe_input", [T, D], F32, kind="Internal").ap()
        logit_dram = nc.dram_tensor("router_logits", [E, T], F32, kind="Internal").ap()
        moe_dram = nc.dram_tensor("moe_output", [T, D], F32, kind="Internal").ap()
        gate_dram = nc.dram_tensor("gates", [T, E], F32, kind="Internal").ap()
        row0_dram = nc.dram_tensor("rows_layer0", [B, 4 * D], F32, kind="Internal").ap()
        row1_dram = nc.dram_tensor("rows_layer1", [B, 5 * D], F32, kind="Internal").ap()
        TILE_T = 96
        NT = -(-S // TILE_T)
        BAND_SIZE = 1568 * P
        assert BAND_SIZE >= (TILE_T + 1) * (P + 1) * HEADS
        band_dram = [nc.dram_tensor(f"bands{i}", [NT, BAND_SIZE], F32, kind="Internal").ap() for i in range(2)]

        ident = core.tile(ctx, "ident", [P, P])
        cols = core.tile(ctx, "mod_columns", [P, 12, B])
        zero = core.tile(ctx, "zero", [P, BAND_SIZE // P])
        pool.do(lambda e: e.memset(ident[:, :], 0.0))
        zero_ready = pool.do(lambda e: e.memset(zero[:, :], 0.0))
        ident_ready = pool.do(lambda e: e.affine_select(
            out=ident[:, :], in_=ident[:, :], compare_op=ALU.not_equal, fill=1.0, base=0,
            pattern=[[-1, P]], channel_multiplier=1), pool.last())

        SHIFT0, SCALE0, SHIFT1A, SCALE1A, SHIFT1B, SCALE1B = range(0, 12, 2)
        with ExitStack() as part:
            rows_sent = []
            mod = [core.tile(part, f"mod{l}", [B, NM]) for l in range(2)]
            for l in range(2):
                cT = core.tile(part, f"cT{l}", [P, KD, B])
                th = core.tile(part, f"c_tanh{l}", [P, KD, B])
                sc = core.tile(part, f"c_silu{l}", [P, KD, B])
                wm = core.tile(part, f"wmod{l}", [P, KD, NM])
                lane = core.lane(f"cond{l}")
                lane.send(sp, lambda e, l=l, cT=cT: e.dma_start(cT[:, :, :], A[f"L{l}_cT"].rearrange("(k p) b -> p k b", p=P)))
                got = lane.send(sp, lambda e, l=l, wm=wm: e.dma_start(wm[:, :, :], A[f"L{l}_wmod"].rearrange("(k p) n -> p k n", p=P)))
                a = act.do(lambda e, th=th, cT=cT: e.activation(th[:, :, :], cT[:, :, :], ACT.Tanh, scale=0.5), got)
                a = dve.do(lambda e, th=th, cT=cT: e.scalar_tensor_tensor(
                    out=th[:, :, :], in0=th[:, :, :], scalar=1.0, in1=cT[:, :, :], op0=ALU.add, op1=ALU.mult), a)
                a = dve.do(lambda e, th=th, sc=sc: e.tensor_scalar(sc[:, :, :], th[:, :, :], 0.5, None, ALU.mult), a)
                for n in range(NM // BANK):
                    u = 3 * l + n
                    for k in range(KD):
                        step = (lambda e, u=u, n=n, k=k, sc=sc, wm=wm: e.matmul(
                            banks[u][0:B, :], sc[:, k, :], wm[:, k, n * BANK:(n + 1) * BANK], start=k == 0, stop=k == KD - 1))
                        m = pe.do(step, a, got)
                    a2 = dve.do(lambda e, u=u, n=n, l=l: e.tensor_copy(mod[l][:, n * BANK:(n + 1) * BANK], banks[u][0:B, :]), m)
                    banks.used(u, a2)

            def field(l, i):
                return mod[l][:, i * D:(i + 1) * D]

            a = dve.last()
            work = core.tile(part, "mod_work", [B, 4, D])
            for l in range(2):
                for i in (2, 5):
                    g, s, m = field(l, i), work[:, 0, :], work[:, 1, :]
                    b = dve.do(lambda e, g=g, m=m: e.tensor_scalar(m, g, -1.0, None, ALU.mult), a)
                    b = dve.do(lambda e, g=g, m=m: e.tensor_tensor(m, m, g, ALU.max), b)
                    b = dve.do(lambda e, m=m: e.tensor_scalar(m, m, 0.25, None, ALU.max), b)
                    b = dve.do(lambda e, g=g, s=s: e.tensor_scalar(s, g, 0.0, 2.0, ALU.is_ge, ALU.mult), b)
                    b = dve.do(lambda e, s=s: e.tensor_scalar(s, s, -1.0, None, ALU.add), b)
                    a = dve.do(lambda e, g=g, s=s, m=m: e.tensor_tensor(g, s, m, ALU.mult), b)
                for i in (1, 4):
                    a = dve.do(lambda e, l=l, i=i: e.tensor_scalar(field(l, i), field(l, i), 1.0, None, ALU.add), a)
            vec = core.tile(part, "vectors_by_batch", [B, 5, D])
            for i, name in enumerate(["L0_attn_ln2_scale", "L0_attn_ln2_bias", "L1_attn_gamma", "L1_attn_beta", "L1_ffn_b2"]):
                got = core.lane("vectors").send(sp, lambda e, i=i, name=name: e.dma_start(
                    vec[:, i, :], A[name].rearrange("(a d) -> a d", a=1).to_broadcast([B, D])))
            rows0 = core.tile(part, "rows0", [B, 4, D])
            rows1 = core.tile(part, "rows1", [B, 5, D])
            dve.wait(a, got)
            dve.quiet(lambda e: e.tensor_tensor(rows0[:, 0, :], field(0, 2), vec[:, 0, :], ALU.mult))
            dve.quiet(lambda e: e.tensor_tensor(rows0[:, 1, :], field(0, 2), vec[:, 1, :], ALU.mult))
            dve.quiet(lambda e: e.tensor_copy(rows0[:, 2, :], field(0, 4)))
            a = dve.do(lambda e: e.tensor_copy(rows0[:, 3, :], field(0, 3)))
            rows_sent.append(core.lane("rows").send(sp, lambda e: e.dma_start(row0_dram, rows0[:, :, :].rearrange("b a d -> b (a d)")), a))
            dve.quiet(lambda e: e.tensor_copy(rows1[:, 0, :], field(0, 5)))
            dve.quiet(lambda e: e.tensor_tensor(rows1[:, 1, :], field(1, 2), vec[:, 2, :], ALU.mult))
            dve.quiet(lambda e: e.tensor_tensor(rows1[:, 2, :], field(1, 2), vec[:, 3, :], ALU.mult))
            dve.quiet(lambda e: e.tensor_copy(rows1[:, 3, :], field(1, 5)))
            a = dve.do(lambda e: e.tensor_tensor(rows1[:, 4, :], field(1, 5), vec[:, 4, :], ALU.mult))
            rows_sent.append(core.lane("rows").send(sp, lambda e: e.dma_start(row1_dram, rows1[:, :, :].rearrange("b a d -> b (a d)")), a))
            blocks = [(0, 0), (0, 1), (1, 0), (1, 1), (1, 3), (1, 4)]
            for n, (l, i) in enumerate(blocks):
                for k in range(KD):
                    step = (lambda e, n=n, l=l, i=i, k=k: e.transpose(
                        banks[6][:, (2 * n + k) * B:(2 * n + k + 1) * B], field(l, i)[:, k * P:(k + 1) * P], ident[0:B, 0:B]))
                    m = pe.do(step, a, ident_ready)
            a = dve.do(lambda e: e.tensor_copy(cols[:, :, :].rearrange("p n b -> p (n b)"), banks[6][:, 0:12 * B]), m)
            banks.used(6, a)
            core.everyone_waits_for_everyone()

        g = dict(B=B, S=S, D=D, T=T, F=F, E=E, CAP=CAP, KD=KD, KF=KF, HEADS=HEADS, KW=KW, TILE_T=TILE_T, NT=NT, BAND_SIZE=BAND_SIZE,
                 ident=ident, cols=cols, zero=zero, zero_ready=zero_ready,
                 SHIFT0=SHIFT0, SCALE0=SCALE0, SHIFT1A=SHIFT1A, SCALE1A=SCALE1A, SHIFT1B=SHIFT1B, SCALE1B=SCALE1B,
                 x1_dram=x1_dram, xn_dram=xn_dram, logit_dram=logit_dram, moe_dram=moe_dram, gate_dram=gate_dram,
                 row0_dram=row0_dram, row1_dram=row1_dram, band_dram=band_dram, out=out)
        retention(core, A, g)
        if debug != "A":
            experts(core, A, g)
            if debug != "M":
                layer_one(core, A, g)
        core.everyone_waits_for_everyone()

        block = ctx.enter_context(nc.Block())
        block.tensor(lambda e: pe.replay(e))
        block.scalar(lambda e: act.replay(e))
        block.vector(lambda e: dve.replay(e))
        block.gpsimd(lambda e: pool.replay(e))
        block.sync(lambda e: sp.replay(e))


def retention(core, A, g):
    pe, act, dve, pool, sp = core.engines
    banks, ident, cols = core.banks, g["ident"], g["cols"]
    B, S, D, T, F, E, KD, KF = (g[n] for n in ("B", "S", "D", "T", "F", "E", "KD", "KF"))
    GT = BANK
    C = GT // P
    N = T // GT
    PER = S // GT
    x_dram = A["L0_attn_x"].rearrange("b (h c p) d -> (b h) p c d", c=C, p=P)
    x1_dram = g["x1_dram"].rearrange("(n c p) d -> n p c d", c=C, p=P)
    xn_dram = g["xn_dram"].rearrange("(n c p) d -> n p c d", c=C, p=P)

    with ExitStack() as part:
        def tile(name, shape, dt=F32):
            return core.tile(part, name, shape, dt)

        def ring(name, n, shape):
            return core.ring(part, name, n, shape)

        w_ret, w1, w2 = tile("w_ret", [P, KD, D]), tile("w1", [P, KD, F]), tile("w2", [P, KF, D])
        w_router = tile("w_router", [P, KD, E])
        ret_bias, ln1_scale, ln1_bias, b1 = (tile(n, [P, k]) for n, k in (("ret_bias", KD), ("ln1_scale", KD), ("ln1_bias", KD), ("b1", KF)))
        router_bias = tile("router_bias", [E, 1])
        b2_row, nw_row = tile("b2_row", [P, D]), tile("nw_row", [P, D])
        half = tile("half", [P, GT])
        x, rows = ring("x", 6, [P, C, D]), ring("rows", 2, [P, 4, D])
        xh, h1T, th, q, r = ring("xh", 1, [P, C, D]), ring("h1T", 2, [P, KD, GT]), ring("th", 1, [P, KD, GT]), ring("q", 2, [P, KD, GT]), ring("r", 2, [P, KD, GT])
        xh2, hT, act_T = ring("xh2", 1, [P, C, D]), ring("hT", 2, [P, KD, GT]), ring("gT", 2, [P, KF, GT])
        v, x1, h2, xn, xnT = (ring(n, k, [P, C, D]) for n, k in (("v", 2), ("x1_", 2), ("h2_", 2), ("xn", 2), ("xnT", 1)))
        square = tile("square", [P, D])
        lg = ring("lg", 2, [E, GT])
        stats, moments = tile("stats", [P, C, 6]), tile("moments", [P, C, 2])
        scratch = tile("scratch", [P, 4, C])
        sumsq = ring("sumsq", 2, [P, C])

        lane = core.lane("weights")
        for dst, src in ((w_ret[:, :, :], A["L0_attn_W_ret"].rearrange("(k p) n -> p k n", p=P)),
                         (w1[:, :, :], A["L0_attn_W1"].rearrange("(k p) n -> p k n", p=P)),
                         (w2[:, :, :], A["L0_attn_W2"].rearrange("(k p) n -> p k n", p=P)),
                         (w_router[:, :, :], A["L0_ffn_router_wT"].rearrange("(k p) n -> p k n", p=P)),
                         (ret_bias[:, :], A["L0_attn_b_ret_c"]), (ln1_scale[:, :], A["L0_attn_ln1_scale_c"]),
                         (ln1_bias[:, :], A["L0_attn_ln1_bias_c"]), (b1[:, :], A["L0_attn_b1_c"]),
                         (router_bias[:, :], A["L0_ffn_router_bias"].rearrange("(e a) -> e a", a=1)),
                         (b2_row[:, :], A["L0_attn_b2"].rearrange("(a d) -> a d", a=1).to_broadcast([P, D])),
                         (nw_row[:, :], A["L0_ffn_norm_weight"].rearrange("(a d) -> a d", a=1).to_broadcast([P, D]))):
            weights = lane.send(sp, lambda e, dst=dst, src=src: e.dma_start(dst, src))
        half_ready = dve.do(lambda e: e.memset(half[:, :], 0.5))
        bias_ready = dve.do(lambda e: e.tensor_scalar(ret_bias[:, :], ret_bias[:, :], 0.5, None, ALU.mult), weights)

        got_x, got_rows, done = {}, {}, {}

        def load(i):
            got_x[i] = core.lane(f"x{i % 6}").send(sp, lambda e: e.dma_start(x[i][:, :, :], x_dram[i]), x.idle(i))
            zl = core.lane("zeros")
            zl.send(sp, lambda e: e.dma_start(g["moe_dram"].rearrange("(n p c) d -> n p (c d)", p=P, c=C)[i],
                                              g["zero"][:, 0:C * D]), g["zero_ready"])
            if i < 2 * g["NT"]:
                size = g["BAND_SIZE"] // P
                zl.send(sp, lambda e: e.dma_start(g["band_dram"][i % 2][i // 2].rearrange("(p c) -> p c", p=P), g["zero"][:, 0:size]))

        def load_rows(i):
            if i % PER == 0:
                b = i // PER
                got_rows[b] = core.lane(f"rows{b % 2}").send(sp, lambda e: e.dma_start(
                    rows[b][:, :, :].rearrange("p a d -> p (a d)"), g["row0_dram"][b:b + 1, :].to_broadcast([P, 4 * D])), rows.idle(b))

        def norm_in(i):
            y, a = statistics(core, stats, moments, lambda c: x[i][:, c, :], C, 1e-5, scratch, got_x[i])
            dve.wait(a, xh.idle(i))
            for c in range(C):
                a = dve.do(lambda e, c=c: e.tensor_scalar(xh[i][:, c, :], x[i][:, c, :], moments[:, c, 0:1], y[:, c:c + 1],
                                                          ALU.subtract, ALU.mult))
            done["xh", i] = a

        def pair(n):
            return (0, 1) if n % 2 == 0 else (2, 3)

        uses = [0]

        def next_pair():
            uses[0] += 1
            return pair(uses[0])

        def to_features(i, source, ready, write):
            for k, u in enumerate(next_pair()):
                t = transpose_into(core, banks[u], C, lambda c, k=k: source[:, c, k * P:(k + 1) * P], ident, [ready, banks.idle(u)])
                banks.used(u, write(k, banks[u], t))
            return t

        def modulate(i):
            b = i // PER

            def write(k, bank, t):
                a = act.do(lambda e: e.activation(h1T[i][:, k, :], bank[:, :], ACT.Identity,
                                                  scale=cols[:, g["SCALE0"] + k, b:b + 1], bias=cols[:, g["SHIFT0"] + k, b:b + 1]), t, h1T.idle(i))
                done["h1T", i] = a
                return a
            t = to_features(i, xh[i], done["xh", i], write)
            xh.used(i, t)

        def retain(i):
            for k, u in enumerate(next_pair()):
                for j in range(KD):
                    m = pe.do(lambda e, j=j, k=k, u=u: e.matmul(banks[u][:, :], w_ret[:, j, k * P:(k + 1) * P], h1T[i][:, j, :],
                                                                start=j == 0, stop=j == KD - 1), done["h1T", i], weights, banks.idle(u))
                a = act.do(lambda e, k=k, u=u: e.activation(th[i][:, k, :], banks[u][:, :], ACT.Tanh, bias=ret_bias[:, k:k + 1], scale=0.5),
                           m, bias_ready, th.idle(i))
                banks.used(u, a)
                a = pool.do(lambda e, k=k: e.tensor_scalar(th[i][:, k, :], th[i][:, k, :], 1.0, None, ALU.add), a)
                start = 0.0 if i % PER == 0 else q[i - 1][:, k, GT - 1:GT]
                a = dve.do(lambda e, k=k, start=start: e.tensor_tensor_scan(
                    q[i][:, k, :], half[:, :], th[i][:, k, :], start, ALU.mult, ALU.add), a, half_ready, done.get(("q", i - 1)))
                if k == KD - 1:
                    th.used(i, a)
                    done["q", i] = a
                a = dve.do(lambda e, k=k: e.scalar_tensor_tensor(out=r[i][:, k, :], in0=q[i][:, k, :], scalar=0.25, in1=h1T[i][:, k, :],
                                                                 op0=ALU.mult, op1=ALU.add), a, r.idle(i))
            done["r", i] = a
            h1T.used(i, a, m)

        def norm_mid(i):
            pairs = next_pair()
            for c in range(C):
                u = pairs[c // 2]
                for k in range(KD):
                    col = (c % 2) * D + k * P
                    m = pe.do(lambda e, c=c, k=k, u=u, col=col: e.transpose(banks[u][:, col:col + P], r[i][:, k, c * P:(c + 1) * P], ident[:, :]),
                              done["r", i], banks.idle(u))
            r.used(i, m)
            chunk = lambda c: banks[pairs[c // 2]][:, (c % 2) * D:(c % 2 + 1) * D]
            y, a = statistics(core, stats, moments, chunk, C, 1e-5, scratch, m)
            dve.wait(a, xh2.idle(i))
            for c in range(C):
                a = dve.do(lambda e, c=c: e.tensor_scalar(xh2[i][:, c, :], chunk(c), moments[:, c, 0:1], y[:, c:c + 1], ALU.subtract, ALU.mult))
            for u in pairs:
                banks.used(u, a)
            done["xh2", i] = a

        def affine_mid(i):
            def write(k, bank, t):
                a = act.do(lambda e: e.activation(hT[i][:, k, :], bank[:, :], ACT.Identity,
                                                  scale=ln1_scale[:, k:k + 1], bias=ln1_bias[:, k:k + 1]), t, hT.idle(i))
                done["hT", i] = a
                return a
            xh2.used(i, to_features(i, xh2[i], done["xh2", i], write))

        def expand(i, fs):
            for f in fs:
                u = 4 + f % 2
                for k in range(KD):
                    step = (lambda e, f=f, k=k, u=u: e.matmul(banks[u][:, :], w1[:, k, f * P:(f + 1) * P], hT[i][:, k, :],
                                                              start=k == 0, stop=k == KD - 1))
                    m = pe.do(step, done["hT", i], banks.idle(u))
                a = act.do(lambda e, f=f, u=u: e.activation(act_T[i][:, f, :], banks[u][:, :], ACT.Gelu_apprx_tanh, bias=b1[:, f:f + 1]),
                           m, act_T.idle(i))
                banks.used(u, a)
            done["gT", i] = a

        def contract(i, c):
            u = 6 + c % 2
            for f in range(KF):
                pe.quiet(lambda e, f=f: e.matmul(banks[u][:, 0:D], act_T[i][:, f, c * P:(c + 1) * P], w2[:, f, :], start=f == 0, stop=False),
                         done["gT", i], banks.idle(u))
            for k in range(KD):
                m = pe.do(lambda e, k=k: e.matmul(banks[u][:, k * P:(k + 1) * P], hT[i][:, k, c * P:(c + 1) * P], ident[:, :],
                                                  start=False, stop=k == KD - 1))
            if c == C - 1:
                act_T.used(i, m)
                hT.used(i, m)
            a = dve.do(lambda e: e.tensor_tensor(v[i][:, c, :], banks[u][:, 0:D], b2_row[:, :], ALU.add), m, v.idle(i))
            banks.used(u, a)
            done["v", i] = a

        def bcast(b, row):
            return rows[b][:, row:row + 1, :].to_broadcast([P, C, D])

        def norm_out(i):
            b = i // PER
            y, a = statistics(core, stats, moments, lambda c: v[i][:, c, :], C, 1e-5, scratch, done["v", i])
            for c in range(C):
                a = dve.do(lambda e, c=c: e.tensor_scalar(v[i][:, c, :], v[i][:, c, :], moments[:, c, 0:1], y[:, c:c + 1],
                                                          ALU.subtract, ALU.mult), a)
            pool.do(lambda e: e.tensor_tensor(x1[i][:, :, :], x[i][:, :, :], bcast(b, 1), ALU.add), got_x[i], got_rows[b], x1.idle(i))
            a = pool.do(lambda e: e.tensor_tensor(v[i][:, :, :], v[i][:, :, :], bcast(b, 0), ALU.mult), a)
            x.used(i, a)
            done["t1", i] = a

        def residual(i):
            b = i // PER
            a = dve.do(lambda e: e.tensor_tensor(x1[i][:, :, :], x1[i][:, :, :], v[i][:, :, :], ALU.add), done["t1", i])
            v.used(i, a)
            sent = core.lane(f"x1_{i % 2}").send(sp, lambda e: e.dma_start(x1_dram[i], x1[i][:, :, :]), a)
            y, a = statistics(core, stats, moments, lambda c: x1[i][:, c, :], C, 1e-5, scratch, a)
            dve.wait(h2.idle(i))
            for c in range(C):
                a = dve.do(lambda e, c=c: e.tensor_scalar(h2[i][:, c, :], x1[i][:, c, :], moments[:, c, 0:1], y[:, c:c + 1],
                                                          ALU.subtract, ALU.mult), a)
            x1.used(i, sent, a)
            a = pool.do(lambda e: e.tensor_tensor(h2[i][:, :, :], h2[i][:, :, :], bcast(b, 2), ALU.mult), a, got_rows[b])
            a = pool.do(lambda e: e.tensor_tensor(h2[i][:, :, :], h2[i][:, :, :], bcast(b, 3), ALU.add), a)
            rows.used(b, a)
            done["h2", i] = a

        def squares(i):
            a = act.last()
            for c in range(C):
                a = act.do(lambda e, c=c: e.activation(square[:, :], h2[i][:, c, :], ACT.Square, scale=D ** -0.5,
                                                       accum_out=sumsq[i][:, c:c + 1]), a, done["h2", i], sumsq.idle(i))
            done["sumsq", i] = a

        def rms_norm(i):
            y, a = inverse_root(core, scratch, sumsq[i][:, :], 1e-5, done["sumsq", i])
            dve.wait(xn.idle(i))
            for c in range(C):
                a = dve.do(lambda e, c=c: e.scalar_tensor_tensor(out=xn[i][:, c, :], in0=h2[i][:, c, :], scalar=y[:, c:c + 1],
                                                                 in1=nw_row[:, :], op0=ALU.mult, op1=ALU.mult), a)
            sumsq.used(i, a)
            h2.used(i, a)
            done["xn", i] = a

        def turn_out(i):
            def write(k, bank, t):
                done["xnT", i] = act.do(lambda e: e.copy(xnT[i][:, k * 2:k * 2 + 2, :].rearrange("p a d -> p (a d)"), bank[:, :]), t, xnT.idle(i))
                return done["xnT", i]
            t = to_features(i, xn[i], done["xn", i], write)
            sent = core.lane(f"xn{i % 2}").send(sp, lambda e: e.dma_start(xn_dram[i], xn[i][:, :, :]), done["xn", i])
            xn.used(i, t, sent)

        def route(i):
            u, _ = next_pair()
            for k in range(KD):
                m = pe.do(lambda e, k=k: e.matmul(banks[u][0:E, :], w_router[:, k, :], xnT[i][:, k * 2:k * 2 + 2, :].rearrange("p a d -> p (a d)"),
                                                  start=k == 0, stop=k == KD - 1), done["xnT", i], banks.idle(u))
            xnT.used(i, m)
            a = act.do(lambda e: e.activation(lg[i][:, :], banks[u][0:E, :], ACT.Identity, bias=router_bias[:, 0:1]), m, lg.idle(i))
            banks.used(u, a)
            sent = core.lane(f"lg{i % 2}").send(sp, lambda e: e.dma_start(g["logit_dram"][:, i * GT:(i + 1) * GT], lg[i][:, :]), a)
            lg.used(i, sent)

        pipeline(N, [
            (load, 0), (load_rows, 3), (norm_in, 1), (squares, 6), (modulate, 1),
            (lambda i: contract(i, 0), 4), (lambda i: contract(i, 1), 4), (norm_mid, 2),
            (rms_norm, 6), (lambda i: contract(i, 2), 4), (lambda i: contract(i, 3), 4), (retain, 1),
            (lambda i: expand(i, (0, 1, 2)), 3), (affine_mid, 2), (residual, 5), (norm_out, 4),
            (lambda i: expand(i, (3, 4)), 3), (turn_out, 6), (lambda i: expand(i, (5, 6, 7)), 3), (route, 6),
        ])
        core.everyone_waits_for_everyone()


def find_threshold(core, part, L, block_ones, ready):
    pe, act, dve, pool, sp = core.engines
    thr, trial, keep = (core.tile(part, n, [P, 1], U32) for n in ("thr", "trial", "keep"))
    count = core.tile(part, "count", [P, 1])
    hits = core.tile(part, "hits", [P, L.shape[1]], BF16)
    bank = core.banks[0]

    def enough(a, wanted):
        a = dve.do(lambda e: e.tensor_scalar(hits[:, :], L[:, :], trial[:, :].bitcast(F32), None, ALU.is_ge, ALU.add,
                                             accum_out=count[:, :]), a, ready)
        m = pe.do(lambda e: e.matmul(bank[:, 0:1], block_ones[:, :], count[:, :], start=True, stop=True), a, core.banks.idle(0))
        return dve.do(lambda e: e.tensor_scalar(keep[:, :], bank[:, 0:1], float(wanted) - 0.5, None, ALU.is_ge), m)

    wanted = 1024
    a = dve.do(lambda e: e.memset(trial[:, :].bitcast(F32), 0.0))
    a = enough(a, wanted)
    a = dve.do(lambda e: e.tensor_scalar(trial[:, :], keep[:, :], 1, None, ALU.bitwise_xor), a)
    a = dve.do(lambda e: e.tensor_scalar(thr[:, :].bitcast(I32), trial[:, :].bitcast(I32), 31, 31, ALU.logical_shift_left,
                                         ALU.arith_shift_right), a)
    for bit in range(30, -1, -1):
        a = dve.do(lambda e, bit=bit: e.tensor_scalar(trial[:, :], thr[:, :], 1 << bit, None, ALU.bitwise_xor), a)
        a = enough(a, wanted)
        a = dve.do(lambda e, bit=bit: e.scalar_tensor_tensor(out=thr[:, :], in0=keep[:, :], scalar=bit, in1=thr[:, :],
                                                             op0=ALU.logical_shift_left, op1=ALU.bitwise_xor), a)
    core.banks.used(0, a)
    return thr[:, :].bitcast(F32), a


def experts(core, A, g):
    pe, act, dve, pool, sp = core.engines
    banks, ident = core.banks, g["ident"]
    D, T, F, E, KD, KF, CAP = (g[n] for n in ("D", "T", "F", "E", "KD", "KF", "CAP"))
    G = P // E
    W = T // G
    CH = W // P
    NONE = 4096
    PER_BANK = BANK // P
    HT = CAP // 2
    C = HT // P
    NI = 2 * E

    with ExitStack() as part:
        def tile(name, shape, dt=F32):
            return core.tile(part, name, shape, dt)

        def ring(name, n, shape, dt=F32):
            return core.ring(part, name, n, shape, dt)

        block_ones, block_below = tile("block_ones", [P, P]), tile("block_below", [P, P])
        iota_p, iota_q, token_low = tile("iota_p", [P, P], BF16), tile("iota_q", [P, G], BF16), tile("token_low", [P, 1])
        token_high = tile("token_high", [P, CH, G], BF16)
        b1 = tile("fc1_bias", [P, E, KF])
        L = tile("logits", [P, W])
        f1, f2, f3 = tile("work1", [P, W]), tile("work2", [P, W]), tile("work3", [P, W])
        slot_i = tile("slot_i", [P, CH, E, G], I32)
        slot_p, slot_q = tile("slot_p", [P, CH, E, G], BF16), tile("slot_q", [P, CH, E, G], BF16)
        small = tile("small", [P, 8])
        xg, gg = ring("xg", 2, [P, C, D]), ring("gg", 4, [P, C, E])
        xgT, hidden = ring("xgT", 2, [P, KD, HT]), ring("hidden", 2, [P, KF, HT])
        w1, w2, b2_row = ring("fc1", 2, [P, KD, F]), ring("fc2", 2, [P, KF, D]), ring("fc2_bias", 2, [P, D])
        y, ys = ring("y", 2, [P, D]), ring("ys", 2, [P, C, D])
        PC = 2
        onehot_p, onehot_q = ring("onehot_p", 4, [P, PC, G, P], BF16), ring("onehot_q", 4, [P, PC, G, 2 * G], BF16)
        eq_q = ring("eq_q", 2, [P, PC, G, G], BF16)
        parts = ring("id_parts", 2, [P, 2 * G])
        idx = ring("idx", 4, [P, G], U32)

        lane = core.lane("routing_in")
        for dst, src in ((L[:, :], g["logit_dram"].rearrange("e (g t) -> (e g) t", g=G)),
                         (block_ones[:, :], A["block_ones"]), (block_below[:, :], A["block_below"]), (f1[:, 0:P], A["iota_row"]),
                         (small[:, 0:1], A["iota_column"]), (f2[:, 0:P], A["chunk_ids"]),
                         (b1[:, :, :], A["L0_ffn_fc1_bias_c"].rearrange("p (e k) -> p e k", e=E))):
            ready = lane.send(sp, lambda e, dst=dst, src=src: e.dma_start(dst, src))
        done = {}

        def load_weights(e_):
            lane = core.lane(f"expert_w{e_ % 2}")
            for dst, src in ((w1[e_][:, :, :], A["L0_ffn_fc1_wT"][e_].rearrange("(k p) n -> p k n", p=P)),
                             (w2[e_][:, :, :], A["L0_ffn_fc2_wT"][e_].rearrange("(k p) n -> p k n", p=P)),
                             (b2_row[e_][:, :], A["L0_ffn_fc2_bias"][e_:e_ + 1, :].to_broadcast([P, D]))):
                done["w", e_] = lane.send(sp, lambda e, dst=dst, src=src: e.dma_start(dst, src), w1.idle(e_))
        load_weights(0)

        dve.quiet(lambda e: e.tensor_copy(iota_p[:, :], f1[:, 0:P]), ready)
        dve.quiet(lambda e: e.tensor_copy(iota_q[:, :], f1[:, 0:G]))
        dve.quiet(lambda e: e.tensor_copy(token_low[:, :], small[:, 0:1]))
        dve.do(lambda e: e.tensor_copy(token_high[:, :, :].rearrange("p c g -> p (c g)"), f2[:, 0:P]))
        limit, a = find_threshold(core, part, L, block_ones, ready)

        above, ties, tied_before, tie_room, counts, base = (small[:, i:i + 1] for i in range(1, 7))
        greater, equal, running = f1, f2, f3
        dve.wait(a)
        a = dve.do(lambda e: e.tensor_scalar(greater[:, :], L[:, :], limit, None, ALU.is_gt, ALU.add, accum_out=above), a)
        a = dve.do(lambda e: e.tensor_scalar(equal[:, :], L[:, :], limit, None, ALU.is_equal, ALU.add, accum_out=ties))
        m = pe.do(lambda e: e.matmul(banks[0][:, 0:1], block_ones[:, :], above, start=True, stop=True), a, banks.idle(0))
        m = pe.do(lambda e: e.matmul(banks[1][:, 0:1], block_below[:, :], ties, start=True, stop=True), banks.idle(1))
        b = dve.do(lambda e: e.tensor_copy(tied_before, banks[1][:, 0:1]), m)
        b = dve.do(lambda e: e.scalar_tensor_tensor(out=tie_room, in0=banks[0][:, 0:1], scalar=-float(CAP), in1=tied_before,
                                                    op0=ALU.add, op1=ALU.add), b)
        tie_a = dve.do(lambda e: e.tensor_scalar(tie_room, tie_room, -1.0, None, ALU.mult), b)
        a = dve.do(lambda e: e.tensor_tensor_scan(running[:, :], equal[:, :], equal[:, :], 0.0, ALU.add, ALU.max), tie_a)
        a = dve.do(lambda e: e.scalar_tensor_tensor(out=equal[:, :], in0=running[:, :], scalar=tie_room, in1=equal[:, :],
                                                    op0=ALU.is_le, op1=ALU.mult), a)
        taken = greater
        a = dve.do(lambda e: e.tensor_tensor(taken[:, :], greater[:, :], equal[:, :], ALU.add), a)
        a = dve.do(lambda e: e.tensor_tensor_scan(running[:, :], taken[:, :], taken[:, :], 0.0, ALU.add, ALU.max), a)
        m = pe.do(lambda e: e.matmul(banks[0][:, 0:1], block_below[:, :], running[:, W - 1:W], start=True, stop=True), a)
        a = dve.do(lambda e: e.tensor_scalar(base, banks[0][:, 0:1], -1.0 - NONE, None, ALU.add), m)
        banks.used(0, a)
        banks.used(1, a)
        a = dve.do(lambda e: e.scalar_tensor_tensor(out=running[:, :], in0=running[:, :], scalar=base, in1=taken[:, :],
                                                    op0=ALU.add, op1=ALU.mult), a)
        for n in range(CH // PER_BANK):
            t = transpose_into(core, banks[n], PER_BANK, lambda c, n=n: running[:, (n * PER_BANK + c) * P:(n * PER_BANK + c + 1) * P],
                               ident, [a, banks.idle(n)])
            b = dve.do(lambda e, n=n: e.tensor_scalar(slot_i[:, n * PER_BANK:(n + 1) * PER_BANK, :, :].rearrange("p c e g -> p (c e g)"),
                                                      banks[n][:, :], float(NONE), None, ALU.add), t)
            banks.used(n, b)
        flat = lambda x: x[:, :, :, :].rearrange("p c e g -> p (c e g)")
        fi = f1[:, :].bitcast(I32)
        b = dve.do(lambda e: e.tensor_scalar(fi, flat(slot_i), P - 1, None, ALU.bitwise_and), b)
        b = dve.do(lambda e: e.tensor_copy(flat(slot_p), fi), b)
        b = dve.do(lambda e: e.tensor_scalar(fi, flat(slot_i), P.bit_length() - 1, None, ALU.logical_shift_right), b)
        slots_ready = dve.do(lambda e: e.tensor_copy(flat(slot_q), fi), b)

        def make_gates():
            probs, kept = f2, f1
            view = lambda x: x[:, :].rearrange("p (c e g) -> p c e g", e=E, g=G)
            over_e = lambda x: x[:, :].rearrange("p (c e g) -> p c g e", e=E, g=G)
            row = gate_row
            bc = lambda x: x[:, :, :].unsqueeze(2).to_broadcast([P, CH, E, G])
            for n in range(CH // PER_BANK):
                u = n % 2
                t = transpose_into(core, banks[u], PER_BANK, lambda c, n=n: L[:, (n * PER_BANK + c) * P:(n * PER_BANK + c + 1) * P],
                                   ident, [banks.idle(u)])
                b = dve.do(lambda e, n=n, u=u: e.tensor_copy(probs[:, n * BANK:(n + 1) * BANK], banks[u][:, :]), t)
                banks.used(u, b)
            b = dve.do(lambda e: e.tensor_reduce(row[:, :, :], over_e(probs), AX_X, ALU.max), b)
            b = dve.do(lambda e: e.tensor_tensor(view(probs), view(probs), bc(row), ALU.subtract), b)
            b = act.do(lambda e: e.activation(probs[:, :], probs[:, :], ACT.Exp), b)
            b = dve.do(lambda e: e.tensor_reduce(row[:, :, :], over_e(probs), AX_X, ALU.add), b)
            b = dve.do(lambda e: e.reciprocal(row[:, :, :], row[:, :, :]), b)
            b = dve.do(lambda e: e.tensor_tensor(view(probs), view(probs), bc(row), ALU.mult), b)
            b = dve.do(lambda e: e.tensor_scalar(kept[:, :], flat(slot_i), float(NONE), None, ALU.is_lt), b)
            b = dve.do(lambda e: e.tensor_tensor(probs[:, :], probs[:, :], kept[:, :], ALU.mult), b)
            b = dve.do(lambda e: e.tensor_reduce(row[:, :, :], over_e(probs), AX_X, ALU.add), b)
            b = dve.do(lambda e: e.scalar_tensor_tensor(out=row[:, :, :], in0=row[:, :, :], scalar=0.0, in1=row[:, :, :],
                                                        op0=ALU.is_le, op1=ALU.add), b)
            b = dve.do(lambda e: e.reciprocal(row[:, :, :], row[:, :, :]), b)
            order = kept[:, :].rearrange("p (g c e) -> p c e g", g=G, c=CH)
            b = dve.do(lambda e: e.tensor_tensor(order, view(probs), bc(row), ALU.mult), b)
            done["gates"] = core.lane("gates").send(sp, lambda e: e.dma_start(
                g["gate_dram"].rearrange("(n p) e -> p n e", p=P), kept[:, :].rearrange("p (n e) -> p n e", e=E)), b)

        gate_row = tile("gate_row", [P, CH, G])

        PIECES = CH // 2 // PC

        def mark(i, piece):
            x, n = i // 2, i * PIECES + piece
            c0 = (i % 2) * CH // 2 + piece * PC
            cs = slice(c0, c0 + PC)
            shape = [P, PC, G]
            of = lambda t, n: t[:, cs, x, :].unsqueeze(3).to_broadcast(shape + [n])
            b = dve.do(lambda e: e.tensor_tensor(eq_q[n][:, :, :, :], iota_q[:, :].unsqueeze(1).unsqueeze(1).to_broadcast(shape + [G]),
                                                 of(slot_q, G), ALU.is_equal), slots_ready, eq_q.idle(n))
            dve.do(lambda e: e.tensor_tensor(onehot_p[n][:, :, :, :], iota_p[:, :].unsqueeze(1).unsqueeze(1).to_broadcast(shape + [P]),
                                             of(slot_p, P), ALU.is_equal), onehot_p.idle(n))
            a = dve.do(lambda e: e.tensor_tensor(onehot_q[n][:, :, :, 0:G], eq_q[n][:, :, :, :],
                                                 token_high[:, cs, :].unsqueeze(3).to_broadcast(shape + [G]), ALU.mult), b, onehot_q.idle(n))
            a = dve.do(lambda e: e.tensor_scalar(onehot_q[n][:, :, :, G:2 * G], eq_q[n][:, :, :, :], token_low[:, 0:1], None, ALU.mult))
            eq_q.used(n, a)
            done["marked", n] = a

        def listing(i, piece):
            x, h, n = i // 2, i % 2, i * PIECES + piece
            u = 2 + x % 2
            opening, closing = h == 0 and piece == 0, h == 1 and piece == PIECES - 1
            for c in range(PC):
                for gr in range(G):
                    end = c == PC - 1 and gr == G - 1
                    step = (lambda e, c=c, gr=gr, first=opening and c == 0 and gr == 0, final=closing and end: e.matmul(
                        banks[u][:, 0:2 * G], onehot_p[n][:, c, gr, :], onehot_q[n][:, c, gr, :], start=first, stop=final))
                    if end:
                        m = pe.do(step)
                    else:
                        pe.quiet(step, done["marked", n], banks.idle(u) if opening else None)
            onehot_p.used(n, m)
            onehot_q.used(n, m)
            if closing:
                b = act.do(lambda e: e.copy(parts[x][:, :], banks[u][:, 0:2 * G]), m)
                banks.used(u, b)
                done["idx", x] = dve.do(lambda e: e.scalar_tensor_tensor(out=idx[x][:, :], in0=parts[x][:, 0:G], scalar=float(P),
                                                                         in1=parts[x][:, G:2 * G], op0=ALU.mult, op1=ALU.add), b, idx.idle(x))

        def fetch(i):
            x, h = i // 2, i % 2
            if i == 0:
                make_gates()
            pool.wait(done["idx", x], xg.idle(i))
            for c in range(C):
                col = idx[x][:, h * C + c:h * C + c + 1]
                done["xg", i] = core.lane(f"xg{i % 2}").send(pool, lambda e, c=c, col=col: e.indirect_dma_start(
                    xg[i][:, c, :], None, g["xn_dram"], bass.IndirectOffsetOnAxis(ap=col, axis=0)))

        def next_weights(i):
            if i % 2 == 0 and i // 2 + 1 < E:
                load_weights(i // 2 + 1)

        def fetch_gates(i):
            x, h = i // 2, i % 2
            pool.wait(done["gates"], gg.idle(i))
            for c in range(C):
                col = idx[x][:, h * C + c:h * C + c + 1]
                done["gg", i] = core.lane(f"gg{i % 4}").send(pool, lambda e, c=c, col=col: e.indirect_dma_start(
                    gg[i][:, c, :], None, g["gate_dram"], bass.IndirectOffsetOnAxis(ap=col, axis=0)))

        def turn(i):
            for k in range(KD):
                t = transpose_into(core, banks[k], C, lambda c, k=k: xg[i][:, c, k * P:(k + 1) * P], ident, [done["xg", i], banks.idle(k)])
                a = act.do(lambda e, k=k: e.copy(xgT[i][:, k, :], banks[k][:, :]), t, xgT.idle(i))
                banks.used(k, a)
            xg.used(i, t)
            done["xgT", i] = a

        def expand(i, fs):
            x = i // 2
            for f in fs:
                u = 4 + f % 2
                for k in range(KD):
                    m = pe.do(lambda e, f=f, k=k, u=u: e.matmul(banks[u][:, :], w1[x][:, k, f * P:(f + 1) * P], xgT[i][:, k, :],
                                                                start=k == 0, stop=k == KD - 1), done["xgT", i], done["w", x], banks.idle(u))
                a = act.do(lambda e, f=f, u=u: e.activation(hidden[i][:, f, :], banks[u][:, :], ACT.Gelu, bias=b1[:, x, f:f + 1]), m, hidden.idle(i))
                banks.used(u, a)
            xgT.used(i, m)
            done["hidden", i] = a

        def contract(i, c):
            x, h = i // 2, i % 2
            u = 6 + c % 2
            for f in range(KF):
                step = (lambda e, f=f: e.matmul(banks[u][:, 0:D], hidden[i][:, f, c * P:(c + 1) * P], w2[x][:, f, :], start=f == 0, stop=f == KF - 1))
                if f == KF - 1:
                    m = pe.do(step)
                else:
                    pe.quiet(step, done["hidden", i], banks.idle(u))
            a = dve.do(lambda e: e.tensor_tensor(y[c][:, :], banks[u][:, 0:D], b2_row[x][:, :], ALU.add), m, y.idle(c))
            banks.used(u, a)
            b = act.do(lambda e: e.activation(ys[i][:, c, :], y[c][:, :], ACT.Copy, scale=gg[i][:, c, x:x + 1]), a, done["gg", i], ys.idle(i))
            y.used(c, b)
            if c == C - 1:
                hidden.used(i, m)
                w1.used(x, m, a)
                gg.used(i, b)
                done["ys", i] = b

        def scatter(i):
            x, h = i // 2, i % 2
            pool.wait(done["ys", i], done.get(("sc", 2 * x - 1)), done.get(("sc", 2 * x - 2)))
            for c in range(C):
                col = idx[x][:, h * C + c:h * C + c + 1]
                done["sc", i] = core.lane(f"sc{i % 4}").send(pool, lambda e, c=c, col=col: e.indirect_dma_start(
                    g["moe_dram"], bass.IndirectOffsetOnAxis(ap=col, axis=0), ys[i][:, c, :], None, compute_op=ALU.add))
            ys.used(i, done["sc", i])
            if h == 1:
                idx.used(x, done["sc", i], done["sc", i - 1])

        pipeline(NI, [
            (next_weights, 5), (fetch, 2), (fetch_gates, 3), (lambda i: mark(i, 0), 0), (turn, 3), (lambda i: contract(i, 0), 5), (lambda i: mark(i, 1), 0),
            (lambda i: contract(i, 1), 5), (lambda i: listing(i, 0), 0), (lambda i: mark(i, 2), 0), (lambda i: contract(i, 2), 5),
            (lambda i: expand(i, (0, 1)), 4), (lambda i: mark(i, 3), 0), (lambda i: listing(i, 1), 0), (lambda i: contract(i, 3), 5),
            (scatter, 5), (lambda i: expand(i, (2, 3)), 4), (lambda i: listing(i, 2), 0),
            (lambda i: expand(i, tuple(range(4, KF))), 4), (lambda i: listing(i, 3), 0),
        ])
        core.everyone_waits_for_everyone()


def layer_one(core, A, g):
    pe, act, dve, pool, sp = core.engines
    banks, ident, cols = core.banks, g["ident"], g["cols"]
    B, S, D, T, KD, H, KW, TT, NT = (g[n] for n in ("B", "S", "D", "T", "KD", "HEADS", "KW", "TILE_T", "NT"))
    F = A["L1_ffn_W1"].shape[1]
    KF = F // P
    C = S // P
    HC = C // 2
    HD = D // H
    PAD = P - TT
    HJ = P // HD
    BC = 4
    x1_dram = g["x1_dram"].rearrange("(b c p) d -> b p c d", c=C, p=P)
    moe_dram = g["moe_dram"].rearrange("(b c p) d -> b p c d", c=C, p=P)
    out_dram = g["out"].rearrange("b (c p) d -> b c p d", p=P)

    with ExitStack() as part:
        def tile(name, shape, dt=F32):
            return core.tile(part, name, shape, dt)

        def ring(name, n, shape):
            return core.ring(part, name, n, shape)

        w_fc, w1, w2 = tile("w_fc", [P, KD, D]), tile("l1_w1", [P, KD, F]), tile("l1_w2", [P, KF, D])
        w_pe = tile("w_pe", [P, 2, HJ, KW])
        pe_bias, energy = tile("pe_bias", [P, 2, KW]), tile("energy", [P, H, KW])
        b1, per_count = tile("l1_b1", [P, KF]), tile("per_count", [P, S])
        x2, moe, xh, v = ring("x2_", 3, [P, C, D]), ring("moe", 1, [P, C, D]), ring("l1_xh", 1, [P, C, D]), ring("l1_v", 1, [P, C, D])
        row_in, row_mid, row_out = ring("row_in", 1, [P, D]), ring("row_mid", 1, [P, 2, D]), ring("row_out", 1, [P, 2, D])
        h3T, avgT = ring("h3T", 2, [P, KD, S]), ring("avgT", 2, [P, KD, PAD + S + PAD])
        convT, h4T, hidden = ring("convT", 1, [P, KD, S]), ring("h4T", 2, [P, KD, S]), ring("l1_hidden", 1, [P, KF, BANK])
        pc, gate, w = ring("pc", 1, [P, 2, H, KW]), ring("gate", 1, [P, H, KW]), ring("w", 2, [P, KW, H])
        e1 = ring("e1", 2, [P, H, KW])
        top, total = ring("top", 2, [P, H]), ring("total", 2, [P, H])
        band, bandT = ring("band", 2, [TT, P, H]), ring("bandT", 2, [P, H, TT])
        window, conv = ring("window", 2, [P, D]), ring("conv", 2, [TT, D])
        o = ring("o", 2, [P, D])
        stats, moments, scratch = tile("l1_stats", [P, C, 6]), tile("l1_moments", [P, C, 2]), tile("l1_scratch", [P, 4, C])

        a = pool.do(lambda e: e.memset(w_pe[:, :, :, :], 0.0))
        lane = core.lane("l1_weights")
        loads = [(w_fc[:, :, :], A["L1_attn_W_fcT"].rearrange("(k p) n -> p k n", p=P)),
                 (w1[:, :, :], A["L1_ffn_W1"].rearrange("(k p) n -> p k n", p=P)),
                 (w2[:, :, :], A["L1_ffn_W2"].rearrange("(k p) n -> p k n", p=P)),
                 (pe_bias[:, :, :].rearrange("p a k -> p (a k)"), A["L1_attn_b_pe"].rearrange("(a d) -> a d", a=1).to_broadcast([P, 2 * KW])),
                 (energy[:, :, :].rearrange("p h k -> p (h k)"), A["L1_attn_stt_energy"].rearrange("a h b k -> (a b) (h k)").to_broadcast([P, H * KW])),
                 (b1[:, :], A["L1_ffn_b1_c"]), (per_count[:, :], A["per_count"].to_broadcast([P, S]))]
        loads += [(w_pe[j * HD:(j + 1) * HD, :, j, :], A["L1_attn_W_pe"].rearrange("d (a k) -> d a k", a=2)) for j in range(HJ)]
        for dst, src in loads:
            weights = lane.send(sp, lambda e, dst=dst, src=src: e.dma_start(dst, src), a)
        for i in range(2):
            pool.quiet(lambda e, i=i: e.memset(avgT[i][:, :, 0:PAD], 0.0))
            pads_ready = pool.do(lambda e, i=i: e.memset(avgT[i][:, :, PAD + S:], 0.0))
        done = {}

        def load(b):
            done["x1", b] = core.lane(f"l1_x{b % 3}").send(sp, lambda e: e.dma_start(x2[b][:, :, :], x1_dram[b]), x2.idle(b))
            lane = core.lane("l1_moe")
            lane.send(sp, lambda e: e.dma_start(moe[b][:, :, :], moe_dram[b]), moe.idle(b))
            done["moe", b] = lane.send(sp, lambda e: e.dma_start(row_in[b][:, :], g["row1_dram"][b:b + 1, 0:D].to_broadcast([P, D])), row_in.idle(b))

        def norm_in(b):
            bc = row_in[b][:, :].unsqueeze(1).to_broadcast([P, C, D])
            a = pool.do(lambda e: e.tensor_tensor(moe[b][:, :, :], moe[b][:, :, :], bc, ALU.mult), done["moe", b])
            row_in.used(b, a)
            a = dve.do(lambda e: e.tensor_tensor(x2[b][:, :, :], x2[b][:, :, :], moe[b][:, :, :], ALU.add), a, done["x1", b])
            moe.used(b, a)
            y, a = statistics(core, stats, moments, lambda c: x2[b][:, c, :], C, 1e-5, scratch, a)
            dve.wait(xh.idle(b))
            for c in range(C):
                a = dve.do(lambda e, c=c: e.tensor_scalar(xh[b][:, c, :], x2[b][:, c, :], moments[:, c, 0:1], y[:, c:c + 1], ALU.subtract, ALU.mult), a)
            done["xh", b] = a

        def turn_in(b, half):
            for k in range(KD):
                u = k
                t = transpose_into(core, banks[u], HC, lambda c, k=k: xh[b][:, half * HC + c, k * P:(k + 1) * P], ident, [done["xh", b], banks.idle(u)])
                a = act.do(lambda e, k=k, u=u: e.activation(h3T[b][:, k, half * BANK:(half + 1) * BANK], banks[u][:, :], ACT.Identity,
                                                            scale=cols[:, g["SCALE1A"] + k, b:b + 1], bias=cols[:, g["SHIFT1A"] + k, b:b + 1]), t, h3T.idle(b))
                banks.used(u, a)
            if half == 1:
                xh.used(b, t)
            done["h3T", b] = a

        def average(b):
            for k in range(KD):
                view = avgT[b][:, k, PAD:PAD + S]
                a = dve.do(lambda e, k=k, view=view: e.tensor_tensor_scan(view, h3T[b][:, k, :], g["zero"][:, 0:S], 0.0, ALU.add, ALU.add),
                           done["h3T", b], avgT.idle(b), weights)
                a = dve.do(lambda e, view=view: e.tensor_tensor(view, view, per_count[:, :], ALU.mult), a)
            done["avgT", b] = a

        def kernels_a(b, c):
            n = b * C + c
            for j in range(KD):
                u = j
                m = pe.do(lambda e, j=j, u=u: e.matmul(banks[u][:, 0:2 * HJ * KW], avgT[b][:, j, PAD + c * P:PAD + (c + 1) * P],
                                                       w_pe[:, :, :, :].rearrange("p a j k -> p (a j k)"), start=True, stop=True),
                          done["avgT", b], weights, banks.idle(u))
                a = dve.do(lambda e, j=j, u=u: e.tensor_tensor(
                    pc[n][:, :, j * HJ:(j + 1) * HJ, :], banks[u][:, 0:2 * HJ * KW].rearrange("p (a j k) -> p a j k", a=2, j=HJ),
                    pe_bias[:, :, :].unsqueeze(2).to_broadcast([P, 2, HJ, KW]), ALU.add), m, pc.idle(n))
                banks.used(u, a)
            a = act.do(lambda e: e.activation(gate[n][:, :, :], pc[n][:, 1, :, :], ACT.Tanh, scale=0.5), a, gate.idle(n))
            a = dve.do(lambda e: e.scalar_tensor_tensor(out=e1[n][:, :, :], in0=gate[n][:, :, :], scalar=1.0, in1=pc[n][:, 0, :, :],
                                                        op0=ALU.add, op1=ALU.mult), a, e1.idle(n))
            pc.used(n, a)
            gate.used(n, a)
            a = dve.do(lambda e: e.scalar_tensor_tensor(out=e1[n][:, :, :], in0=e1[n][:, :, :], scalar=0.5, in1=energy[:, :, :],
                                                        op0=ALU.mult, op1=ALU.add), a)
            a = dve.do(lambda e: e.tensor_reduce(top[n][:, :], e1[n][:, :, :], AX_X, ALU.max), a, top.idle(n))
            a = pool.do(lambda e: e.tensor_tensor(e1[n][:, :, :], e1[n][:, :, :], top[n][:, :].unsqueeze(2).to_broadcast([P, H, KW]), ALU.subtract), a)
            top.used(n, a)
            done["exp", n] = act.do(lambda e: e.activation(e1[n][:, :, :], e1[n][:, :, :], ACT.Exp), a)

        def kernels_b(b, c):
            n = b * C + c
            a = dve.do(lambda e: e.tensor_reduce(total[n][:, :], e1[n][:, :, :], AX_X, ALU.add), done["exp", n])
            a = dve.do(lambda e: e.reciprocal(total[n][:, :], total[n][:, :]), a)
            a = dve.do(lambda e: e.tensor_tensor(w[n][:, :, :].rearrange("p k h -> p h k"), e1[n][:, :, :],
                                                 total[n][:, :].unsqueeze(2).to_broadcast([P, H, KW]), ALU.mult), a, w.idle(n))
            e1.used(n, a)
            row = (P + 1) * H
            t = c * P
            while t < (c + 1) * P:
                i, tt = t // TT, t % TT
                rows = min(TT - tt, (c + 1) * P - t)
                off = tt * row + (PAD - KW + 1) * H
                dst = g["band_dram"][b % 2][i:i + 1, off:off + rows * row].rearrange("a (n r) -> (a n) r", r=row)[:, 0:KW * H]
                src = w[n][t - c * P:t - c * P + rows, :, :].rearrange("p k h -> p (k h)")
                sent = core.lane(f"w{n % 2}").send(sp, lambda e, dst=dst, src=src: e.dma_start(dst, src), a, done.get(("band", b - 2, i)))
                t += rows
            w.used(n, sent)
            done["w", b, c] = sent

        def load_band(b, i):
            n = b * NT + i
            chunks = range(i * TT // P, min(C - 1, (i * TT + TT - 1) // P) + 1)
            done["band", b, i] = core.lane(f"band{n % 2}").send(sp, lambda e: e.dma_start(
                band[n][:, :, :].rearrange("t s h -> t (s h)"), g["band_dram"][b % 2][i:i + 1, 0:TT * P * H].rearrange("a (t r) -> (a t) r", t=TT)),
                band.idle(n), *[done["w", b, c] for c in chunks])

        def band_turn(b, i):
            n = b * NT + i
            for q in range(H // BC):
                u = q % 2
                for j in range(BC):
                    h = q * BC + j
                    t = pe.do(lambda e, h=h, j=j, u=u: e.transpose(banks[u][:, j * TT:(j + 1) * TT], band[n][:, :, h], ident[0:TT, 0:TT]),
                              done["band", b, i], banks.idle(u))
                if q % 2 == 0:
                    a = act.do(lambda e, q=q, u=u: e.copy(bandT[n][:, q * BC:(q + 1) * BC, :].rearrange("p h t -> p (h t)"), banks[u][:, 0:BC * TT]),
                               t, bandT.idle(n))
                    done["bandT0", n] = a
                else:
                    a = dve.do(lambda e, q=q, u=u: e.tensor_copy(bandT[n][:, q * BC:(q + 1) * BC, :].rearrange("p h t -> p (h t)"), banks[u][:, 0:BC * TT]),
                               t, bandT.idle(n))
                    done["bandT1", n] = a
                banks.used(u, a)
            band.used(n, t)
            for k in range(KD):
                t = pe.do(lambda e, k=k: e.transpose(banks[2][:, k * P:(k + 1) * P], avgT[b][:, k, i * TT:i * TT + P], ident[:, :]),
                          banks.idle(2), pads_ready)
            if i == NT - 1:
                avgT.used(b, t)
            a = act.do(lambda e: e.copy(window[n][:, :], banks[2][:, 0:D]), t, window.idle(n))
            banks.used(2, a)
            done["window", n] = a

        def band_product(b, i):
            n = b * NT + i
            for h in range(H):
                m = pe.do(lambda e, h=h: e.matmul(banks[3][0:TT, h * HD:(h + 1) * HD], bandT[n][:, h, :], window[n][:, h * HD:(h + 1) * HD],
                                                  start=True, stop=True), done["bandT0", n], done["bandT1", n], done["window", n], banks.idle(3))
            bandT.used(n, m)
            window.used(n, m)
            a = dve.do(lambda e: e.tensor_copy(conv[n][:, :], banks[3][0:TT, 0:D]), m, conv.idle(n))
            banks.used(3, a)
            done["conv", n] = a

        def conv_turn(b, i):
            n = b * NT + i
            size = min(TT, S - i * TT)
            for k in range(KD):
                t = pe.do(lambda e, k=k: e.transpose(banks[2][:, k * TT:(k + 1) * TT], conv[n][:, k * P:(k + 1) * P], ident[0:TT, 0:TT]),
                          done["conv", n], banks.idle(2))
            conv.used(n, t)
            a = act.do(lambda e: e.copy(convT[b][:, :, i * TT:i * TT + size],
                                        banks[2][:, 0:KD * TT].rearrange("p (k t) -> p k t", k=KD)[:, :, 0:size]), t, convT.idle(b))
            banks.used(2, a)
            done["convT", b] = a

        def mix(b, c):
            for k in range(KD):
                pe.quiet(lambda e, k=k: e.matmul(banks[3][:, 0:D], convT[b][:, k, c * P:(c + 1) * P], w_fc[:, k, :], start=k == 0, stop=False),
                         done["convT", b], banks.idle(3))
            for k in range(KD):
                m = pe.do(lambda e, k=k: e.matmul(banks[3][:, k * P:(k + 1) * P], h3T[b][:, k, c * P:(c + 1) * P], ident[:, :],
                                                  start=False, stop=k == KD - 1))
            a = act.do(lambda e: e.copy(v[b][:, c, :], banks[3][:, 0:D]), m, v.idle(b))
            banks.used(3, a)
            done["v", b, c // HC] = a
            if c == C - 1:
                convT.used(b, m)
                h3T.used(b, m)

        def load_rows(b):
            done["row_mid", b] = core.lane("row_mid").send(sp, lambda e: e.dma_start(
                row_mid[b][:, :, :].rearrange("p a d -> p (a d)"), g["row1_dram"][b:b + 1, D:3 * D].to_broadcast([P, 2 * D])), row_mid.idle(b))

        def load_out_rows(b):
            done["row_out", b] = core.lane("row_out").send(sp, lambda e: e.dma_start(
                row_out[b][:, :, :].rearrange("p a d -> p (a d)"), g["row1_dram"][b:b + 1, 3 * D:5 * D].to_broadcast([P, 2 * D])), row_out.idle(b))

        def norm_mid_a(b, half):
            cs = slice(half * HC, (half + 1) * HC)
            y, a = statistics(core, stats, moments, lambda c: v[b][:, half * HC + c, :], HC, 1e-6, scratch[:, :, 0:HC], done["v", b, half])
            for c in range(HC):
                a = dve.do(lambda e, c=c: e.tensor_scalar(v[b][:, half * HC + c, :], v[b][:, half * HC + c, :], moments[:, c, 0:1],
                                                          y[:, c:c + 1], ALU.subtract, ALU.mult), a)
            bc = lambda r: row_mid[b][:, r:r + 1, :].to_broadcast([P, HC, D])
            pool.do(lambda e: e.tensor_tensor(x2[b][:, cs, :], x2[b][:, cs, :], bc(1), ALU.add), done["row_mid", b], done["xh", b])
            a = pool.do(lambda e: e.tensor_tensor(v[b][:, cs, :], v[b][:, cs, :], bc(0), ALU.mult), a)
            if half == 1:
                row_mid.used(b, a)
            done["mid", b, half] = a

        def norm_mid_b(b, half):
            cs = slice(half * HC, (half + 1) * HC)
            a = dve.do(lambda e: e.tensor_tensor(x2[b][:, cs, :], x2[b][:, cs, :], v[b][:, cs, :], ALU.add), done["mid", b, half])
            y, a = statistics(core, stats, moments, lambda c: x2[b][:, half * HC + c, :], HC, 1e-5, scratch[:, :, 0:HC], a)
            for c in range(HC):
                a = dve.do(lambda e, c=c: e.tensor_scalar(v[b][:, half * HC + c, :], x2[b][:, half * HC + c, :], moments[:, c, 0:1],
                                                          y[:, c:c + 1], ALU.subtract, ALU.mult), a)
            done["h4", b, half] = a

        def turn_mid(b, half):
            for k in range(KD):
                u = k
                t = transpose_into(core, banks[u], HC, lambda c, k=k: v[b][:, half * HC + c, k * P:(k + 1) * P], ident, [done["h4", b, half], banks.idle(u)])
                a = act.do(lambda e, k=k, u=u: e.activation(h4T[b][:, k, half * BANK:(half + 1) * BANK], banks[u][:, :], ACT.Identity,
                                                            scale=cols[:, g["SCALE1B"] + k, b:b + 1], bias=cols[:, g["SHIFT1B"] + k, b:b + 1]), t, h4T.idle(b))
                banks.used(u, a)
            if half == 1:
                v.used(b, t)
            done["h4T", b, half] = a

        def expand(b, half, f):
            n = 2 * b + half
            u = 4 + f % 2
            for k in range(KD):
                m = pe.do(lambda e, k=k: e.matmul(banks[u][:, :], w1[:, k, f * P:(f + 1) * P], h4T[b][:, k, half * BANK:(half + 1) * BANK],
                                                  start=k == 0, stop=k == KD - 1), done["h4T", b, half], banks.idle(u))
            a = act.do(lambda e: e.activation(hidden[n][:, f, :], banks[u][:, :], ACT.Relu, bias=b1[:, f:f + 1]), m, hidden.idle(n))
            banks.used(u, a)
            done["hidden", n] = a
            if half == 1 and f == KF - 1:
                h4T.used(b, m)

        def row_gain(b):
            bc = row_out[b][:, 1:2, :].to_broadcast([P, C, D])
            done["x3", b] = pool.do(lambda e: e.tensor_tensor(x2[b][:, :, :], x2[b][:, :, :], bc, ALU.add), done["row_out", b], done["h4", b, 1])

        def contract(b, half, c):
            n, at = 2 * b + half, half * HC + c
            u = 6 + c % 2
            for f in range(KF):
                step = (lambda e, f=f: e.matmul(banks[u][:, 0:D], hidden[n][:, f, c * P:(c + 1) * P], w2[:, f, :], start=f == 0, stop=f == KF - 1))
                if f == KF - 1:
                    m = pe.do(step)
                else:
                    pe.quiet(step, done["hidden", n], banks.idle(u))
            if c == HC - 1:
                hidden.used(n, m)
            a = dve.do(lambda e: e.tensor_tensor(o[c][:, :], banks[u][:, 0:D], row_out[b][:, 0, :], ALU.mult), m, done["row_out", b], o.idle(c))
            banks.used(u, a)
            a = dve.do(lambda e: e.tensor_tensor(o[c][:, :], o[c][:, :], x2[b][:, at, :], ALU.add), a, done["x3", b])
            o.used(c, core.lane(f"out{c % 2}").send(sp, lambda e: e.dma_start(out_dram[b, at], o[c][:, :]), a))
            if half == 1 and c == HC - 1:
                x2.used(b, a)
                row_out.used(b, a)

        mlp = [lambda b: row_gain(b)]
        for half in range(2):
            mlp += [lambda b, half=half, f=f: expand(b, half, f) for f in range(KF)]
            mlp += [lambda b, half=half, c=c: contract(b, half, c) for c in range(HC)]
        conv_units = []
        for i in range(NT + 2):
            def unit(b, i=i):
                if i + 1 < NT:
                    load_band(b, i + 1)
                if i < NT:
                    band_turn(b, i)
                if 1 <= i <= NT:
                    band_product(b, i - 1)
                if i >= 2:
                    conv_turn(b, i - 2)
            conv_units.append(unit)
        mix_units = [lambda b, half=half, c=c: mix(b, half * HC + c) for half in range(2) for c in range(HC)]
        mid_units = mix_units + [lambda b: norm_mid_a(b, 0), lambda b: norm_mid_a(b, 1), lambda b: norm_mid_b(b, 0),
                                 lambda b: norm_mid_b(b, 1), lambda b: turn_mid(b, 0), lambda b: turn_mid(b, 1)]
        in_units = [load, norm_in, lambda b: turn_in(b, 0), lambda b: turn_in(b, 1), average]
        for c in range(C + 1):
            def unit(b, c=c):
                if c < C:
                    kernels_a(b, c)
                if c >= 1:
                    kernels_b(b, c - 1)
            in_units.append(unit)

        first = [(load_rows, 1), (load_out_rows, 2), (lambda b: load_band(b, 0), 1)]
        side = [(u, 1) for u in conv_units] + [(u, 1) for u in mid_units]
        ins = [(u, 0) for u in in_units]
        spread = []
        total_units = [(k / len(x), u) for x in (side, ins, [(u, 2) for u in mlp]) for k, u in enumerate(x)]
        spread = [u for _, u in sorted(total_units, key=lambda z: z[0])]
        pipeline(B, first + spread)
        core.everyone_waits_for_everyone()


def columns(vector):
    return vector.reshape(-1, P).T


def kernel(**inputs):
    import numpy as np
    import concourse.bacc as bacc
    from concourse.bass_utils import run_bass_kernel_spmd

    x = {name: np.asarray(a) for name, a in inputs.items()}
    B, S, D = x["L0_attn_x"].shape
    E = x["L0_ffn_router_weight"].shape[0]
    keep = ["L0_attn_x", "L0_attn_W_ret", "L0_attn_W1", "L0_attn_W2", "L0_attn_b2", "L0_attn_ln2_scale", "L0_attn_ln2_bias",
            "L0_ffn_norm_weight", "L0_ffn_router_bias", "L0_ffn_router_weight", "L0_ffn_fc2_bias", "L0_wmod", "L1_wmod",
            "L1_attn_W_pe", "L1_attn_b_pe", "L1_attn_stt_energy", "L1_attn_gamma", "L1_attn_beta", "L1_ffn_W1", "L1_ffn_W2", "L1_ffn_b2"]
    arrays = {n: x[n] for n in keep}
    arrays["L0_cT"], arrays["L1_cT"] = x["L0_c"].T, x["L1_c"].T
    arrays["L0_ffn_router_wT"] = x["L0_ffn_router_weight"].T
    arrays["L0_ffn_fc1_wT"] = x["L0_ffn_fc1_weight"].transpose(0, 2, 1)
    arrays["L0_ffn_fc2_wT"] = x["L0_ffn_fc2_weight"].transpose(0, 2, 1)
    arrays["L1_attn_W_fcT"] = x["L1_attn_W_fc"].T
    for n in ("L0_attn_b_ret", "L0_attn_ln1_scale", "L0_attn_ln1_bias", "L0_attn_b1", "L0_ffn_fc1_bias", "L1_ffn_b1"):
        arrays[n + "_c"] = columns(x[n])
    p = np.arange(P)
    G = P // E
    same = p[:, None] // G == p[None, :] // G
    arrays["block_ones"] = same.astype(np.float32)
    arrays["block_below"] = (same & (p[:, None] < p[None, :])).astype(np.float32)
    arrays["iota_row"] = np.tile(p.astype(np.float32), (P, 1))
    arrays["iota_column"] = p.astype(np.float32).reshape(P, 1)
    c, gr = np.divmod(np.arange(P), G)
    arrays["chunk_ids"] = np.tile((gr * (B * S // G // P) + c).astype(np.float32), (P, 1))
    arrays["per_count"] = (np.float32(1) / np.arange(1, S + 1, dtype=np.float32)).reshape(1, S)

    nc = bacc.Bacc("TRN2", target_bir_lowering=False, num_devices=1)
    feed, A = {}, {}
    for name, a in arrays.items():
        a = np.ascontiguousarray(a)
        feed[f"in_{name}"] = a
        A[name] = nc.dram_tensor(f"in_{name}", a.shape, mybir.dt.from_np(a.dtype), kind="ExternalInput").ap()
    out = nc.dram_tensor("out", (B, S, D), F32, kind="ExternalOutput").ap()
    build(nc, A, out)
    r = run_bass_kernel_spmd(nc, [feed], core_ids=[0])
    return r.results[0]["out"]
```

```python
from contextlib import ExitStack

import concourse.bass as bass
from concourse import mybir

F32 = mybir.dt.float32
F32R = mybir.dt.float32r
BF16 = mybir.dt.bfloat16
I32 = mybir.dt.int32
U32 = mybir.dt.uint32
ALU = mybir.AluOpType
ACT = mybir.ActivationFunctionType
AX_X = mybir.AxisListType.X

P = 128
BANK = 512


class Engine:

    def __init__(self, name, sem):
        self.name, self.sem, self.count, self.queue, self.reached = name, sem, 0, [], {}

    def wait(self, *tokens):
        for token in tokens:
            if token is None:
                continue
            if isinstance(token, list):
                self.wait(*token)
                continue
            sem, value, key = token
            if self.reached.get(key, 0) < value:
                self.reached[key] = value
                self.queue.append(lambda e, s=sem, v=value: e.wait_ge(s, v))

    def quiet(self, instruction, *tokens):
        self.wait(*tokens)
        self.queue.append(instruction)

    def do(self, instruction, *tokens):
        self.wait(*tokens)
        self.count += 1
        self.queue.append(lambda e: instruction(e).then_inc(self.sem, 1))
        return (self.sem, self.count, self.name)

    def last(self):
        return (self.sem, self.count, self.name) if self.count else None

    def replay(self, e):
        for instruction in self.queue:
            instruction(e)


class Lane:

    def __init__(self, name, sem):
        self.name, self.sem, self.count = name, sem, 0

    def send(self, engine, instruction, *tokens):
        engine.wait(*tokens)
        self.count += 16
        engine.queue.append(lambda e: instruction(e).then_inc(self.sem, 16))
        return (self.sem, self.count, self.name)

    def last(self):
        return (self.sem, self.count, self.name) if self.count else None


class Ring:

    def __init__(self, buffers):
        self.buffers, self.free = buffers, [[] for _ in buffers]

    def __getitem__(self, i):
        return self.buffers[i % len(self.buffers)]

    def idle(self, i):
        return self.free[i % len(self.buffers)]

    def used(self, i, *tokens):
        self.free[i % len(self.buffers)] = list(tokens)


class Core:

    def __init__(self, nc, ctx):
        self.nc, self.ctx, self.lanes, self.names = nc, ctx, {}, {}
        self.pe, self.act, self.dve, self.pool, self.sp = (
            Engine(n, ctx.enter_context(nc.semaphore("done_" + n))) for n in ("pe", "act", "dve", "pool", "sp"))
        self.engines = [self.pe, self.act, self.dve, self.pool, self.sp]
        self.banks = Ring([ctx.enter_context(nc.psum_tensor(f"bank{i}", [P, BANK], F32)) for i in range(8)])

    def lane(self, name):
        if name not in self.lanes:
            self.lanes[name] = Lane(name, self.ctx.enter_context(self.nc.semaphore("dma_" + name)))
        return self.lanes[name]

    def tile(self, ctx, name, shape, dt=F32):
        self.names[name] = self.names.get(name, 0) + 1
        if self.names[name] > 1:
            name = f"{name}_v{self.names[name]}"
        return ctx.enter_context(self.nc.sbuf_tensor(name, shape, dt))

    def split_tile(self, ctx, name, shape):
        return Split(self.tile(ctx, name + "_high", shape, F32R), self.tile(ctx, name + "_low", shape, F32R))

    def split_ring(self, ctx, name, n, shape):
        return Ring([self.split_tile(ctx, f"{name}{i}", shape) for i in range(n)])

    def ring(self, ctx, name, n, shape, dt=F32):
        return Ring([self.tile(ctx, f"{name}{i}", shape, dt) for i in range(n)])

    def everyone_waits_for_everyone(self):
        ends = [e.last() for e in self.engines] + [lane.last() for lane in self.lanes.values()]
        for e in self.engines:
            e.wait(*[t for t in ends if t is not None])


def pipeline(count, schedule):
    for step in range(count + max(lag for _, lag in schedule)):
        for stage, lag in schedule:
            if 0 <= step - lag < count:
                stage(step - lag)


def inverse_root(core, scratch, variance, eps, *tokens):
    dve = core.dve
    v, half, t, y = (scratch[:, i, :] for i in range(4))
    a = dve.do(lambda e: e.tensor_scalar(v, variance, eps, None, ALU.add), *tokens)
    dve.quiet(lambda e: e.tensor_scalar(half, variance, -0.5, -0.5 * eps, ALU.mult, ALU.add))
    a = dve.do(lambda e: e.tensor_scalar(t.bitcast(I32), v.bitcast(I32), 1, None, ALU.logical_shift_right), a)
    a = dve.do(lambda e: e.tensor_scalar(y.bitcast(I32), t.bitcast(I32), -1.0, float(0x5F3759DF), ALU.mult, ALU.add), a)
    for _ in range(3):
        a = dve.do(lambda e: e.tensor_tensor(t, y, y, ALU.mult), a)
        a = dve.do(lambda e: e.tensor_tensor(t, t, half, ALU.mult), a)
        a = dve.do(lambda e: e.scalar_tensor_tensor(out=y, in0=t, scalar=1.5, in1=y, op0=ALU.add, op1=ALU.mult), a)
    return y, a


def statistics(core, stats, moments, source, n, eps, scratch, *tokens):
    dve = core.dve
    for i in range(n):
        a = dve.do(lambda e, i=i: e.bn_stats(stats[:, i, :], source(i)), *(tokens if i == 0 else ()))
    dve.wait(a)
    for i in range(n):
        a = dve.do(lambda e, i=i: e.bn_aggr(moments[:, i, :], stats[:, i, :]))
    return inverse_root(core, scratch, moments[:, 0:n, 1], eps, a)


class Split:

    def __init__(self, high, low):
        self.high, self.low = high, low

    def __getitem__(self, key):
        return Split(self.high[key], self.low[key])

    def pairs(self, other):
        return [(self.low, other.high), (self.high, other.low), (self.high, other.high)]


def split(core, full, parts, subtractor, *tokens):
    high = core.act.do(lambda e: e.copy(parts.high, full), *tokens)
    return subtractor.do(lambda e: e.tensor_tensor(parts.low, full, parts.high, ALU.subtract), high)


def transpose_into(core, bank, columns, source, ident, wait, rows=P):
    for i in range(columns):
        core.pe.wait(*wait)
        wait = ()
        step = (lambda e, i=i: e.transpose(bank[:, i * rows:(i + 1) * rows], source(i), ident[0:rows, 0:rows]))
        token = core.pe.do(step) if i == columns - 1 else core.pe.quiet(step)
    return token


def build(nc, A, out, debug=None):
    B, S, D = A["L0_attn_x"].shape
    T = B * S
    F = A["L0_attn_W1"].shape[1]
    E = A["L0_ffn_router_weight"].shape[0]
    CAP = T // E
    KD, KF = D // P, F // P
    NM = 6 * D
    HEADS, KW = A["L1_attn_stt_energy"].shape[1], A["L1_attn_stt_energy"].shape[3]
    assert D == 2 * P and S == 1024 and CAP == 1024 and E == 16

    ctx = ExitStack()
    with ctx:
        core = Core(nc, ctx)
        pe, act, dve, pool, sp = core.engines
        banks = core.banks

        x1_dram = nc.dram_tensor("x_after_retention", [T, D], F32, kind="Internal").ap()
        xn_dram = nc.dram_tensor("moe_input", [T, D], F32, kind="Internal").ap()
        logit_dram = nc.dram_tensor("router_logits", [E, T], F32, kind="Internal").ap()
        moe_dram = nc.dram_tensor("moe_output", [T, D], F32, kind="Internal").ap()
        gate_dram = nc.dram_tensor("gates", [T, E], F32, kind="Internal").ap()
        row0_dram = nc.dram_tensor("rows_layer0", [B, 4 * D], F32, kind="Internal").ap()
        row1_dram = nc.dram_tensor("rows_layer1", [B, 5 * D], F32, kind="Internal").ap()
        TILE_T = 96
        NT = -(-S // TILE_T)
        BAND_SIZE = 1568 * P
        assert BAND_SIZE >= (TILE_T + 1) * (P + 1) * HEADS
        band_dram = [nc.dram_tensor(f"bands{i}", [NT, BAND_SIZE], F32, kind="Internal").ap() for i in range(2)]

        ident = core.tile(ctx, "ident", [P, P])
        cols = core.tile(ctx, "mod_columns", [P, 12, B])
        zero = core.tile(ctx, "zero", [P, 1])
        pool.do(lambda e: e.memset(ident[:, :], 0.0))
        zero_ready = pool.do(lambda e: e.memset(zero[:, :], 0.0))
        ident_ready = pool.do(lambda e: e.affine_select(
            out=ident[:, :], in_=ident[:, :], compare_op=ALU.not_equal, fill=1.0, base=0,
            pattern=[[-1, P]], channel_multiplier=1), pool.last())

        mlp_weights = ExitStack()
        split_w1, split_w2 = core.split_tile(mlp_weights, "w1", [P, KD, F]), core.split_tile(mlp_weights, "w2", [P, KF, D])

        SHIFT0, SCALE0, SHIFT1A, SCALE1A, SHIFT1B, SCALE1B = range(0, 12, 2)
        with ExitStack() as part:
            rows_sent = []
            mod = [core.tile(part, f"mod{l}", [B, NM]) for l in range(2)]
            for l in range(2):
                cT = core.tile(part, f"cT{l}", [P, KD, B])
                th = core.tile(part, f"c_tanh{l}", [P, KD, B])
                sc = core.tile(part, f"c_silu{l}", [P, KD, B])
                wm = core.tile(part, f"wmod{l}", [P, KD, NM])
                lane = core.lane(f"cond{l}")
                lane.send(sp, lambda e, l=l, cT=cT: e.dma_start(cT[:, :, :], A[f"L{l}_cT"].rearrange("(k p) b -> p k b", p=P)))
                got = lane.send(sp, lambda e, l=l, wm=wm: e.dma_start(wm[:, :, :], A[f"L{l}_wmod"].rearrange("(k p) n -> p k n", p=P)))
                a = act.do(lambda e, th=th, cT=cT: e.activation(th[:, :, :], cT[:, :, :], ACT.Tanh, scale=0.5), got)
                a = dve.do(lambda e, th=th, cT=cT: e.scalar_tensor_tensor(
                    out=th[:, :, :], in0=th[:, :, :], scalar=1.0, in1=cT[:, :, :], op0=ALU.add, op1=ALU.mult), a)
                a = dve.do(lambda e, th=th, sc=sc: e.tensor_scalar(sc[:, :, :], th[:, :, :], 0.5, None, ALU.mult), a)
                for n in range(NM // BANK):
                    u = 3 * l + n
                    for k in range(KD):
                        step = (lambda e, u=u, n=n, k=k, sc=sc, wm=wm: e.matmul(
                            banks[u][0:B, :], sc[:, k, :], wm[:, k, n * BANK:(n + 1) * BANK], start=k == 0, stop=k == KD - 1))
                        m = pe.do(step, a, got)
                    a2 = dve.do(lambda e, u=u, n=n, l=l: e.tensor_copy(mod[l][:, n * BANK:(n + 1) * BANK], banks[u][0:B, :]), m)
                    banks.used(u, a2)

            for name, parts, k in (("L0_attn_W1", split_w1, KD), ("L0_attn_W2", split_w2, KF)):
                full = core.tile(part, name, [P, k, A[name].shape[1]])
                got = core.lane(name).send(sp, lambda e, full=full, name=name: e.dma_start(full[:, :, :], A[name].rearrange("(k p) n -> p k n", p=P)))
                split(core, full[:, :, :], parts[:, :, :], dve, got)

            def field(l, i):
                return mod[l][:, i * D:(i + 1) * D]

            a = dve.last()
            work = core.tile(part, "mod_work", [B, 4, D])
            for l in range(2):
                for i in (2, 5):
                    g, s, m = field(l, i), work[:, 0, :], work[:, 1, :]
                    b = dve.do(lambda e, g=g, m=m: e.tensor_scalar(m, g, -1.0, None, ALU.mult), a)
                    b = dve.do(lambda e, g=g, m=m: e.tensor_tensor(m, m, g, ALU.max), b)
                    b = dve.do(lambda e, m=m: e.tensor_scalar(m, m, 0.25, None, ALU.max), b)
                    b = dve.do(lambda e, g=g, s=s: e.tensor_scalar(s, g, 0.0, 2.0, ALU.is_ge, ALU.mult), b)
                    b = dve.do(lambda e, s=s: e.tensor_scalar(s, s, -1.0, None, ALU.add), b)
                    a = dve.do(lambda e, g=g, s=s, m=m: e.tensor_tensor(g, s, m, ALU.mult), b)
                for i in (1, 4):
                    a = dve.do(lambda e, l=l, i=i: e.tensor_scalar(field(l, i), field(l, i), 1.0, None, ALU.add), a)
            vec = core.tile(part, "vectors_by_batch", [B, 5, D])
            for i, name in enumerate(["L0_attn_ln2_scale", "L0_attn_ln2_bias", "L1_attn_gamma", "L1_attn_beta", "L1_ffn_b2"]):
                got = core.lane("vectors").send(sp, lambda e, i=i, name=name: e.dma_start(
                    vec[:, i, :], A[name].rearrange("(a d) -> a d", a=1).to_broadcast([B, D])))
            rows0 = core.tile(part, "rows0", [B, 4, D])
            rows1 = core.tile(part, "rows1", [B, 5, D])
            dve.wait(a, got)
            dve.quiet(lambda e: e.tensor_tensor(rows0[:, 0, :], field(0, 2), vec[:, 0, :], ALU.mult))
            dve.quiet(lambda e: e.tensor_tensor(rows0[:, 1, :], field(0, 2), vec[:, 1, :], ALU.mult))
            dve.quiet(lambda e: e.tensor_copy(rows0[:, 2, :], field(0, 4)))
            a = dve.do(lambda e: e.tensor_copy(rows0[:, 3, :], field(0, 3)))
            rows_sent.append(core.lane("rows").send(sp, lambda e: e.dma_start(row0_dram, rows0[:, :, :].rearrange("b a d -> b (a d)")), a))
            dve.quiet(lambda e: e.tensor_copy(rows1[:, 0, :], field(0, 5)))
            dve.quiet(lambda e: e.tensor_tensor(rows1[:, 1, :], field(1, 2), vec[:, 2, :], ALU.mult))
            dve.quiet(lambda e: e.tensor_tensor(rows1[:, 2, :], field(1, 2), vec[:, 3, :], ALU.mult))
            dve.quiet(lambda e: e.tensor_copy(rows1[:, 3, :], field(1, 5)))
            a = dve.do(lambda e: e.tensor_tensor(rows1[:, 4, :], field(1, 5), vec[:, 4, :], ALU.mult))
            rows_sent.append(core.lane("rows").send(sp, lambda e: e.dma_start(row1_dram, rows1[:, :, :].rearrange("b a d -> b (a d)")), a))
            blocks = [(0, 0), (0, 1), (1, 0), (1, 1), (1, 3), (1, 4)]
            for n, (l, i) in enumerate(blocks):
                for k in range(KD):
                    step = (lambda e, n=n, l=l, i=i, k=k: e.transpose(
                        banks[6][:, (2 * n + k) * B:(2 * n + k + 1) * B], field(l, i)[:, k * P:(k + 1) * P], ident[0:B, 0:B]))
                    m = pe.do(step, a, ident_ready)
            a = dve.do(lambda e: e.tensor_copy(cols[:, :, :].rearrange("p n b -> p (n b)"), banks[6][:, 0:12 * B]), m)
            banks.used(6, a)
            core.everyone_waits_for_everyone()

        g = dict(B=B, S=S, D=D, T=T, F=F, E=E, CAP=CAP, KD=KD, KF=KF, HEADS=HEADS, KW=KW, TILE_T=TILE_T, NT=NT, BAND_SIZE=BAND_SIZE,
                 ident=ident, cols=cols, zero=zero, zero_ready=zero_ready,
                 SHIFT0=SHIFT0, SCALE0=SCALE0, SHIFT1A=SHIFT1A, SCALE1A=SCALE1A, SHIFT1B=SHIFT1B, SCALE1B=SCALE1B,
                 x1_dram=x1_dram, xn_dram=xn_dram, logit_dram=logit_dram, moe_dram=moe_dram, gate_dram=gate_dram,
                 row0_dram=row0_dram, row1_dram=row1_dram, band_dram=band_dram, out=out)
        retention(core, A, g, split_w1, split_w2)
        mlp_weights.close()
        if debug != "A":
            experts(core, A, g)
            if debug != "M":
                layer_one(core, A, g)
        core.everyone_waits_for_everyone()

        block = ctx.enter_context(nc.Block())
        block.tensor(lambda e: pe.replay(e))
        block.scalar(lambda e: act.replay(e))
        block.vector(lambda e: dve.replay(e))
        block.gpsimd(lambda e: pool.replay(e))
        block.sync(lambda e: sp.replay(e))


def retention(core, A, g, w1, w2):
    pe, act, dve, pool, sp = core.engines
    banks, ident, cols = core.banks, g["ident"], g["cols"]
    B, S, D, T, F, E, KD, KF = (g[n] for n in ("B", "S", "D", "T", "F", "E", "KD", "KF"))
    GT = BANK
    C = GT // P
    N = T // GT
    PER = S // GT
    x_dram = A["L0_attn_x"].rearrange("b (h c p) d -> (b h) p c d", c=C, p=P)
    x1_dram = g["x1_dram"].rearrange("(n c p) d -> n p c d", c=C, p=P)
    xn_dram = g["xn_dram"].rearrange("(n c p) d -> n p c d", c=C, p=P)

    with ExitStack() as part:
        def tile(name, shape, dt=F32):
            return core.tile(part, name, shape, dt)

        def ring(name, n, shape):
            return core.ring(part, name, n, shape)

        w_ret = tile("w_ret", [P, KD, D])
        w_router = tile("w_router", [P, KD, E])
        ret_bias, ln1_scale, ln1_bias, b1 = (tile(n, [P, k]) for n, k in (("ret_bias", KD), ("ln1_scale", KD), ("ln1_bias", KD), ("b1", KF)))
        router_bias = tile("router_bias", [E, 1])
        b2_row, nw_row = tile("b2_row", [P, D]), tile("nw_row", [P, D])
        half, zeros = tile("half", [P, 1]), tile("zeros", [P, g["BAND_SIZE"] // P])
        x, rows = ring("x", 6, [P, C, D]), ring("rows", 2, [P, 4, D])
        xh, h1T, th, q, r = ring("xh", 1, [P, C, D]), ring("h1T", 1, [P, KD, GT]), ring("th", 1, [P, KD, GT]), ring("q", 2, [P, KD, GT]), ring("r", 1, [P, KD, GT])
        xh2, h_full, g_full = ring("xh2", 1, [P, C, D]), ring("h_full", 2, [P, GT]), ring("g_full", 4, [P, GT])
        hT, act_T = core.split_ring(part, "hT", 2, [P, KD, GT]), core.split_ring(part, "gT", 1, [P, KF, GT])
        ident_r = tile("ident_r", [P, P], F32R)
        v, x1, h2, xn, xnT = (ring(n, k, [P, C, D]) for n, k in (("v", 2), ("x1_", 2), ("h2_", 2), ("xn", 2), ("xnT", 1)))
        square = tile("square", [P, D])
        lg = ring("lg", 2, [E, GT])
        stats, moments = tile("stats", [P, C, 6]), tile("moments", [P, C, 2])
        scratch = tile("scratch", [P, 4, C])
        sumsq = ring("sumsq", 2, [P, C])

        lane = core.lane("weights")
        for dst, src in ((w_ret[:, :, :], A["L0_attn_W_ret"].rearrange("(k p) n -> p k n", p=P)),
                         (w_router[:, :, :], A["L0_ffn_router_wT"].rearrange("(k p) n -> p k n", p=P)),
                         (ret_bias[:, :], A["L0_attn_b_ret_c"]), (ln1_scale[:, :], A["L0_attn_ln1_scale_c"]),
                         (ln1_bias[:, :], A["L0_attn_ln1_bias_c"]), (b1[:, :], A["L0_attn_b1_c"]),
                         (router_bias[:, :], A["L0_ffn_router_bias"].rearrange("(e a) -> e a", a=1)),
                         (b2_row[:, :], A["L0_attn_b2"].rearrange("(a d) -> a d", a=1).to_broadcast([P, D])),
                         (nw_row[:, :], A["L0_ffn_norm_weight"].rearrange("(a d) -> a d", a=1).to_broadcast([P, D]))):
            weights = lane.send(sp, lambda e, dst=dst, src=src: e.dma_start(dst, src))
        zeros_ready = pool.do(lambda e: e.memset(zeros[:, :], 0.0))
        ident_r_ready = dve.do(lambda e: e.tensor_copy(ident_r[:, :], ident[:, :]))
        half_ready = dve.do(lambda e: e.memset(half[:, :], 0.5))
        bias_ready = dve.do(lambda e: e.tensor_scalar(ret_bias[:, :], ret_bias[:, :], 0.5, None, ALU.mult), weights)

        got_x, got_rows, done = {}, {}, {}

        def load(i):
            got_x[i] = core.lane(f"x{i % 6}").send(sp, lambda e: e.dma_start(x[i][:, :, :], x_dram[i]), x.idle(i))
            zl = core.lane("zeros")
            zl.send(sp, lambda e: e.dma_start(g["moe_dram"].rearrange("(n p c) d -> n p (c d)", p=P, c=C)[i],
                                              zeros[:, 0:C * D]), zeros_ready)
            if i < 2 * g["NT"]:
                size = g["BAND_SIZE"] // P
                zl.send(sp, lambda e: e.dma_start(g["band_dram"][i % 2][i // 2].rearrange("(p c) -> p c", p=P), zeros[:, 0:size]))

        def load_rows(i):
            if i % PER == 0:
                b = i // PER
                got_rows[b] = core.lane(f"rows{b % 2}").send(sp, lambda e: e.dma_start(
                    rows[b][:, :, :].rearrange("p a d -> p (a d)"), g["row0_dram"][b:b + 1, :].to_broadcast([P, 4 * D])), rows.idle(b))

        def norm_in(i):
            y, a = statistics(core, stats, moments, lambda c: x[i][:, c, :], C, 1e-5, scratch, got_x[i])
            dve.wait(a, xh.idle(i))
            for c in range(C):
                a = dve.do(lambda e, c=c: e.tensor_scalar(xh[i][:, c, :], x[i][:, c, :], moments[:, c, 0:1], y[:, c:c + 1],
                                                          ALU.subtract, ALU.mult))
            done["xh", i] = a

        uses = [0]

        def next_bank():
            uses[0] += 1
            return uses[0] % 4

        def next_pair():
            return next_bank(), next_bank()

        def to_features(i, source, ready, write):
            for k, u in enumerate(next_pair()):
                t = transpose_into(core, banks[u], C, lambda c, k=k: source[:, c, k * P:(k + 1) * P], ident, [ready, banks.idle(u)])
                banks.used(u, write(k, banks[u], t))
            return t

        def modulate(i):
            b = i // PER

            def write(k, bank, t):
                a = act.do(lambda e: e.activation(h1T[i][:, k, :], bank[:, :], ACT.Identity,
                                                  scale=cols[:, g["SCALE0"] + k, b:b + 1], bias=cols[:, g["SHIFT0"] + k, b:b + 1]), t, h1T.idle(i))
                done["h1T", i] = a
                return a
            t = to_features(i, xh[i], done["xh", i], write)
            xh.used(i, t)

        def retain(i, k):
            u = next_bank()
            for j in range(KD):
                m = pe.do(lambda e, j=j: e.matmul(banks[u][:, :], w_ret[:, j, k * P:(k + 1) * P], h1T[i][:, j, :],
                                                  start=j == 0, stop=j == KD - 1), done["h1T", i], weights, banks.idle(u))
            a = act.do(lambda e: e.activation(th[i][:, k, :], banks[u][:, :], ACT.Tanh, bias=ret_bias[:, k:k + 1], scale=0.5),
                       m, bias_ready, th.idle(i))
            banks.used(u, a)
            done["tanh", i, k] = pool.do(lambda e: e.tensor_scalar(th[i][:, k, :], th[i][:, k, :], 1.0, 1.0, ALU.mult, ALU.add), a)
            if k == KD - 1:
                done["retained", i] = m

        def run(i, k):
            start = 0.0 if i % PER == 0 else q[i - 1][:, k, GT - 1:GT]
            a = dve.do(lambda e: e.tensor_tensor_scan(
                q[i][:, k, :], half[:, 0:1].to_broadcast([P, GT]), th[i][:, k, :], start, ALU.mult, ALU.add),
                done["tanh", i, k], half_ready, done.get(("q", i - 1)))
            if k == KD - 1:
                th.used(i, a)
                done["q", i] = a
            a = dve.do(lambda e: e.scalar_tensor_tensor(out=r[i][:, k, :], in0=q[i][:, k, :], scalar=0.25, in1=h1T[i][:, k, :],
                                                        op0=ALU.mult, op1=ALU.add), a, r.idle(i))
            if k == KD - 1:
                done["r", i] = a
                h1T.used(i, a, done["retained", i])

        def norm_mid(i):
            pairs = next_pair()
            for c in range(C):
                u = pairs[c // 2]
                for k in range(KD):
                    col = (c % 2) * D + k * P
                    m = pe.do(lambda e, c=c, k=k, u=u, col=col: e.transpose(banks[u][:, col:col + P], r[i][:, k, c * P:(c + 1) * P], ident[:, :]),
                              done["r", i], banks.idle(u))
            r.used(i, m)
            chunk = lambda c: banks[pairs[c // 2]][:, (c % 2) * D:(c % 2 + 1) * D]
            y, a = statistics(core, stats, moments, chunk, C, 1e-5, scratch, m)
            dve.wait(a, xh2.idle(i))
            for c in range(C):
                a = dve.do(lambda e, c=c: e.tensor_scalar(xh2[i][:, c, :], chunk(c), moments[:, c, 0:1], y[:, c:c + 1], ALU.subtract, ALU.mult))
            for u in pairs:
                banks.used(u, a)
            done["xh2", i] = a

        def affine_mid(i):
            def write(k, bank, t):
                n = KD * i + k
                a = act.do(lambda e: e.activation(h_full[n][:, :], bank[:, :], ACT.Identity,
                                                  scale=ln1_scale[:, k:k + 1], bias=ln1_bias[:, k:k + 1]), t, h_full.idle(n))
                b = split(core, h_full[n][:, :], hT[i][:, k, :], pool, a, hT.idle(i))
                h_full.used(n, b)
                done["hT", i] = b
                return a
            xh2.used(i, to_features(i, xh2[i], done["xh2", i], write))

        def take_apart(i, f):
            n = KF * i + f
            done["gT", i] = split(core, g_full[n][:, :], act_T[i][:, f, :], pool, done["g", n], act_T.idle(i))
            g_full.used(n, done["gT", i])

        def expand(i, fs):
            for f in fs:
                u, n = 4 + f % 2, KF * i + f
                for k in range(KD):
                    for j, (w, h) in enumerate(w1[:, k, f * P:(f + 1) * P].pairs(hT[i][:, k, :])):
                        m = pe.do(lambda e, w=w, h=h, u=u, first=k + j == 0, final=k == KD - 1 and j == 2: e.matmul(
                            banks[u][:, :], w, h, start=first, stop=final), done["hT", i], banks.idle(u))
                a = act.do(lambda e, f=f, u=u, n=n: e.activation(g_full[n][:, :], banks[u][:, :], ACT.Gelu_apprx_tanh, bias=b1[:, f:f + 1]),
                           m, g_full.idle(n))
                banks.used(u, a)
                done["g", n] = a
                if f > 0:
                    take_apart(i, f - 1)
            if f == KF - 1:
                take_apart(i, f)

        def contract(i, c):
            u = 6 + c % 2
            chunk = slice(c * P, (c + 1) * P)
            pe.wait(done["gT", i], banks.idle(u), ident_r_ready)
            for f in range(KF):
                for j, (x_, w) in enumerate(act_T[i][:, f, chunk].pairs(w2[:, f, :])):
                    pe.quiet(lambda e, x_=x_, w=w, first=f + j == 0: e.matmul(banks[u][:, 0:D], x_, w, start=first, stop=False))
            for k in range(KD):
                for j, x_ in enumerate((hT[i].low, hT[i].high)):
                    m = pe.do(lambda e, k=k, x_=x_, final=k == KD - 1 and j == 1: e.matmul(
                        banks[u][:, k * P:(k + 1) * P], x_[:, k, chunk], ident_r[:, :], start=False, stop=final))
            if c == C - 1:
                act_T.used(i, m)
                hT.used(i, m)
            a = act.do(lambda e: e.copy(v[i][:, c, :], banks[u][:, 0:D]), m, v.idle(i))
            banks.used(u, a)
            done["v", i] = a

        def bcast(b, row):
            return rows[b][:, row:row + 1, :].to_broadcast([P, C, D])

        def norm_out(i):
            a = dve.do(lambda e: e.tensor_tensor(v[i][:, :, :], v[i][:, :, :], b2_row[:, :].unsqueeze(1).to_broadcast([P, C, D]), ALU.add), done["v", i])
            y, a = statistics(core, stats, moments, lambda c: v[i][:, c, :], C, 1e-5, scratch, a)
            dve.wait(a)
            for c in range(C):
                a = dve.do(lambda e, c=c: e.tensor_scalar(v[i][:, c, :], v[i][:, c, :], moments[:, c, 0:1], y[:, c:c + 1],
                                                          ALU.subtract, ALU.mult))
            done["vhat", i] = a

        def gain_out(i):
            b = i // PER
            a = pool.do(lambda e: e.tensor_tensor(v[i][:, :, :], v[i][:, :, :], bcast(b, 0), ALU.mult), done["vhat", i], got_rows[b])
            a = pool.do(lambda e: e.tensor_tensor(x1[i][:, :, :], x[i][:, :, :], bcast(b, 1), ALU.add), got_x[i], got_rows[b], x1.idle(i))
            x.used(i, a)
            done["t1", i] = a

        def residual(i):
            a = dve.do(lambda e: e.tensor_tensor(x1[i][:, :, :], x1[i][:, :, :], v[i][:, :, :], ALU.add), done["t1", i])
            v.used(i, a)
            sent = core.lane(f"x1_{i % 2}").send(sp, lambda e: e.dma_start(x1_dram[i], x1[i][:, :, :]), a)
            y, a = statistics(core, stats, moments, lambda c: x1[i][:, c, :], C, 1e-5, scratch, a)
            dve.wait(a, h2.idle(i))
            for c in range(C):
                a = dve.do(lambda e, c=c: e.tensor_scalar(h2[i][:, c, :], x1[i][:, c, :], moments[:, c, 0:1], y[:, c:c + 1],
                                                          ALU.subtract, ALU.mult))
            x1.used(i, sent, a)
            done["x1hat", i] = a

        def modulate_out(i):
            b = i // PER
            a = pool.do(lambda e: e.tensor_tensor(h2[i][:, :, :], h2[i][:, :, :], bcast(b, 2), ALU.mult), done["x1hat", i])
            a = pool.do(lambda e: e.tensor_tensor(h2[i][:, :, :], h2[i][:, :, :], bcast(b, 3), ALU.add), a)
            rows.used(b, a)
            done["h2", i] = a

        def squares(i):
            a = act.last()
            for c in range(C):
                a = act.do(lambda e, c=c: e.activation(square[:, :], h2[i][:, c, :], ACT.Square, scale=D ** -0.5,
                                                       accum_out=sumsq[i][:, c:c + 1]), a, done["h2", i], sumsq.idle(i))
            done["sumsq", i] = a

        def rms_norm(i):
            y, a = inverse_root(core, scratch, sumsq[i][:, :], 1e-5, done["sumsq", i])
            dve.wait(xn.idle(i))
            dve.wait(a)
            for c in range(C):
                a = dve.do(lambda e, c=c: e.scalar_tensor_tensor(out=xn[i][:, c, :], in0=h2[i][:, c, :], scalar=y[:, c:c + 1],
                                                                 in1=nw_row[:, :], op0=ALU.mult, op1=ALU.mult))
            sumsq.used(i, a)
            h2.used(i, a)
            done["xn", i] = a

        def turn_out(i):
            def write(k, bank, t):
                done["xnT", i] = act.do(lambda e: e.copy(xnT[i][:, k * 2:k * 2 + 2, :].rearrange("p a d -> p (a d)"), bank[:, :]), t, xnT.idle(i))
                return done["xnT", i]
            t = to_features(i, xn[i], done["xn", i], write)
            sent = core.lane(f"xn{i % 2}").send(sp, lambda e: e.dma_start(xn_dram[i], xn[i][:, :, :]), done["xn", i])
            xn.used(i, t, sent)

        def route(i):
            u = next_bank()
            for k in range(KD):
                m = pe.do(lambda e, k=k: e.matmul(banks[u][0:E, :], w_router[:, k, :], xnT[i][:, k * 2:k * 2 + 2, :].rearrange("p a d -> p (a d)"),
                                                  start=k == 0, stop=k == KD - 1), done["xnT", i], banks.idle(u))
            xnT.used(i, m)
            a = act.do(lambda e: e.activation(lg[i][:, :], banks[u][0:E, :], ACT.Identity, bias=router_bias[:, 0:1]), m, lg.idle(i))
            banks.used(u, a)
            sent = core.lane(f"lg{i % 2}").send(sp, lambda e: e.dma_start(g["logit_dram"][:, i * GT:(i + 1) * GT], lg[i][:, :]), a)
            lg.used(i, sent)

        def part_of(stage, *args):
            return lambda i: stage(i, *args)

        pipeline(N, [
            (load, 0), (modulate_out, 6), (turn_out, 7), (modulate, 1), (norm_mid, 2), (part_of(contract, 0), 4), (gain_out, 5), (route, 7),
            (part_of(contract, 1), 4), (squares, 6), (part_of(contract, 2), 4), (residual, 5), (part_of(contract, 3), 4),
            (affine_mid, 2), (rms_norm, 6),
            (part_of(expand, (0, 1)), 3), (norm_in, 0), (part_of(retain, 0), 1), (part_of(expand, (2, 3)), 3), (part_of(retain, 1), 1),
            (part_of(run, 0), 1), (part_of(expand, (4,)), 3), (part_of(run, 1), 1), (norm_out, 4), (part_of(expand, (5, 6)), 3),
            (part_of(expand, (7,)), 3), (load_rows, 3),
        ])
        core.everyone_waits_for_everyone()


def find_threshold(core, part, L, block_ones, ready):
    pe, act, dve, pool, sp = core.engines
    thr, trial, keep = (core.tile(part, n, [P, 1], U32) for n in ("thr", "trial", "keep"))
    count = core.tile(part, "count", [P, 1])
    hits = core.tile(part, "hits", [P, L.shape[1]], BF16)
    bank = core.banks[0]

    def enough(a, wanted):
        a = dve.do(lambda e: e.tensor_scalar(hits[:, :], L[:, :], trial[:, :].bitcast(F32), None, ALU.is_ge, ALU.add,
                                             accum_out=count[:, :]), a, ready)
        m = pe.do(lambda e: e.matmul(bank[:, 0:1], block_ones[:, :], count[:, :], start=True, stop=True), a, core.banks.idle(0))
        return dve.do(lambda e: e.tensor_scalar(keep[:, :], bank[:, 0:1], float(wanted) - 0.5, None, ALU.is_ge), m)

    wanted = 1024
    a = dve.do(lambda e: e.memset(trial[:, :].bitcast(F32), 0.0))
    a = enough(a, wanted)
    a = dve.do(lambda e: e.tensor_scalar(trial[:, :], keep[:, :], 1, None, ALU.bitwise_xor), a)
    a = dve.do(lambda e: e.tensor_scalar(thr[:, :].bitcast(I32), trial[:, :].bitcast(I32), 31, 31, ALU.logical_shift_left,
                                         ALU.arith_shift_right), a)
    for bit in range(30, -1, -1):
        a = dve.do(lambda e, bit=bit: e.tensor_scalar(trial[:, :], thr[:, :], 1 << bit, None, ALU.bitwise_xor), a)
        a = enough(a, wanted)
        a = dve.do(lambda e, bit=bit: e.scalar_tensor_tensor(out=thr[:, :], in0=keep[:, :], scalar=bit, in1=thr[:, :],
                                                             op0=ALU.logical_shift_left, op1=ALU.bitwise_xor), a)
    core.banks.used(0, a)
    return thr[:, :].bitcast(F32), a


def experts(core, A, g):
    pe, act, dve, pool, sp = core.engines
    banks, ident = core.banks, g["ident"]
    D, T, F, E, KD, KF, CAP = (g[n] for n in ("D", "T", "F", "E", "KD", "KF", "CAP"))
    G = P // E
    W = T // G
    CH = W // P
    NONE = 4096
    PER_BANK = BANK // P
    HT = CAP // 2
    C = HT // P
    NI = 2 * E

    with ExitStack() as part:
        def tile(name, shape, dt=F32):
            return core.tile(part, name, shape, dt)

        def ring(name, n, shape, dt=F32):
            return core.ring(part, name, n, shape, dt)

        block_ones, block_below = tile("block_ones", [P, P]), tile("block_below", [P, P])
        iota_p, iota_q, token_low = tile("iota_p", [P, P], BF16), tile("iota_q", [P, G], BF16), tile("token_low", [P, 1])
        token_high = tile("token_high", [P, CH, G], BF16)
        b1 = tile("fc1_bias", [P, E, KF])
        L = tile("logits", [P, W])
        f1, f2, f3 = tile("work1", [P, W]), tile("work2", [P, W]), tile("work3", [P, W])
        slot_i = tile("slot_i", [P, CH, E, G], I32)
        slot_p, slot_q = tile("slot_p", [P, CH, E, G], BF16), tile("slot_q", [P, CH, E, G], BF16)
        small = tile("small", [P, 8])
        xg, gg = ring("xg", 2, [P, C, D]), ring("gg", 4, [P, C, E])
        xgT, hidden = ring("xgT", 2, [P, KD, HT]), ring("hidden", 2, [P, KF, HT])
        w1, w2, b2_row = ring("fc1", 2, [P, KD, F]), ring("fc2", 2, [P, KF, D]), ring("fc2_bias", 2, [P, D])
        y, ys = ring("y", 2, [P, D]), ring("ys", 2, [P, C, D])
        PC = 2
        onehot_p, onehot_q = ring("onehot_p", 4, [P, PC, G, P], BF16), ring("onehot_q", 4, [P, PC, G, 2 * G], BF16)
        eq_q = ring("eq_q", 2, [P, PC, G, G], BF16)
        parts = ring("id_parts", 2, [P, 2 * G])
        idx = ring("idx", 4, [P, G], U32)

        lane = core.lane("routing_in")
        for dst, src in ((L[:, :], g["logit_dram"].rearrange("e (g t) -> (e g) t", g=G)),
                         (block_ones[:, :], A["block_ones"]), (block_below[:, :], A["block_below"]), (f1[:, 0:P], A["iota_row"]),
                         (small[:, 0:1], A["iota_column"]), (f2[:, 0:P], A["chunk_ids"]),
                         (b1[:, :, :], A["L0_ffn_fc1_bias_c"].rearrange("p (e k) -> p e k", e=E))):
            ready = lane.send(sp, lambda e, dst=dst, src=src: e.dma_start(dst, src))
        done = {}

        def load_weights(e_):
            lane = core.lane(f"expert_w{e_ % 2}")
            for dst, src in ((w1[e_][:, :, :], A["L0_ffn_fc1_wT"][e_].rearrange("(k p) n -> p k n", p=P)),
                             (w2[e_][:, :, :], A["L0_ffn_fc2_wT"][e_].rearrange("(k p) n -> p k n", p=P)),
                             (b2_row[e_][:, :], A["L0_ffn_fc2_bias"][e_:e_ + 1, :].to_broadcast([P, D]))):
                done["w", e_] = lane.send(sp, lambda e, dst=dst, src=src: e.dma_start(dst, src), w1.idle(e_))
        load_weights(0)

        dve.quiet(lambda e: e.tensor_copy(iota_p[:, :], f1[:, 0:P]), ready)
        dve.quiet(lambda e: e.tensor_copy(iota_q[:, :], f1[:, 0:G]))
        dve.quiet(lambda e: e.tensor_copy(token_low[:, :], small[:, 0:1]))
        dve.do(lambda e: e.tensor_copy(token_high[:, :, :].rearrange("p c g -> p (c g)"), f2[:, 0:P]))
        limit, a = find_threshold(core, part, L, block_ones, ready)

        above, ties, tied_before, tie_room, counts, base = (small[:, i:i + 1] for i in range(1, 7))
        greater, equal, running = f1, f2, f3
        dve.wait(a)
        a = dve.do(lambda e: e.tensor_scalar(greater[:, :], L[:, :], limit, None, ALU.is_gt, ALU.add, accum_out=above), a)
        a = dve.do(lambda e: e.tensor_scalar(equal[:, :], L[:, :], limit, None, ALU.is_equal, ALU.add, accum_out=ties))
        m = pe.do(lambda e: e.matmul(banks[0][:, 0:1], block_ones[:, :], above, start=True, stop=True), a, banks.idle(0))
        m = pe.do(lambda e: e.matmul(banks[1][:, 0:1], block_below[:, :], ties, start=True, stop=True), banks.idle(1))
        b = dve.do(lambda e: e.tensor_copy(tied_before, banks[1][:, 0:1]), m)
        b = dve.do(lambda e: e.scalar_tensor_tensor(out=tie_room, in0=banks[0][:, 0:1], scalar=-float(CAP), in1=tied_before,
                                                    op0=ALU.add, op1=ALU.add), b)
        tie_a = dve.do(lambda e: e.tensor_scalar(tie_room, tie_room, -1.0, None, ALU.mult), b)
        a = dve.do(lambda e: e.tensor_tensor_scan(running[:, :], equal[:, :], equal[:, :], 0.0, ALU.add, ALU.max), tie_a)
        a = dve.do(lambda e: e.scalar_tensor_tensor(out=equal[:, :], in0=running[:, :], scalar=tie_room, in1=equal[:, :],
                                                    op0=ALU.is_le, op1=ALU.mult), a)
        taken = greater
        a = dve.do(lambda e: e.tensor_tensor(taken[:, :], greater[:, :], equal[:, :], ALU.add), a)
        a = dve.do(lambda e: e.tensor_tensor_scan(running[:, :], taken[:, :], taken[:, :], 0.0, ALU.add, ALU.max), a)
        m = pe.do(lambda e: e.matmul(banks[0][:, 0:1], block_below[:, :], running[:, W - 1:W], start=True, stop=True), a)
        a = dve.do(lambda e: e.tensor_scalar(base, banks[0][:, 0:1], -1.0 - NONE, None, ALU.add), m)
        banks.used(0, a)
        banks.used(1, a)
        a = dve.do(lambda e: e.scalar_tensor_tensor(out=running[:, :], in0=running[:, :], scalar=base, in1=taken[:, :],
                                                    op0=ALU.add, op1=ALU.mult), a)
        for n in range(CH // PER_BANK):
            t = transpose_into(core, banks[n], PER_BANK, lambda c, n=n: running[:, (n * PER_BANK + c) * P:(n * PER_BANK + c + 1) * P],
                               ident, [a, banks.idle(n)])
            b = dve.do(lambda e, n=n: e.tensor_scalar(slot_i[:, n * PER_BANK:(n + 1) * PER_BANK, :, :].rearrange("p c e g -> p (c e g)"),
                                                      banks[n][:, :], float(NONE), None, ALU.add), t)
            banks.used(n, b)
        flat = lambda x: x[:, :, :, :].rearrange("p c e g -> p (c e g)")
        fi = f1[:, :].bitcast(I32)
        b = dve.do(lambda e: e.tensor_scalar(fi, flat(slot_i), P - 1, None, ALU.bitwise_and), b)
        b = dve.do(lambda e: e.tensor_copy(flat(slot_p), fi), b)
        b = dve.do(lambda e: e.tensor_scalar(fi, flat(slot_i), P.bit_length() - 1, None, ALU.logical_shift_right), b)
        slots_ready = dve.do(lambda e: e.tensor_copy(flat(slot_q), fi), b)

        def make_gates():
            probs, kept = f2, f1
            view = lambda x: x[:, :].rearrange("p (c e g) -> p c e g", e=E, g=G)
            over_e = lambda x: x[:, :].rearrange("p (c e g) -> p c g e", e=E, g=G)
            row = gate_row
            bc = lambda x: x[:, :, :].unsqueeze(2).to_broadcast([P, CH, E, G])
            for n in range(CH // PER_BANK):
                u = n % 2
                t = transpose_into(core, banks[u], PER_BANK, lambda c, n=n: L[:, (n * PER_BANK + c) * P:(n * PER_BANK + c + 1) * P],
                                   ident, [banks.idle(u)])
                b = dve.do(lambda e, n=n, u=u: e.tensor_copy(probs[:, n * BANK:(n + 1) * BANK], banks[u][:, :]), t)
                banks.used(u, b)
            b = dve.do(lambda e: e.tensor_reduce(row[:, :, :], over_e(probs), AX_X, ALU.max), b)
            b = dve.do(lambda e: e.tensor_tensor(view(probs), view(probs), bc(row), ALU.subtract), b)
            b = act.do(lambda e: e.activation(probs[:, :], probs[:, :], ACT.Exp), b)
            b = dve.do(lambda e: e.tensor_reduce(row[:, :, :], over_e(probs), AX_X, ALU.add), b)
            b = dve.do(lambda e: e.reciprocal(row[:, :, :], row[:, :, :]), b)
            b = dve.do(lambda e: e.tensor_tensor(view(probs), view(probs), bc(row), ALU.mult), b)
            b = dve.do(lambda e: e.tensor_scalar(kept[:, :], flat(slot_i), float(NONE), None, ALU.is_lt), b)
            b = dve.do(lambda e: e.tensor_tensor(probs[:, :], probs[:, :], kept[:, :], ALU.mult), b)
            b = dve.do(lambda e: e.tensor_reduce(row[:, :, :], over_e(probs), AX_X, ALU.add), b)
            b = dve.do(lambda e: e.scalar_tensor_tensor(out=row[:, :, :], in0=row[:, :, :], scalar=0.0, in1=row[:, :, :],
                                                        op0=ALU.is_le, op1=ALU.add), b)
            b = dve.do(lambda e: e.reciprocal(row[:, :, :], row[:, :, :]), b)
            order = kept[:, :].rearrange("p (g c e) -> p c e g", g=G, c=CH)
            b = dve.do(lambda e: e.tensor_tensor(order, view(probs), bc(row), ALU.mult), b)
            done["gates"] = core.lane("gates").send(sp, lambda e: e.dma_start(
                g["gate_dram"].rearrange("(n p) e -> p n e", p=P), kept[:, :].rearrange("p (n e) -> p n e", e=E)), b)

        gate_row = tile("gate_row", [P, CH, G])

        PIECES = CH // 2 // PC

        def mark(i, piece):
            x, n = i // 2, i * PIECES + piece
            c0 = (i % 2) * CH // 2 + piece * PC
            cs = slice(c0, c0 + PC)
            shape = [P, PC, G]
            of = lambda t, n: t[:, cs, x, :].unsqueeze(3).to_broadcast(shape + [n])
            b = dve.do(lambda e: e.tensor_tensor(eq_q[n][:, :, :, :], iota_q[:, :].unsqueeze(1).unsqueeze(1).to_broadcast(shape + [G]),
                                                 of(slot_q, G), ALU.is_equal), slots_ready, eq_q.idle(n))
            dve.do(lambda e: e.tensor_tensor(onehot_p[n][:, :, :, :], iota_p[:, :].unsqueeze(1).unsqueeze(1).to_broadcast(shape + [P]),
                                             of(slot_p, P), ALU.is_equal), onehot_p.idle(n))
            a = dve.do(lambda e: e.tensor_tensor(onehot_q[n][:, :, :, 0:G], eq_q[n][:, :, :, :],
                                                 token_high[:, cs, :].unsqueeze(3).to_broadcast(shape + [G]), ALU.mult), b, onehot_q.idle(n))
            a = dve.do(lambda e: e.tensor_scalar(onehot_q[n][:, :, :, G:2 * G], eq_q[n][:, :, :, :], token_low[:, 0:1], None, ALU.mult))
            eq_q.used(n, a)
            done["marked", n] = a

        def listing(i, piece):
            x, h, n = i // 2, i % 2, i * PIECES + piece
            u = 2 + x % 2
            opening, closing = h == 0 and piece == 0, h == 1 and piece == PIECES - 1
            for c in range(PC):
                for gr in range(G):
                    end = c == PC - 1 and gr == G - 1
                    step = (lambda e, c=c, gr=gr, first=opening and c == 0 and gr == 0, final=closing and end: e.matmul(
                        banks[u][:, 0:2 * G], onehot_p[n][:, c, gr, :], onehot_q[n][:, c, gr, :], start=first, stop=final))
                    if end:
                        m = pe.do(step)
                    else:
                        pe.quiet(step, done["marked", n], banks.idle(u) if opening else None)
            onehot_p.used(n, m)
            onehot_q.used(n, m)
            if closing:
                b = act.do(lambda e: e.copy(parts[x][:, :], banks[u][:, 0:2 * G]), m)
                banks.used(u, b)
                done["idx", x] = dve.do(lambda e: e.scalar_tensor_tensor(out=idx[x][:, :], in0=parts[x][:, 0:G], scalar=float(P),
                                                                         in1=parts[x][:, G:2 * G], op0=ALU.mult, op1=ALU.add), b, idx.idle(x))

        def fetch(i):
            x, h = i // 2, i % 2
            if i == 0:
                make_gates()
            pool.wait(done["idx", x], xg.idle(i))
            for c in range(C):
                col = idx[x][:, h * C + c:h * C + c + 1]
                done["xg", i] = core.lane(f"xg{i % 2}").send(pool, lambda e, c=c, col=col: e.indirect_dma_start(
                    xg[i][:, c, :], None, g["xn_dram"], bass.IndirectOffsetOnAxis(ap=col, axis=0)))

        def next_weights(i):
            if i % 2 == 0 and i // 2 + 1 < E:
                load_weights(i // 2 + 1)

        def fetch_gates(i):
            x, h = i // 2, i % 2
            pool.wait(done["gates"], gg.idle(i))
            for c in range(C):
                col = idx[x][:, h * C + c:h * C + c + 1]
                done["gg", i] = core.lane(f"gg{i % 4}").send(pool, lambda e, c=c, col=col: e.indirect_dma_start(
                    gg[i][:, c, :], None, g["gate_dram"], bass.IndirectOffsetOnAxis(ap=col, axis=0)))

        def turn(i):
            for k in range(KD):
                t = transpose_into(core, banks[k], C, lambda c, k=k: xg[i][:, c, k * P:(k + 1) * P], ident, [done["xg", i], banks.idle(k)])
                a = act.do(lambda e, k=k: e.copy(xgT[i][:, k, :], banks[k][:, :]), t, xgT.idle(i))
                banks.used(k, a)
            xg.used(i, t)
            done["xgT", i] = a

        def expand(i, fs):
            x = i // 2
            for f in fs:
                u = 4 + f % 2
                for k in range(KD):
                    m = pe.do(lambda e, f=f, k=k, u=u: e.matmul(banks[u][:, :], w1[x][:, k, f * P:(f + 1) * P], xgT[i][:, k, :],
                                                                start=k == 0, stop=k == KD - 1), done["xgT", i], done["w", x], banks.idle(u))
                a = act.do(lambda e, f=f, u=u: e.activation(hidden[i][:, f, :], banks[u][:, :], ACT.Gelu, bias=b1[:, x, f:f + 1]), m, hidden.idle(i))
                banks.used(u, a)
            xgT.used(i, m)
            done["hidden", i] = a

        def contract(i, c):
            x, h = i // 2, i % 2
            u = 6 + c % 2
            for f in range(KF):
                step = (lambda e, f=f: e.matmul(banks[u][:, 0:D], hidden[i][:, f, c * P:(c + 1) * P], w2[x][:, f, :], start=f == 0, stop=f == KF - 1))
                if f == KF - 1:
                    m = pe.do(step)
                else:
                    pe.quiet(step, done["hidden", i], banks.idle(u))
            a = dve.do(lambda e: e.tensor_tensor(y[c][:, :], banks[u][:, 0:D], b2_row[x][:, :], ALU.add), m, y.idle(c))
            banks.used(u, a)
            b = act.do(lambda e: e.activation(ys[i][:, c, :], y[c][:, :], ACT.Copy, scale=gg[i][:, c, x:x + 1]), a, done["gg", i], ys.idle(i))
            y.used(c, b)
            if c == C - 1:
                hidden.used(i, m)
                w1.used(x, m, a)
                gg.used(i, b)
                done["ys", i] = b

        def scatter(i):
            x, h = i // 2, i % 2
            pool.wait(done["ys", i], done.get(("sc", 2 * x - 1)), done.get(("sc", 2 * x - 2)))
            for c in range(C):
                col = idx[x][:, h * C + c:h * C + c + 1]
                done["sc", i] = core.lane(f"sc{i % 4}").send(pool, lambda e, c=c, col=col: e.indirect_dma_start(
                    g["moe_dram"], bass.IndirectOffsetOnAxis(ap=col, axis=0), ys[i][:, c, :], None, compute_op=ALU.add))
            ys.used(i, done["sc", i])
            if h == 1:
                idx.used(x, done["sc", i], done["sc", i - 1])

        pipeline(NI, [
            (next_weights, 5), (fetch, 2), (fetch_gates, 3), (lambda i: mark(i, 0), 0), (turn, 3), (lambda i: contract(i, 0), 5), (lambda i: mark(i, 1), 0),
            (lambda i: contract(i, 1), 5), (lambda i: listing(i, 0), 0), (lambda i: mark(i, 2), 0), (lambda i: contract(i, 2), 5),
            (lambda i: expand(i, (0, 1)), 4), (lambda i: mark(i, 3), 0), (lambda i: listing(i, 1), 0), (lambda i: contract(i, 3), 5),
            (scatter, 5), (lambda i: expand(i, (2, 3)), 4), (lambda i: listing(i, 2), 0),
            (lambda i: expand(i, tuple(range(4, KF))), 4), (lambda i: listing(i, 3), 0),
        ])
        core.everyone_waits_for_everyone()


def layer_one(core, A, g):
    pe, act, dve, pool, sp = core.engines
    banks, ident, cols = core.banks, g["ident"], g["cols"]
    B, S, D, T, KD, H, KW, TT, NT = (g[n] for n in ("B", "S", "D", "T", "KD", "HEADS", "KW", "TILE_T", "NT"))
    F = A["L1_ffn_W1"].shape[1]
    KF = F // P
    C = S // P
    HC = C // 2
    HD = D // H
    PAD = P - TT
    HJ = P // HD
    BC = 4
    x1_dram = g["x1_dram"].rearrange("(b c p) d -> b p c d", c=C, p=P)
    moe_dram = g["moe_dram"].rearrange("(b c p) d -> b p c d", c=C, p=P)
    out_dram = g["out"].rearrange("b (c p) d -> b c p d", p=P)

    with ExitStack() as part:
        def tile(name, shape, dt=F32):
            return core.tile(part, name, shape, dt)

        def ring(name, n, shape):
            return core.ring(part, name, n, shape)

        w_fc, w1, w2 = tile("w_fc", [P, KD, D]), tile("l1_w1", [P, KD, F]), tile("l1_w2", [P, KF, D])
        w_pe = tile("w_pe", [P, 2, HJ, KW])
        pe_bias, energy = tile("pe_bias", [P, 2, KW]), tile("energy", [P, H, KW])
        b1, per_count = tile("l1_b1", [P, KF]), tile("per_count", [P, S])
        x2, moe, xh, v = (ring(n, k, [P, HC, D]) for n, k in (("x2_", 7), ("moe", 2), ("l1_xh", 2), ("l1_v", 2)))
        h4T, hidden = ring("h4T", 2, [P, KD, BANK]), ring("l1_hidden", 1, [P, KF, BANK])
        row_in, row_mid, row_out = ring("row_in", 1, [P, D]), ring("row_mid", 1, [P, 2, D]), ring("row_out", 1, [P, 2, D])
        h3T, avgT = ring("h3T", 2, [P, KD, S]), ring("avgT", 2, [P, KD, PAD + S + PAD])
        convT = ring("convT", 1, [P, KD, S])
        pc, e1, w = ring("pc", 2, [P, 2, H, KW]), ring("e1", 3, [P, H, KW]), ring("w", 2, [P, KW, H])
        top, total = ring("top", 2, [P, H]), ring("total", 2, [P, H])
        band, bandT = ring("band", 2, [TT, P, H]), ring("bandT", 2, [P, H, TT])
        window, conv = ring("window", 2, [P, D]), ring("conv", 2, [TT, D])
        o = ring("o", 2, [P, D])
        stats, moments, scratch = tile("l1_stats", [P, HC, 6]), tile("l1_moments", [P, HC, 2]), tile("l1_scratch", [P, 4, HC])
        small_bank, expand_bank, contract_bank = (Ring([banks[u] for u in us]) for us in ((0, 1, 2, 3), (4, 5), (6, 7)))
        uses = [0]

        def take():
            uses[0] += 1
            return uses[0]

        a = pool.do(lambda e: e.memset(w_pe[:, :, :, :], 0.0))
        lane = core.lane("l1_weights")
        loads = [(w_fc[:, :, :], A["L1_attn_W_fcT"].rearrange("(k p) n -> p k n", p=P)),
                 (w1[:, :, :], A["L1_ffn_W1"].rearrange("(k p) n -> p k n", p=P)),
                 (w2[:, :, :], A["L1_ffn_W2"].rearrange("(k p) n -> p k n", p=P)),
                 (pe_bias[:, :, :].rearrange("p a k -> p (a k)"), A["L1_attn_b_pe"].rearrange("(a d) -> a d", a=1).to_broadcast([P, 2 * KW])),
                 (energy[:, :, :].rearrange("p h k -> p (h k)"), A["L1_attn_stt_energy"].rearrange("a h b k -> (a b) (h k)").to_broadcast([P, H * KW])),
                 (b1[:, :], A["L1_ffn_b1_c"]), (per_count[:, :], A["per_count"].to_broadcast([P, S]))]
        loads += [(w_pe[j * HD:(j + 1) * HD, :, j, :], A["L1_attn_W_pe"].rearrange("d (a k) -> d a k", a=2)) for j in range(HJ)]
        for dst, src in loads:
            weights = lane.send(sp, lambda e, dst=dst, src=src: e.dma_start(dst, src), a)
        for i in range(2):
            pool.quiet(lambda e, i=i: e.memset(avgT[i][:, :, 0:PAD], 0.0))
            pads_ready = pool.do(lambda e, i=i: e.memset(avgT[i][:, :, PAD + S:], 0.0))
        done = {}

        def load(b, half):
            n = 2 * b + half
            cs = slice(half * HC, (half + 1) * HC)
            if half == 0:
                done["row_in", b] = core.lane("row_in").send(sp, lambda e: e.dma_start(
                    row_in[b][:, :], g["row1_dram"][b:b + 1, 0:D].to_broadcast([P, D])), row_in.idle(b))
            done["x1", n] = core.lane(f"l1_x{n % 7}").send(sp, lambda e: e.dma_start(x2[n][:, :, :], x1_dram[b][:, cs, :]), x2.idle(n))
            done["moe", n] = core.lane(f"l1_moe{n % 2}").send(sp, lambda e: e.dma_start(moe[n][:, :, :], moe_dram[b][:, cs, :]), moe.idle(n))

        def join(b, half):
            n = 2 * b + half
            bc = row_in[b][:, :].unsqueeze(1).to_broadcast([P, HC, D])
            done["gained", n] = pool.do(lambda e: e.tensor_tensor(moe[n][:, :, :], moe[n][:, :, :], bc, ALU.mult), done["moe", n], done["row_in", b])
            if half == 1:
                row_in.used(b, done["gained", n])

        def norm_in(b, half):
            n = 2 * b + half
            a = dve.do(lambda e: e.tensor_tensor(x2[n][:, :, :], x2[n][:, :, :], moe[n][:, :, :], ALU.add), done["gained", n], done["x1", n])
            moe.used(n, a)
            y, a = statistics(core, stats, moments, lambda c: x2[n][:, c, :], HC, 1e-5, scratch, a)
            dve.wait(xh.idle(n))
            dve.wait(a)
            for c in range(HC):
                a = dve.do(lambda e, c=c: e.tensor_scalar(xh[n][:, c, :], x2[n][:, c, :], moments[:, c, 0:1], y[:, c:c + 1], ALU.subtract, ALU.mult))
            done["xh", n] = a

        def to_features(b, half, source, ready, target, scale, shift, free):
            for k in range(KD):
                u = take()
                t = transpose_into(core, small_bank[u], HC, lambda c, k=k: source[:, c, k * P:(k + 1) * P], ident, [ready, small_bank.idle(u)])
                a = act.do(lambda e, k=k, u=u: e.activation(target(k), small_bank[u][:, :], ACT.Identity, scale=cols[:, g[scale] + k, b:b + 1],
                                                            bias=cols[:, g[shift] + k, b:b + 1]), t, free)
                small_bank.used(u, a)
            return t, a

        def turn_in(b, half):
            n = 2 * b + half
            t, a = to_features(b, half, xh[n], done["xh", n], lambda k: h3T[b][:, k, half * BANK:(half + 1) * BANK], "SCALE1A", "SHIFT1A", h3T.idle(b))
            xh.used(n, t)
            done["h3T", b] = a

        def average(b, k):
            view = avgT[b][:, k, PAD:PAD + S]
            a = dve.do(lambda e: e.tensor_tensor_scan(view, h3T[b][:, k, :], g["zero"][:, 0:1].to_broadcast([P, S]), 0.0, ALU.add, ALU.add),
                       done["h3T", b], avgT.idle(b), weights)
            done["avgT", b] = dve.do(lambda e: e.tensor_tensor(view, view, per_count[:, :], ALU.mult), a)

        def kernel_product(b, c, j):
            n, u = b * C + c, take()
            m = pe.do(lambda e: e.matmul(small_bank[u][:, 0:2 * HJ * KW], avgT[b][:, j, PAD + c * P:PAD + (c + 1) * P],
                                         w_pe[:, :, :, :].rearrange("p a j k -> p (a j k)"), start=True, stop=True),
                      done["avgT", b], weights, small_bank.idle(u))
            a = dve.do(lambda e: e.tensor_tensor(
                pc[n][:, :, j * HJ:(j + 1) * HJ, :], small_bank[u][:, 0:2 * HJ * KW].rearrange("p (a j k) -> p a j k", a=2, j=HJ),
                pe_bias[:, :, :].unsqueeze(2).to_broadcast([P, 2, HJ, KW]), ALU.add), m, pc.idle(n))
            small_bank.used(u, a)
            done["pc", n] = a

        def gate(b, c):
            n = b * C + c
            done["gate", n] = act.do(lambda e: e.activation(pc[n][:, 1, :, :], pc[n][:, 1, :, :], ACT.Tanh, scale=0.5), done["pc", n])

        def energies(b, c):
            n = b * C + c
            a = dve.do(lambda e: e.scalar_tensor_tensor(out=e1[n][:, :, :], in0=pc[n][:, 1, :, :], scalar=1.0, in1=pc[n][:, 0, :, :],
                                                        op0=ALU.add, op1=ALU.mult), done["gate", n], e1.idle(n))
            pc.used(n, a)
            a = dve.do(lambda e: e.scalar_tensor_tensor(out=e1[n][:, :, :], in0=e1[n][:, :, :], scalar=0.5, in1=energy[:, :, :],
                                                        op0=ALU.mult, op1=ALU.add), a)
            a = dve.do(lambda e: e.tensor_reduce(top[n][:, :], e1[n][:, :, :], AX_X, ALU.max), a, top.idle(n))
            a = pool.do(lambda e: e.tensor_tensor(e1[n][:, :, :], e1[n][:, :, :], top[n][:, :].unsqueeze(2).to_broadcast([P, H, KW]), ALU.subtract), a)
            top.used(n, a)
            done["energy", n] = a

        def exponentials(b, c):
            n = b * C + c
            done["exp", n] = act.do(lambda e: e.activation(e1[n][:, :, :], e1[n][:, :, :], ACT.Exp), done["energy", n])

        def softmax(b, c):
            n = b * C + c
            a = dve.do(lambda e: e.tensor_reduce(total[n][:, :], e1[n][:, :, :], AX_X, ALU.add), done["exp", n])
            a = dve.do(lambda e: e.reciprocal(total[n][:, :], total[n][:, :]), a)
            a = dve.do(lambda e: e.tensor_tensor(w[n][:, :, :].rearrange("p k h -> p h k"), e1[n][:, :, :],
                                                 total[n][:, :].unsqueeze(2).to_broadcast([P, H, KW]), ALU.mult), a, w.idle(n))
            e1.used(n, a)
            row = (P + 1) * H
            t = c * P
            while t < (c + 1) * P:
                i, tt = t // TT, t % TT
                rows = min(TT - tt, (c + 1) * P - t)
                off = tt * row + (PAD - KW + 1) * H
                dst = g["band_dram"][b % 2][i:i + 1, off:off + rows * row].rearrange("a (n r) -> (a n) r", r=row)[:, 0:KW * H]
                src = w[n][t - c * P:t - c * P + rows, :, :].rearrange("p k h -> p (k h)")
                sent = core.lane(f"w{n % 2}").send(sp, lambda e, dst=dst, src=src: e.dma_start(dst, src), a, done.get(("band", b - 2, i)))
                t += rows
            w.used(n, sent)
            done["w", b, c] = sent

        def load_band(n):
            b, i = divmod(n, NT)
            if b == B:
                return
            chunks = range(i * TT // P, min(C - 1, (i * TT + TT - 1) // P) + 1)
            done["band", b, i] = core.lane(f"band{n % 2}").send(sp, lambda e: e.dma_start(
                band[n][:, :, :].rearrange("t s h -> t (s h)"), g["band_dram"][b % 2][i:i + 1, 0:TT * P * H].rearrange("a (t r) -> (a t) r", t=TT)),
                band.idle(n), *[done["w", b, c] for c in chunks])

        def band_turn(b, i, qs):
            n = b * NT + i
            for q in qs:
                u = take()
                for j in range(BC):
                    h = q * BC + j
                    step = lambda e, h=h, j=j, u=u: e.transpose(small_bank[u][:, j * TT:(j + 1) * TT], band[n][:, :, h], ident[0:TT, 0:TT])
                    if j < BC - 1:
                        pe.quiet(step, done["band", b, i], small_bank.idle(u))
                    else:
                        t = pe.do(step)
                a = act.do(lambda e, q=q, u=u: e.copy(bandT[n][:, q * BC:(q + 1) * BC, :].rearrange("p h t -> p (h t)"), small_bank[u][:, 0:BC * TT]),
                           t, bandT.idle(n))
                small_bank.used(u, a)
            done["bandT", n] = a
            if qs[-1] == H // BC - 1:
                band.used(n, t)
                load_band(n + 2)

        def window_turn(b, i):
            n, u = b * NT + i, take()
            for k in range(KD):
                t = pe.do(lambda e, k=k: e.transpose(small_bank[u][:, k * P:(k + 1) * P], avgT[b][:, k, i * TT:i * TT + P], ident[:, :]),
                          small_bank.idle(u), pads_ready)
            if i == NT - 1:
                avgT.used(b, t)
            a = act.do(lambda e: e.copy(window[n][:, :], small_bank[u][:, 0:D]), t, window.idle(n))
            small_bank.used(u, a)
            done["window", n] = a

        def band_product(b, i):
            n, u = b * NT + i, take()
            for h in range(H):
                step = lambda e, h=h: e.matmul(small_bank[u][0:TT, h * HD:(h + 1) * HD], bandT[n][:, h, :], window[n][:, h * HD:(h + 1) * HD],
                                               start=True, stop=True)
                if h < H - 1:
                    pe.quiet(step, done["bandT", n], done["window", n], small_bank.idle(u))
                else:
                    m = pe.do(step)
            bandT.used(n, m)
            window.used(n, m)
            a = act.do(lambda e: e.copy(conv[n][:, :], small_bank[u][0:TT, 0:D]), m, conv.idle(n))
            small_bank.used(u, a)
            done["conv", n] = a

        def conv_turn(b, i):
            n, u = b * NT + i, take()
            size = min(TT, S - i * TT)
            for k in range(KD):
                t = pe.do(lambda e, k=k: e.transpose(small_bank[u][:, k * TT:(k + 1) * TT], conv[n][:, k * P:(k + 1) * P], ident[0:TT, 0:TT]),
                          done["conv", n], small_bank.idle(u))
            conv.used(n, t)
            a = act.do(lambda e: e.copy(convT[b][:, :, i * TT:i * TT + size],
                                        small_bank[u][:, 0:KD * TT].rearrange("p (k t) -> p k t", k=KD)[:, :, 0:size]), t, convT.idle(b))
            small_bank.used(u, a)
            done["convT", b] = a

        def mix(b, c):
            n, u = 2 * b + c // HC, take()
            for k in range(KD):
                pe.quiet(lambda e, k=k: e.matmul(small_bank[u][:, 0:D], convT[b][:, k, c * P:(c + 1) * P], w_fc[:, k, :], start=k == 0, stop=False),
                         done["convT", b], small_bank.idle(u))
            for k in range(KD):
                m = pe.do(lambda e, k=k: e.matmul(small_bank[u][:, k * P:(k + 1) * P], h3T[b][:, k, c * P:(c + 1) * P], ident[:, :],
                                                  start=False, stop=k == KD - 1))
            a = act.do(lambda e: e.copy(v[n][:, c % HC, :], small_bank[u][:, 0:D]), m, v.idle(n))
            small_bank.used(u, a)
            done["v", n] = a
            if c == C - 1:
                convT.used(b, m)
                h3T.used(b, m)

        def load_rows(b):
            done["row_mid", b] = core.lane("row_mid").send(sp, lambda e: e.dma_start(
                row_mid[b][:, :, :].rearrange("p a d -> p (a d)"), g["row1_dram"][b:b + 1, D:3 * D].to_broadcast([P, 2 * D])), row_mid.idle(b))

        def load_out_rows(b):
            done["row_out", b] = core.lane("row_out").send(sp, lambda e: e.dma_start(
                row_out[b][:, :, :].rearrange("p a d -> p (a d)"), g["row1_dram"][b:b + 1, 3 * D:5 * D].to_broadcast([P, 2 * D])), row_out.idle(b))

        def norm_mid_a(b, half):
            n = 2 * b + half
            y, a = statistics(core, stats, moments, lambda c: v[n][:, c, :], HC, 1e-6, scratch, done["v", n])
            dve.wait(a)
            for c in range(HC):
                a = dve.do(lambda e, c=c: e.tensor_scalar(v[n][:, c, :], v[n][:, c, :], moments[:, c, 0:1], y[:, c:c + 1], ALU.subtract, ALU.mult))
            bc = lambda r: row_mid[b][:, r:r + 1, :].to_broadcast([P, HC, D])
            pool.do(lambda e: e.tensor_tensor(x2[n][:, :, :], x2[n][:, :, :], bc(1), ALU.add), done["row_mid", b], done["xh", n])
            a = pool.do(lambda e: e.tensor_tensor(v[n][:, :, :], v[n][:, :, :], bc(0), ALU.mult), a)
            if half == 1:
                row_mid.used(b, a)
            done["mid", n] = a

        def norm_mid_b(b, half):
            n = 2 * b + half
            a = dve.do(lambda e: e.tensor_tensor(x2[n][:, :, :], x2[n][:, :, :], v[n][:, :, :], ALU.add), done["mid", n])
            y, a = statistics(core, stats, moments, lambda c: x2[n][:, c, :], HC, 1e-5, scratch, a)
            dve.wait(a)
            for c in range(HC):
                a = dve.do(lambda e, c=c: e.tensor_scalar(v[n][:, c, :], x2[n][:, c, :], moments[:, c, 0:1], y[:, c:c + 1], ALU.subtract, ALU.mult))
            done["h4", n] = a

        def turn_mid(b, half):
            n = 2 * b + half
            t, a = to_features(b, half, v[n], done["h4", n], lambda k: h4T[n][:, k, :], "SCALE1B", "SHIFT1B", h4T.idle(n))
            v.used(n, t)
            done["h4T", n] = a

        def expand(b, half, f):
            n, u = 2 * b + half, f
            for k in range(KD):
                m = pe.do(lambda e, k=k: e.matmul(expand_bank[u][:, :], w1[:, k, f * P:(f + 1) * P], h4T[n][:, k, :],
                                                  start=k == 0, stop=k == KD - 1), done["h4T", n], expand_bank.idle(u))
            a = act.do(lambda e: e.activation(hidden[n][:, f, :], expand_bank[u][:, :], ACT.Relu, bias=b1[:, f:f + 1]), m, hidden.idle(n))
            expand_bank.used(u, a)
            done["hidden", n] = a
            if f == KF - 1:
                h4T.used(n, m)

        def row_gain(b, half):
            n = 2 * b + half
            bc = row_out[b][:, 1:2, :].to_broadcast([P, HC, D])
            done["x3", n] = pool.do(lambda e: e.tensor_tensor(x2[n][:, :, :], x2[n][:, :, :], bc, ALU.add), done["row_out", b], done["h4", n])

        def contract(b, half, c):
            n, u = 2 * b + half, c
            for f in range(KF):
                step = (lambda e, f=f: e.matmul(contract_bank[u][:, 0:D], hidden[n][:, f, c * P:(c + 1) * P], w2[:, f, :], start=f == 0, stop=f == KF - 1))
                if f == KF - 1:
                    m = pe.do(step)
                else:
                    pe.quiet(step, done["hidden", n], contract_bank.idle(u))
            if c == HC - 1:
                hidden.used(n, m)
            a = dve.do(lambda e: e.tensor_tensor(o[c][:, :], contract_bank[u][:, 0:D], row_out[b][:, 0, :], ALU.mult), m, done["row_out", b], o.idle(c))
            contract_bank.used(u, a)
            a = dve.do(lambda e: e.tensor_tensor(o[c][:, :], o[c][:, :], x2[n][:, c, :], ALU.add), a, done["x3", n])
            o.used(c, core.lane(f"out{c % 2}").send(sp, lambda e: e.dma_start(out_dram[b, half * HC + c], o[c][:, :]), a))
            if c == HC - 1:
                x2.used(n, a)
                if half == 1:
                    row_out.used(b, a)

        plan = []

        def at(place, lag, stage, *args):
            plan.append((place, len(plan), lambda b: stage(b, *args), lag))

        at(0.0, 3, load_out_rows)
        at(2.0, 2, load_rows)
        at(0.3, 0, load, 0)
        at(3.5, 0, join, 0)
        at(4.5, 0, norm_in, 0)
        at(6.9, 0, load, 1)
        at(8.5, 0, join, 1)
        at(10.0, 0, norm_in, 1)
        at(0.0, 1, turn_in, 0)
        at(0.15, 1, turn_in, 1)
        at(0.4, 1, average, 0)
        at(0.6, 1, average, 1)
        for c in range(C):
            start = 1.8 + 1.25 * c
            for j in range(KD):
                at(start + 0.4 * j, 1, kernel_product, c, j)
            at(start + 0.75, 1, gate, c)
            at(start + 1.05, 1, energies, c)
            at(start + 1.5, 1, exponentials, c)
            at(start + 2.0, 1, softmax, c)
        at(6.0, 1, lambda b: [load_band(n) for n in range(2)] if b == 0 else None)
        mixed = 0
        for i in range(NT):
            at(i + 0.1, 2, band_turn, i, (0, 1))
            at(i + 0.4, 2, window_turn, i)
            at(i + 0.6, 2, band_turn, i, (2, 3))
            at(i + 1.2, 2, band_product, i)
            at(i + 1.7, 2, conv_turn, i)
            while mixed < C and (mixed + 1) * P <= (i + 1) * TT:
                at(i + 2.05, 2, mix, mixed)
                mixed += 1
        while mixed < C:
            at(NT + 1.3, 2, mix, mixed)
            mixed += 1
        at(7.4, 2, norm_mid_a, 0)
        at(8.8, 2, norm_mid_b, 0)
        at(11.1, 2, turn_mid, 0)
        at(0.2, 3, norm_mid_a, 1)
        at(1.7, 3, norm_mid_b, 1)
        at(4.2, 3, turn_mid, 1)
        at(0.9, 3, row_gain, 0)
        at(4.3, 3, row_gain, 1)
        for half in range(2):
            for f in range(KF):
                at(6.4 * half + 0.4 * f + 0.25, 3, expand, half, f)
            for c in range(HC):
                at(6.4 * half + 3.45 + 0.8 * c, 3, contract, half, c)
        pipeline(B, [(stage, lag) for _, _, stage, lag in sorted(plan, key=lambda z: z[:2])])
        core.everyone_waits_for_everyone()


def columns(vector):
    return vector.reshape(-1, P).T


def kernel(**inputs):
    import numpy as np
    import concourse.bacc as bacc
    from concourse.bass_utils import run_bass_kernel_spmd

    x = {name: np.asarray(a) for name, a in inputs.items()}
    B, S, D = x["L0_attn_x"].shape
    E = x["L0_ffn_router_weight"].shape[0]
    keep = ["L0_attn_x", "L0_attn_W_ret", "L0_attn_W1", "L0_attn_W2", "L0_attn_b2", "L0_attn_ln2_scale", "L0_attn_ln2_bias",
            "L0_ffn_norm_weight", "L0_ffn_router_bias", "L0_ffn_router_weight", "L0_ffn_fc2_bias", "L0_wmod", "L1_wmod",
            "L1_attn_W_pe", "L1_attn_b_pe", "L1_attn_stt_energy", "L1_attn_gamma", "L1_attn_beta", "L1_ffn_W1", "L1_ffn_W2", "L1_ffn_b2"]
    arrays = {n: x[n] for n in keep}
    arrays["L0_cT"], arrays["L1_cT"] = x["L0_c"].T, x["L1_c"].T
    arrays["L0_ffn_router_wT"] = x["L0_ffn_router_weight"].T
    arrays["L0_ffn_fc1_wT"] = x["L0_ffn_fc1_weight"].transpose(0, 2, 1)
    arrays["L0_ffn_fc2_wT"] = x["L0_ffn_fc2_weight"].transpose(0, 2, 1)
    arrays["L1_attn_W_fcT"] = x["L1_attn_W_fc"].T
    for n in ("L0_attn_b_ret", "L0_attn_ln1_scale", "L0_attn_ln1_bias", "L0_attn_b1", "L0_ffn_fc1_bias", "L1_ffn_b1"):
        arrays[n + "_c"] = columns(x[n])
    p = np.arange(P)
    G = P // E
    same = p[:, None] // G == p[None, :] // G
    arrays["block_ones"] = same.astype(np.float32)
    arrays["block_below"] = (same & (p[:, None] < p[None, :])).astype(np.float32)
    arrays["iota_row"] = np.tile(p.astype(np.float32), (P, 1))
    arrays["iota_column"] = p.astype(np.float32).reshape(P, 1)
    c, gr = np.divmod(np.arange(P), G)
    arrays["chunk_ids"] = np.tile((gr * (B * S // G // P) + c).astype(np.float32), (P, 1))
    arrays["per_count"] = (np.float32(1) / np.arange(1, S + 1, dtype=np.float32)).reshape(1, S)

    nc = bacc.Bacc("TRN2", target_bir_lowering=False, num_devices=1)
    feed, A = {}, {}
    for name, a in arrays.items():
        a = np.ascontiguousarray(a)
        feed[f"in_{name}"] = a
        A[name] = nc.dram_tensor(f"in_{name}", a.shape, mybir.dt.from_np(a.dtype), kind="ExternalInput").ap()
    out = nc.dram_tensor("out", (B, S, D), F32, kind="ExternalOutput").ap()
    build(nc, A, out)
    r = run_bass_kernel_spmd(nc, [feed], core_ids=[0])
    return r.results[0]["out"]
```

```python
from contextlib import ExitStack

import concourse.bass as bass
from concourse import mybir

F32 = mybir.dt.float32
F32R = mybir.dt.float32r
BF16 = mybir.dt.bfloat16
I32 = mybir.dt.int32
U32 = mybir.dt.uint32
ALU = mybir.AluOpType
ACT = mybir.ActivationFunctionType
AX_X = mybir.AxisListType.X

P = 128
BANK = 512


class Engine:

    def __init__(self, name, sem):
        self.name, self.sem, self.count, self.queue, self.reached = name, sem, 0, [], {}

    def wait(self, *tokens):
        for token in tokens:
            if token is None:
                continue
            if isinstance(token, list):
                self.wait(*token)
                continue
            sem, value, key = token
            if self.reached.get(key, 0) < value:
                self.reached[key] = value
                self.queue.append(lambda e, s=sem, v=value: e.wait_ge(s, v))

    def quiet(self, instruction, *tokens):
        self.wait(*tokens)
        self.queue.append(instruction)

    def do(self, instruction, *tokens):
        self.wait(*tokens)
        self.count += 1
        self.queue.append(lambda e: instruction(e).then_inc(self.sem, 1))
        return (self.sem, self.count, self.name)

    def last(self):
        return (self.sem, self.count, self.name) if self.count else None

    def replay(self, e):
        for instruction in self.queue:
            instruction(e)


class Lane:

    def __init__(self, name, sem):
        self.name, self.sem, self.count = name, sem, 0

    def send(self, engine, instruction, *tokens):
        engine.wait(*tokens)
        self.count += 16
        engine.queue.append(lambda e: instruction(e).then_inc(self.sem, 16))
        return (self.sem, self.count, self.name)

    def last(self):
        return (self.sem, self.count, self.name) if self.count else None


class Ring:

    def __init__(self, buffers):
        self.buffers, self.free = buffers, [[] for _ in buffers]

    def __getitem__(self, i):
        return self.buffers[i % len(self.buffers)]

    def idle(self, i):
        return self.free[i % len(self.buffers)]

    def used(self, i, *tokens):
        self.free[i % len(self.buffers)] = list(tokens)


class Core:

    def __init__(self, nc, ctx):
        self.nc, self.ctx, self.lanes, self.names = nc, ctx, {}, {}
        self.pe, self.act, self.dve, self.pool, self.sp = (
            Engine(n, ctx.enter_context(nc.semaphore("done_" + n))) for n in ("pe", "act", "dve", "pool", "sp"))
        self.engines = [self.pe, self.act, self.dve, self.pool, self.sp]
        self.banks = Ring([ctx.enter_context(nc.psum_tensor(f"bank{i}", [P, BANK], F32)) for i in range(8)])

    def lane(self, name):
        if name not in self.lanes:
            self.lanes[name] = Lane(name, self.ctx.enter_context(self.nc.semaphore("dma_" + name)))
        return self.lanes[name]

    def tile(self, ctx, name, shape, dt=F32):
        self.names[name] = self.names.get(name, 0) + 1
        if self.names[name] > 1:
            name = f"{name}_v{self.names[name]}"
        return ctx.enter_context(self.nc.sbuf_tensor(name, shape, dt))

    def split_tile(self, ctx, name, shape):
        return Split(self.tile(ctx, name + "_high", shape, F32R), self.tile(ctx, name + "_low", shape, F32R))

    def split_ring(self, ctx, name, n, shape):
        return Ring([self.split_tile(ctx, f"{name}{i}", shape) for i in range(n)])

    def ring(self, ctx, name, n, shape, dt=F32):
        return Ring([self.tile(ctx, f"{name}{i}", shape, dt) for i in range(n)])

    def everyone_waits_for_everyone(self):
        ends = [e.last() for e in self.engines] + [lane.last() for lane in self.lanes.values()]
        for e in self.engines:
            e.wait(*[t for t in ends if t is not None])


def pipeline(count, schedule):
    for step in range(count + max(lag for _, lag in schedule)):
        for stage, lag in schedule:
            if 0 <= step - lag < count:
                stage(step - lag)


def part_of(stage, *args):
    return lambda i: stage(i, *args)


def inverse_root(core, scratch, variance, eps, *tokens):
    dve = core.dve
    v, half, t, y = (scratch[:, i, :] for i in range(4))
    a = dve.do(lambda e: e.tensor_scalar(v, variance, eps, None, ALU.add), *tokens)
    dve.quiet(lambda e: e.tensor_scalar(half, variance, -0.5, -0.5 * eps, ALU.mult, ALU.add))
    a = dve.do(lambda e: e.tensor_scalar(t.bitcast(I32), v.bitcast(I32), 1, None, ALU.logical_shift_right), a)
    a = dve.do(lambda e: e.tensor_scalar(y.bitcast(I32), t.bitcast(I32), -1.0, float(0x5F3759DF), ALU.mult, ALU.add), a)
    for _ in range(3):
        a = dve.do(lambda e: e.tensor_tensor(t, y, y, ALU.mult), a)
        a = dve.do(lambda e: e.tensor_tensor(t, t, half, ALU.mult), a)
        a = dve.do(lambda e: e.scalar_tensor_tensor(out=y, in0=t, scalar=1.5, in1=y, op0=ALU.add, op1=ALU.mult), a)
    return y, a


def statistics(core, stats, moments, source, n, eps, scratch, *tokens):
    dve = core.dve
    for i in range(n):
        a = dve.do(lambda e, i=i: e.bn_stats(stats[:, i, :], source(i)), *(tokens if i == 0 else ()))
    dve.wait(a)
    for i in range(n):
        a = dve.do(lambda e, i=i: e.bn_aggr(moments[:, i, :], stats[:, i, :]))
    return inverse_root(core, scratch, moments[:, 0:n, 1], eps, a)


class Split:

    def __init__(self, high, low):
        self.high, self.low = high, low

    def __getitem__(self, key):
        return Split(self.high[key], self.low[key])

    def pairs(self, other):
        return [(self.low, other.high), (self.high, other.low), (self.high, other.high)]


def split(core, full, parts, subtractor, *tokens):
    high = core.act.do(lambda e: e.copy(parts.high, full), *tokens)
    return subtractor.do(lambda e: e.tensor_tensor(parts.low, full, parts.high, ALU.subtract), high)


def transpose_into(core, bank, columns, source, ident, wait, rows=P):
    for i in range(columns):
        core.pe.wait(*wait)
        wait = ()
        step = (lambda e, i=i: e.transpose(bank[:, i * rows:(i + 1) * rows], source(i), ident[0:rows, 0:rows]))
        token = core.pe.do(step) if i == columns - 1 else core.pe.quiet(step)
    return token


def build(nc, A, out, debug=None):
    B, S, D = A["L0_attn_x"].shape
    T = B * S
    F = A["L0_attn_W1"].shape[1]
    E = A["L0_ffn_router_weight"].shape[0]
    CAP = T // E
    KD, KF = D // P, F // P
    NM = 6 * D
    HEADS, KW = A["L1_attn_stt_energy"].shape[1], A["L1_attn_stt_energy"].shape[3]
    assert D == 2 * P and S == 1024 and CAP == 1024 and E == 16

    ctx = ExitStack()
    with ctx:
        core = Core(nc, ctx)
        pe, act, dve, pool, sp = core.engines
        banks = core.banks

        x1_dram = nc.dram_tensor("x_after_retention", [T, D], F32, kind="Internal").ap()
        xn_dram = nc.dram_tensor("moe_input", [T, D], F32, kind="Internal").ap()
        logit_dram = nc.dram_tensor("router_logits", [E, T], F32, kind="Internal").ap()
        moe_dram = nc.dram_tensor("moe_output", [T, D], F32, kind="Internal").ap()
        gate_dram = nc.dram_tensor("gates", [T, E], F32, kind="Internal").ap()
        row0_dram = nc.dram_tensor("rows_layer0", [B, 4 * D], F32, kind="Internal").ap()
        row1_dram = nc.dram_tensor("rows_layer1", [B, 5 * D], F32, kind="Internal").ap()
        TILE_T = 96
        NT = -(-S // TILE_T)
        BAND_SIZE = 1568 * P
        assert BAND_SIZE >= (TILE_T + 1) * (P + 1) * HEADS
        band_dram = [nc.dram_tensor(f"bands{i}", [NT, BAND_SIZE], F32, kind="Internal").ap() for i in range(2)]

        ident = core.tile(ctx, "ident", [P, P])
        cols = core.tile(ctx, "mod_columns", [P, 12, B])
        zero = core.tile(ctx, "zero", [P, 1])
        pool.do(lambda e: e.memset(ident[:, :], 0.0))
        zero_ready = pool.do(lambda e: e.memset(zero[:, :], 0.0))
        ident_ready = pool.do(lambda e: e.affine_select(
            out=ident[:, :], in_=ident[:, :], compare_op=ALU.not_equal, fill=1.0, base=0,
            pattern=[[-1, P]], channel_multiplier=1), pool.last())

        mlp_weights = ExitStack()
        split_w1, split_w2 = core.split_tile(mlp_weights, "w1", [P, KD, F]), core.split_tile(mlp_weights, "w2", [P, KF, D])

        SHIFT0, SCALE0, SHIFT1A, SCALE1A, SHIFT1B, SCALE1B = range(0, 12, 2)
        with ExitStack() as part:
            rows_sent = []
            mod = [core.tile(part, f"mod{l}", [B, NM]) for l in range(2)]
            for l in range(2):
                cT = core.tile(part, f"cT{l}", [P, KD, B])
                th = core.tile(part, f"c_tanh{l}", [P, KD, B])
                sc = core.tile(part, f"c_silu{l}", [P, KD, B])
                wm = core.tile(part, f"wmod{l}", [P, KD, NM])
                lane = core.lane(f"cond{l}")
                lane.send(sp, lambda e, l=l, cT=cT: e.dma_start(cT[:, :, :], A[f"L{l}_cT"].rearrange("(k p) b -> p k b", p=P)))
                got = lane.send(sp, lambda e, l=l, wm=wm: e.dma_start(wm[:, :, :], A[f"L{l}_wmod"].rearrange("(k p) n -> p k n", p=P)))
                a = act.do(lambda e, th=th, cT=cT: e.activation(th[:, :, :], cT[:, :, :], ACT.Tanh, scale=0.5), got)
                a = dve.do(lambda e, th=th, cT=cT: e.scalar_tensor_tensor(
                    out=th[:, :, :], in0=th[:, :, :], scalar=1.0, in1=cT[:, :, :], op0=ALU.add, op1=ALU.mult), a)
                a = dve.do(lambda e, th=th, sc=sc: e.tensor_scalar(sc[:, :, :], th[:, :, :], 0.5, None, ALU.mult), a)
                for n in range(NM // BANK):
                    u = 3 * l + n
                    for k in range(KD):
                        step = (lambda e, u=u, n=n, k=k, sc=sc, wm=wm: e.matmul(
                            banks[u][0:B, :], sc[:, k, :], wm[:, k, n * BANK:(n + 1) * BANK], start=k == 0, stop=k == KD - 1))
                        m = pe.do(step, a, got)
                    a2 = dve.do(lambda e, u=u, n=n, l=l: e.tensor_copy(mod[l][:, n * BANK:(n + 1) * BANK], banks[u][0:B, :]), m)
                    banks.used(u, a2)

            for name, parts, k in (("L0_attn_W1", split_w1, KD), ("L0_attn_W2", split_w2, KF)):
                full = core.tile(part, name, [P, k, A[name].shape[1]])
                got = core.lane(name).send(sp, lambda e, full=full, name=name: e.dma_start(full[:, :, :], A[name].rearrange("(k p) n -> p k n", p=P)))
                split(core, full[:, :, :], parts[:, :, :], dve, got)

            def field(l, i):
                return mod[l][:, i * D:(i + 1) * D]

            a = dve.last()
            work = core.tile(part, "mod_work", [B, 4, D])
            for l in range(2):
                for i in (2, 5):
                    g, s, m = field(l, i), work[:, 0, :], work[:, 1, :]
                    b = dve.do(lambda e, g=g, m=m: e.tensor_scalar(m, g, -1.0, None, ALU.mult), a)
                    b = dve.do(lambda e, g=g, m=m: e.tensor_tensor(m, m, g, ALU.max), b)
                    b = dve.do(lambda e, m=m: e.tensor_scalar(m, m, 0.25, None, ALU.max), b)
                    b = dve.do(lambda e, g=g, s=s: e.tensor_scalar(s, g, 0.0, 2.0, ALU.is_ge, ALU.mult), b)
                    b = dve.do(lambda e, s=s: e.tensor_scalar(s, s, -1.0, None, ALU.add), b)
                    a = dve.do(lambda e, g=g, s=s, m=m: e.tensor_tensor(g, s, m, ALU.mult), b)
                for i in (1, 4):
                    a = dve.do(lambda e, l=l, i=i: e.tensor_scalar(field(l, i), field(l, i), 1.0, None, ALU.add), a)
            vec = core.tile(part, "vectors_by_batch", [B, 5, D])
            for i, name in enumerate(["L0_attn_ln2_scale", "L0_attn_ln2_bias", "L1_attn_gamma", "L1_attn_beta", "L1_ffn_b2"]):
                got = core.lane("vectors").send(sp, lambda e, i=i, name=name: e.dma_start(
                    vec[:, i, :], A[name].rearrange("(a d) -> a d", a=1).to_broadcast([B, D])))
            rows0 = core.tile(part, "rows0", [B, 4, D])
            rows1 = core.tile(part, "rows1", [B, 5, D])
            dve.wait(a, got)
            dve.quiet(lambda e: e.tensor_tensor(rows0[:, 0, :], field(0, 2), vec[:, 0, :], ALU.mult))
            dve.quiet(lambda e: e.tensor_tensor(rows0[:, 1, :], field(0, 2), vec[:, 1, :], ALU.mult))
            dve.quiet(lambda e: e.tensor_copy(rows0[:, 2, :], field(0, 4)))
            a = dve.do(lambda e: e.tensor_copy(rows0[:, 3, :], field(0, 3)))
            rows_sent.append(core.lane("rows").send(sp, lambda e: e.dma_start(row0_dram, rows0[:, :, :].rearrange("b a d -> b (a d)")), a))
            dve.quiet(lambda e: e.tensor_copy(rows1[:, 0, :], field(0, 5)))
            dve.quiet(lambda e: e.tensor_tensor(rows1[:, 1, :], field(1, 2), vec[:, 2, :], ALU.mult))
            dve.quiet(lambda e: e.tensor_tensor(rows1[:, 2, :], field(1, 2), vec[:, 3, :], ALU.mult))
            dve.quiet(lambda e: e.tensor_copy(rows1[:, 3, :], field(1, 5)))
            a = dve.do(lambda e: e.tensor_tensor(rows1[:, 4, :], field(1, 5), vec[:, 4, :], ALU.mult))
            rows_sent.append(core.lane("rows").send(sp, lambda e: e.dma_start(row1_dram, rows1[:, :, :].rearrange("b a d -> b (a d)")), a))
            blocks = [(0, 0), (0, 1), (1, 0), (1, 1), (1, 3), (1, 4)]
            for n, (l, i) in enumerate(blocks):
                for k in range(KD):
                    step = (lambda e, n=n, l=l, i=i, k=k: e.transpose(
                        banks[6][:, (2 * n + k) * B:(2 * n + k + 1) * B], field(l, i)[:, k * P:(k + 1) * P], ident[0:B, 0:B]))
                    m = pe.do(step, a, ident_ready)
            a = dve.do(lambda e: e.tensor_copy(cols[:, :, :].rearrange("p n b -> p (n b)"), banks[6][:, 0:12 * B]), m)
            banks.used(6, a)
            core.everyone_waits_for_everyone()

        g = dict(B=B, S=S, D=D, T=T, F=F, E=E, CAP=CAP, KD=KD, KF=KF, HEADS=HEADS, KW=KW, TILE_T=TILE_T, NT=NT, BAND_SIZE=BAND_SIZE,
                 ident=ident, cols=cols, zero=zero, zero_ready=zero_ready,
                 SHIFT0=SHIFT0, SCALE0=SCALE0, SHIFT1A=SHIFT1A, SCALE1A=SCALE1A, SHIFT1B=SHIFT1B, SCALE1B=SCALE1B,
                 x1_dram=x1_dram, xn_dram=xn_dram, logit_dram=logit_dram, moe_dram=moe_dram, gate_dram=gate_dram,
                 row0_dram=row0_dram, row1_dram=row1_dram, band_dram=band_dram, out=out)
        retention(core, A, g, split_w1, split_w2)
        mlp_weights.close()
        if debug != "A":
            experts(core, A, g)
            if debug != "M":
                layer_one(core, A, g)
        core.everyone_waits_for_everyone()

        block = ctx.enter_context(nc.Block())
        block.tensor(lambda e: pe.replay(e))
        block.scalar(lambda e: act.replay(e))
        block.vector(lambda e: dve.replay(e))
        block.gpsimd(lambda e: pool.replay(e))
        block.sync(lambda e: sp.replay(e))


def retention(core, A, g, w1, w2):
    pe, act, dve, pool, sp = core.engines
    banks, ident, cols = core.banks, g["ident"], g["cols"]
    B, S, D, T, F, E, KD, KF = (g[n] for n in ("B", "S", "D", "T", "F", "E", "KD", "KF"))
    GT = BANK
    C = GT // P
    N = T // GT
    PER = S // GT
    x_dram = A["L0_attn_x"].rearrange("b (h c p) d -> (b h) p c d", c=C, p=P)
    x1_dram = g["x1_dram"].rearrange("(n c p) d -> n p c d", c=C, p=P)
    xn_dram = g["xn_dram"].rearrange("(n c p) d -> n p c d", c=C, p=P)

    with ExitStack() as part:
        def tile(name, shape, dt=F32):
            return core.tile(part, name, shape, dt)

        def ring(name, n, shape):
            return core.ring(part, name, n, shape)

        w_ret = tile("w_ret", [P, KD, D])
        w_router = tile("w_router", [P, KD, E])
        ret_bias, ln1_scale, ln1_bias, b1 = (tile(n, [P, k]) for n, k in (("ret_bias", KD), ("ln1_scale", KD), ("ln1_bias", KD), ("b1", KF)))
        router_bias = tile("router_bias", [E, 1])
        b2_row, nw_row = tile("b2_row", [P, D]), tile("nw_row", [P, D])
        half, zeros = tile("half", [P, 1]), tile("zeros", [P, g["BAND_SIZE"] // P])
        x, rows = ring("x", 6, [P, C, D]), ring("rows", 2, [P, 4, D])
        xh, h1T, th, q, r = ring("xh", 1, [P, C, D]), ring("h1T", 1, [P, KD, GT]), ring("th", 1, [P, KD, GT]), ring("q", 2, [P, KD, GT]), ring("r", 1, [P, KD, GT])
        xh2, h_full, g_full = ring("xh2", 1, [P, C, D]), ring("h_full", 2, [P, GT]), ring("g_full", 4, [P, GT])
        hT, act_T = core.split_ring(part, "hT", 2, [P, KD, GT]), core.split_ring(part, "gT", 1, [P, KF, GT])
        ident_r = tile("ident_r", [P, P], F32R)
        v, x1, h2, xn, xnT = (ring(n, k, [P, C, D]) for n, k in (("v", 2), ("x1_", 2), ("h2_", 2), ("xn", 2), ("xnT", 1)))
        square = tile("square", [P, D])
        lg = ring("lg", 2, [E, GT])
        stats, moments = tile("stats", [P, C, 6]), tile("moments", [P, C, 2])
        scratch = tile("scratch", [P, 4, C])
        sumsq = ring("sumsq", 2, [P, C])

        lane = core.lane("weights")
        for dst, src in ((w_ret[:, :, :], A["L0_attn_W_ret"].rearrange("(k p) n -> p k n", p=P)),
                         (w_router[:, :, :], A["L0_ffn_router_wT"].rearrange("(k p) n -> p k n", p=P)),
                         (ret_bias[:, :], A["L0_attn_b_ret_c"]), (ln1_scale[:, :], A["L0_attn_ln1_scale_c"]),
                         (ln1_bias[:, :], A["L0_attn_ln1_bias_c"]), (b1[:, :], A["L0_attn_b1_c"]),
                         (router_bias[:, :], A["L0_ffn_router_bias"].rearrange("(e a) -> e a", a=1)),
                         (b2_row[:, :], A["L0_attn_b2"].rearrange("(a d) -> a d", a=1).to_broadcast([P, D])),
                         (nw_row[:, :], A["L0_ffn_norm_weight"].rearrange("(a d) -> a d", a=1).to_broadcast([P, D]))):
            weights = lane.send(sp, lambda e, dst=dst, src=src: e.dma_start(dst, src))
        zeros_ready = pool.do(lambda e: e.memset(zeros[:, :], 0.0))
        ident_r_ready = dve.do(lambda e: e.tensor_copy(ident_r[:, :], ident[:, :]))
        half_ready = dve.do(lambda e: e.memset(half[:, :], 0.5))
        bias_ready = dve.do(lambda e: e.tensor_scalar(ret_bias[:, :], ret_bias[:, :], 0.5, None, ALU.mult), weights)

        got_x, got_rows, done = {}, {}, {}

        def load(i):
            got_x[i] = core.lane(f"x{i % 6}").send(sp, lambda e: e.dma_start(x[i][:, :, :], x_dram[i]), x.idle(i))
            zl = core.lane("zeros")
            zl.send(sp, lambda e: e.dma_start(g["moe_dram"].rearrange("(n p c) d -> n p (c d)", p=P, c=C)[i],
                                              zeros[:, 0:C * D]), zeros_ready)
            if i < 2 * g["NT"]:
                size = g["BAND_SIZE"] // P
                zl.send(sp, lambda e: e.dma_start(g["band_dram"][i % 2][i // 2].rearrange("(p c) -> p c", p=P), zeros[:, 0:size]))

        def load_rows(i):
            if i % PER == 0:
                b = i // PER
                got_rows[b] = core.lane(f"rows{b % 2}").send(sp, lambda e: e.dma_start(
                    rows[b][:, :, :].rearrange("p a d -> p (a d)"), g["row0_dram"][b:b + 1, :].to_broadcast([P, 4 * D])), rows.idle(b))

        def norm_in(i):
            y, a = statistics(core, stats, moments, lambda c: x[i][:, c, :], C, 1e-5, scratch, got_x[i])
            dve.wait(a, xh.idle(i))
            for c in range(C):
                a = dve.do(lambda e, c=c: e.tensor_scalar(xh[i][:, c, :], x[i][:, c, :], moments[:, c, 0:1], y[:, c:c + 1],
                                                          ALU.subtract, ALU.mult))
            done["xh", i] = a

        uses = [0]

        def next_bank():
            uses[0] += 1
            return uses[0] % 4

        def next_pair():
            return next_bank(), next_bank()

        def to_features(i, source, ready, write):
            for k, u in enumerate(next_pair()):
                t = transpose_into(core, banks[u], C, lambda c, k=k: source[:, c, k * P:(k + 1) * P], ident, [ready, banks.idle(u)])
                banks.used(u, write(k, banks[u], t))
            return t

        def modulate(i):
            b = i // PER

            def write(k, bank, t):
                a = act.do(lambda e: e.activation(h1T[i][:, k, :], bank[:, :], ACT.Identity,
                                                  scale=cols[:, g["SCALE0"] + k, b:b + 1], bias=cols[:, g["SHIFT0"] + k, b:b + 1]), t, h1T.idle(i))
                done["h1T", i] = a
                return a
            t = to_features(i, xh[i], done["xh", i], write)
            xh.used(i, t)

        def retain(i, k):
            u = next_bank()
            for j in range(KD):
                m = pe.do(lambda e, j=j: e.matmul(banks[u][:, :], w_ret[:, j, k * P:(k + 1) * P], h1T[i][:, j, :],
                                                  start=j == 0, stop=j == KD - 1), done["h1T", i], weights, banks.idle(u))
            a = act.do(lambda e: e.activation(th[i][:, k, :], banks[u][:, :], ACT.Tanh, bias=ret_bias[:, k:k + 1], scale=0.5),
                       m, bias_ready, th.idle(i))
            banks.used(u, a)
            done["tanh", i, k] = pool.do(lambda e: e.tensor_scalar(th[i][:, k, :], th[i][:, k, :], 1.0, 1.0, ALU.mult, ALU.add), a)
            if k == KD - 1:
                done["retained", i] = m

        def run(i, k):
            start = 0.0 if i % PER == 0 else q[i - 1][:, k, GT - 1:GT]
            a = dve.do(lambda e: e.tensor_tensor_scan(
                q[i][:, k, :], half[:, 0:1].to_broadcast([P, GT]), th[i][:, k, :], start, ALU.mult, ALU.add),
                done["tanh", i, k], half_ready, done.get(("q", i - 1)))
            if k == KD - 1:
                th.used(i, a)
                done["q", i] = a
            a = dve.do(lambda e: e.scalar_tensor_tensor(out=r[i][:, k, :], in0=q[i][:, k, :], scalar=0.25, in1=h1T[i][:, k, :],
                                                        op0=ALU.mult, op1=ALU.add), a, r.idle(i))
            if k == KD - 1:
                done["r", i] = a
                h1T.used(i, a, done["retained", i])

        def norm_mid(i):
            pairs = next_pair()
            for c in range(C):
                u = pairs[c // 2]
                for k in range(KD):
                    col = (c % 2) * D + k * P
                    m = pe.do(lambda e, c=c, k=k, u=u, col=col: e.transpose(banks[u][:, col:col + P], r[i][:, k, c * P:(c + 1) * P], ident[:, :]),
                              done["r", i], banks.idle(u))
            r.used(i, m)
            chunk = lambda c: banks[pairs[c // 2]][:, (c % 2) * D:(c % 2 + 1) * D]
            y, a = statistics(core, stats, moments, chunk, C, 1e-5, scratch, m)
            dve.wait(a, xh2.idle(i))
            for c in range(C):
                a = dve.do(lambda e, c=c: e.tensor_scalar(xh2[i][:, c, :], chunk(c), moments[:, c, 0:1], y[:, c:c + 1], ALU.subtract, ALU.mult))
            for u in pairs:
                banks.used(u, a)
            done["xh2", i] = a

        def affine_mid(i):
            def write(k, bank, t):
                n = KD * i + k
                a = act.do(lambda e: e.activation(h_full[n][:, :], bank[:, :], ACT.Identity,
                                                  scale=ln1_scale[:, k:k + 1], bias=ln1_bias[:, k:k + 1]), t, h_full.idle(n))
                b = split(core, h_full[n][:, :], hT[i][:, k, :], pool, a, hT.idle(i))
                h_full.used(n, b)
                done["hT", i] = b
                return a
            xh2.used(i, to_features(i, xh2[i], done["xh2", i], write))

        def take_apart(i, f):
            n = KF * i + f
            done["gT", i] = split(core, g_full[n][:, :], act_T[i][:, f, :], pool, done["g", n], act_T.idle(i))
            g_full.used(n, done["gT", i])

        def expand(i, fs):
            for f in fs:
                u, n = 4 + f % 2, KF * i + f
                for k in range(KD):
                    for j, (w, h) in enumerate(w1[:, k, f * P:(f + 1) * P].pairs(hT[i][:, k, :])):
                        m = pe.do(lambda e, w=w, h=h, u=u, first=k + j == 0, final=k == KD - 1 and j == 2: e.matmul(
                            banks[u][:, :], w, h, start=first, stop=final), done["hT", i], banks.idle(u))
                a = act.do(lambda e, f=f, u=u, n=n: e.activation(g_full[n][:, :], banks[u][:, :], ACT.Gelu_apprx_tanh, bias=b1[:, f:f + 1]),
                           m, g_full.idle(n))
                banks.used(u, a)
                done["g", n] = a
                if f > 0:
                    take_apart(i, f - 1)
            if f == KF - 1:
                take_apart(i, f)

        def contract(i, c):
            u = 6 + c % 2
            chunk = slice(c * P, (c + 1) * P)
            pe.wait(done["gT", i], banks.idle(u), ident_r_ready)
            for f in range(KF):
                for j, (x_, w) in enumerate(act_T[i][:, f, chunk].pairs(w2[:, f, :])):
                    pe.quiet(lambda e, x_=x_, w=w, first=f + j == 0: e.matmul(banks[u][:, 0:D], x_, w, start=first, stop=False))
            for k in range(KD):
                for j, x_ in enumerate((hT[i].low, hT[i].high)):
                    m = pe.do(lambda e, k=k, x_=x_, final=k == KD - 1 and j == 1: e.matmul(
                        banks[u][:, k * P:(k + 1) * P], x_[:, k, chunk], ident_r[:, :], start=False, stop=final))
            if c == C - 1:
                act_T.used(i, m)
                hT.used(i, m)
            a = act.do(lambda e: e.copy(v[i][:, c, :], banks[u][:, 0:D]), m, v.idle(i))
            banks.used(u, a)
            done["v", i] = a

        def bcast(b, row):
            return rows[b][:, row:row + 1, :].to_broadcast([P, C, D])

        def norm_out(i):
            a = dve.do(lambda e: e.tensor_tensor(v[i][:, :, :], v[i][:, :, :], b2_row[:, :].unsqueeze(1).to_broadcast([P, C, D]), ALU.add), done["v", i])
            y, a = statistics(core, stats, moments, lambda c: v[i][:, c, :], C, 1e-5, scratch, a)
            dve.wait(a)
            for c in range(C):
                a = dve.do(lambda e, c=c: e.tensor_scalar(v[i][:, c, :], v[i][:, c, :], moments[:, c, 0:1], y[:, c:c + 1],
                                                          ALU.subtract, ALU.mult))
            done["vhat", i] = a

        def gain_out(i):
            b = i // PER
            a = pool.do(lambda e: e.tensor_tensor(v[i][:, :, :], v[i][:, :, :], bcast(b, 0), ALU.mult), done["vhat", i], got_rows[b])
            a = pool.do(lambda e: e.tensor_tensor(x1[i][:, :, :], x[i][:, :, :], bcast(b, 1), ALU.add), got_x[i], got_rows[b], x1.idle(i))
            x.used(i, a)
            done["t1", i] = a

        def residual(i):
            a = dve.do(lambda e: e.tensor_tensor(x1[i][:, :, :], x1[i][:, :, :], v[i][:, :, :], ALU.add), done["t1", i])
            v.used(i, a)
            sent = core.lane(f"x1_{i % 2}").send(sp, lambda e: e.dma_start(x1_dram[i], x1[i][:, :, :]), a)
            y, a = statistics(core, stats, moments, lambda c: x1[i][:, c, :], C, 1e-5, scratch, a)
            dve.wait(a, h2.idle(i))
            for c in range(C):
                a = dve.do(lambda e, c=c: e.tensor_scalar(h2[i][:, c, :], x1[i][:, c, :], moments[:, c, 0:1], y[:, c:c + 1],
                                                          ALU.subtract, ALU.mult))
            x1.used(i, sent, a)
            done["x1hat", i] = a

        def modulate_out(i):
            b = i // PER
            a = pool.do(lambda e: e.tensor_tensor(h2[i][:, :, :], h2[i][:, :, :], bcast(b, 2), ALU.mult), done["x1hat", i])
            a = pool.do(lambda e: e.tensor_tensor(h2[i][:, :, :], h2[i][:, :, :], bcast(b, 3), ALU.add), a)
            rows.used(b, a)
            done["h2", i] = a

        def squares(i):
            a = act.last()
            for c in range(C):
                a = act.do(lambda e, c=c: e.activation(square[:, :], h2[i][:, c, :], ACT.Square, scale=D ** -0.5,
                                                       accum_out=sumsq[i][:, c:c + 1]), a, done["h2", i], sumsq.idle(i))
            done["sumsq", i] = a

        def rms_norm(i):
            y, a = inverse_root(core, scratch, sumsq[i][:, :], 1e-5, done["sumsq", i])
            dve.wait(xn.idle(i))
            dve.wait(a)
            for c in range(C):
                a = dve.do(lambda e, c=c: e.scalar_tensor_tensor(out=xn[i][:, c, :], in0=h2[i][:, c, :], scalar=y[:, c:c + 1],
                                                                 in1=nw_row[:, :], op0=ALU.mult, op1=ALU.mult))
            sumsq.used(i, a)
            h2.used(i, a)
            done["xn", i] = a

        def turn_out(i):
            def write(k, bank, t):
                done["xnT", i] = act.do(lambda e: e.copy(xnT[i][:, k * 2:k * 2 + 2, :].rearrange("p a d -> p (a d)"), bank[:, :]), t, xnT.idle(i))
                return done["xnT", i]
            t = to_features(i, xn[i], done["xn", i], write)
            sent = core.lane(f"xn{i % 2}").send(sp, lambda e: e.dma_start(xn_dram[i], xn[i][:, :, :]), done["xn", i])
            xn.used(i, t, sent)

        def route(i):
            u = next_bank()
            for k in range(KD):
                m = pe.do(lambda e, k=k: e.matmul(banks[u][0:E, :], w_router[:, k, :], xnT[i][:, k * 2:k * 2 + 2, :].rearrange("p a d -> p (a d)"),
                                                  start=k == 0, stop=k == KD - 1), done["xnT", i], banks.idle(u))
            xnT.used(i, m)
            a = act.do(lambda e: e.activation(lg[i][:, :], banks[u][0:E, :], ACT.Identity, bias=router_bias[:, 0:1]), m, lg.idle(i))
            banks.used(u, a)
            sent = core.lane(f"lg{i % 2}").send(sp, lambda e: e.dma_start(g["logit_dram"][:, i * GT:(i + 1) * GT], lg[i][:, :]), a)
            lg.used(i, sent)

        pipeline(N, [
            (load, 0), (modulate_out, 6), (turn_out, 7), (modulate, 1), (norm_mid, 2), (part_of(contract, 0), 4), (gain_out, 5), (route, 7),
            (part_of(contract, 1), 4), (squares, 6), (part_of(contract, 2), 4), (residual, 5), (part_of(contract, 3), 4),
            (affine_mid, 2), (rms_norm, 6),
            (part_of(expand, (0, 1)), 3), (norm_in, 0), (part_of(retain, 0), 1), (part_of(expand, (2, 3)), 3), (part_of(retain, 1), 1),
            (part_of(run, 0), 1), (part_of(expand, (4,)), 3), (part_of(run, 1), 1), (norm_out, 4), (part_of(expand, (5, 6)), 3),
            (part_of(expand, (7,)), 3), (load_rows, 3),
        ])
        core.everyone_waits_for_everyone()


def find_threshold(core, part, L, block_ones, ready):
    pe, act, dve, pool, sp = core.engines
    thr, trial, keep = (core.tile(part, n, [P, 1], U32) for n in ("thr", "trial", "keep"))
    count = core.tile(part, "count", [P, 1])
    hits = core.tile(part, "hits", [P, L.shape[1]], BF16)
    bank = core.banks[0]

    def enough(a, wanted):
        a = dve.do(lambda e: e.tensor_scalar(hits[:, :], L[:, :], trial[:, :].bitcast(F32), None, ALU.is_ge, ALU.add,
                                             accum_out=count[:, :]), a, ready)
        m = pe.do(lambda e: e.matmul(bank[:, 0:1], block_ones[:, :], count[:, :], start=True, stop=True), a, core.banks.idle(0))
        return dve.do(lambda e: e.tensor_scalar(keep[:, :], bank[:, 0:1], float(wanted) - 0.5, None, ALU.is_ge), m)

    wanted = 1024
    a = dve.do(lambda e: e.memset(trial[:, :].bitcast(F32), 0.0))
    a = enough(a, wanted)
    a = dve.do(lambda e: e.tensor_scalar(trial[:, :], keep[:, :], 1, None, ALU.bitwise_xor), a)
    a = dve.do(lambda e: e.tensor_scalar(thr[:, :].bitcast(I32), trial[:, :].bitcast(I32), 31, 31, ALU.logical_shift_left,
                                         ALU.arith_shift_right), a)
    for bit in range(30, -1, -1):
        a = dve.do(lambda e, bit=bit: e.tensor_scalar(trial[:, :], thr[:, :], 1 << bit, None, ALU.bitwise_xor), a)
        a = enough(a, wanted)
        a = dve.do(lambda e, bit=bit: e.scalar_tensor_tensor(out=thr[:, :], in0=keep[:, :], scalar=bit, in1=thr[:, :],
                                                             op0=ALU.logical_shift_left, op1=ALU.bitwise_xor), a)
    core.banks.used(0, a)
    return thr[:, :].bitcast(F32), a


def experts(core, A, g):
    pe, act, dve, pool, sp = core.engines
    banks, ident = core.banks, g["ident"]
    D, T, F, E, KD, KF, CAP = (g[n] for n in ("D", "T", "F", "E", "KD", "KF", "CAP"))
    G = P // E
    W = T // G
    CH = W // P
    NONE = 4096
    PER_BANK = BANK // P
    HT = CAP // 2
    C = HT // P
    NI = 2 * E

    with ExitStack() as part:
        def tile(name, shape, dt=F32):
            return core.tile(part, name, shape, dt)

        def ring(name, n, shape, dt=F32):
            return core.ring(part, name, n, shape, dt)

        block_ones, block_below = tile("block_ones", [P, P]), tile("block_below", [P, P])
        iota_p, iota_q, token_low = tile("iota_p", [P, P], BF16), tile("iota_q", [P, G], BF16), tile("token_low", [P, 1])
        token_high = tile("token_high", [P, CH, G], BF16)
        b1 = tile("fc1_bias", [P, E, KF])
        L = tile("logits", [P, W])
        f1, f2, f3 = tile("work1", [P, W]), tile("work2", [P, W]), tile("work3", [P, W])
        slot_i = tile("slot_i", [P, CH, E, G], I32)
        slot_p, slot_q = tile("slot_p", [P, CH, E, G], BF16), tile("slot_q", [P, CH, E, G], BF16)
        small = tile("small", [P, 8])
        xg, gg = ring("xg", 2, [P, C, D]), ring("gg", 4, [P, C, E])
        xg_full, hidden_full = ring("xg_full", 2, [P, HT]), ring("hidden_full", 4, [P, HT])
        xgT, hidden = core.split_ring(part, "xgT", 1, [P, KD, HT]), core.split_ring(part, "hidden", 1, [P, KF, HT])
        w1_full, w2_full, b2_row = ring("fc1_full", 1, [P, KD, F]), ring("fc2_full", 1, [P, KF, D]), ring("fc2_bias", 2, [P, D])
        w1, w2 = core.split_ring(part, "fc1", 1, [P, KD, F]), core.split_ring(part, "fc2", 1, [P, KF, D])
        ys = ring("ys", 2, [P, C, D])
        PC = 2
        onehot_p, onehot_q = ring("onehot_p", 4, [P, PC, G, P], BF16), ring("onehot_q", 4, [P, PC, G, 2 * G], BF16)
        eq_q = ring("eq_q", 2, [P, PC, G, G], BF16)
        parts = ring("id_parts", 2, [P, 2 * G])
        idx = ring("idx", 4, [P, G], U32)

        lane = core.lane("routing_in")
        for dst, src in ((L[:, :], g["logit_dram"].rearrange("e (g t) -> (e g) t", g=G)),
                         (block_ones[:, :], A["block_ones"]), (block_below[:, :], A["block_below"]), (f1[:, 0:P], A["iota_row"]),
                         (small[:, 0:1], A["iota_column"]), (f2[:, 0:P], A["chunk_ids"]),
                         (b1[:, :, :], A["L0_ffn_fc1_bias_c"].rearrange("p (e k) -> p e k", e=E))):
            ready = lane.send(sp, lambda e, dst=dst, src=src: e.dma_start(dst, src))
        done = {}

        def load_weights(e_):
            done["w1_full", e_] = core.lane("fc1").send(sp, lambda e: e.dma_start(
                w1_full[e_][:, :, :], A["L0_ffn_fc1_wT"][e_].rearrange("(k p) n -> p k n", p=P)), w1_full.idle(e_))
            done["w2_full", e_] = core.lane("fc2").send(sp, lambda e: e.dma_start(
                w2_full[e_][:, :, :], A["L0_ffn_fc2_wT"][e_].rearrange("(k p) n -> p k n", p=P)), w2_full.idle(e_))
            done["b2", e_] = core.lane(f"fc2_bias{e_ % 2}").send(sp, lambda e: e.dma_start(
                b2_row[e_][:, :], A["L0_ffn_fc2_bias"][e_:e_ + 1, :].to_broadcast([P, D])), b2_row.idle(e_))
        load_weights(0)

        def split_w1(e_, k):
            done["w1", e_] = split(core, w1_full[e_][:, k, :], w1[e_][:, k, :], pool, done["w1_full", e_], w1.idle(e_))
            if k == KD - 1:
                w1_full.used(e_, done["w1", e_])

        def split_w2(e_, piece):
            fs = slice(piece * KF // 2, (piece + 1) * KF // 2)
            done["w2", e_] = split(core, w2_full[e_][:, fs, :], w2[e_][:, fs, :], pool, done["w2_full", e_], w2.idle(e_))
            if piece == 1:
                w2_full.used(e_, done["w2", e_])

        dve.quiet(lambda e: e.tensor_copy(iota_p[:, :], f1[:, 0:P]), ready)
        dve.quiet(lambda e: e.tensor_copy(iota_q[:, :], f1[:, 0:G]))
        dve.quiet(lambda e: e.tensor_copy(token_low[:, :], small[:, 0:1]))
        dve.do(lambda e: e.tensor_copy(token_high[:, :, :].rearrange("p c g -> p (c g)"), f2[:, 0:P]))
        limit, a = find_threshold(core, part, L, block_ones, ready)

        above, ties, tied_before, tie_room, counts, base = (small[:, i:i + 1] for i in range(1, 7))
        greater, equal, running = f1, f2, f3
        dve.wait(a)
        a = dve.do(lambda e: e.tensor_scalar(greater[:, :], L[:, :], limit, None, ALU.is_gt, ALU.add, accum_out=above), a)
        a = dve.do(lambda e: e.tensor_scalar(equal[:, :], L[:, :], limit, None, ALU.is_equal, ALU.add, accum_out=ties))
        m = pe.do(lambda e: e.matmul(banks[0][:, 0:1], block_ones[:, :], above, start=True, stop=True), a, banks.idle(0))
        m = pe.do(lambda e: e.matmul(banks[1][:, 0:1], block_below[:, :], ties, start=True, stop=True), banks.idle(1))
        b = dve.do(lambda e: e.tensor_copy(tied_before, banks[1][:, 0:1]), m)
        b = dve.do(lambda e: e.scalar_tensor_tensor(out=tie_room, in0=banks[0][:, 0:1], scalar=-float(CAP), in1=tied_before,
                                                    op0=ALU.add, op1=ALU.add), b)
        tie_a = dve.do(lambda e: e.tensor_scalar(tie_room, tie_room, -1.0, None, ALU.mult), b)
        a = dve.do(lambda e: e.tensor_tensor_scan(running[:, :], equal[:, :], equal[:, :], 0.0, ALU.add, ALU.max), tie_a)
        a = dve.do(lambda e: e.scalar_tensor_tensor(out=equal[:, :], in0=running[:, :], scalar=tie_room, in1=equal[:, :],
                                                    op0=ALU.is_le, op1=ALU.mult), a)
        taken = greater
        a = dve.do(lambda e: e.tensor_tensor(taken[:, :], greater[:, :], equal[:, :], ALU.add), a)
        a = dve.do(lambda e: e.tensor_tensor_scan(running[:, :], taken[:, :], taken[:, :], 0.0, ALU.add, ALU.max), a)
        m = pe.do(lambda e: e.matmul(banks[0][:, 0:1], block_below[:, :], running[:, W - 1:W], start=True, stop=True), a)
        a = dve.do(lambda e: e.tensor_scalar(base, banks[0][:, 0:1], -1.0 - NONE, None, ALU.add), m)
        banks.used(0, a)
        banks.used(1, a)
        a = dve.do(lambda e: e.scalar_tensor_tensor(out=running[:, :], in0=running[:, :], scalar=base, in1=taken[:, :],
                                                    op0=ALU.add, op1=ALU.mult), a)
        for n in range(CH // PER_BANK):
            t = transpose_into(core, banks[n], PER_BANK, lambda c, n=n: running[:, (n * PER_BANK + c) * P:(n * PER_BANK + c + 1) * P],
                               ident, [a, banks.idle(n)])
            b = dve.do(lambda e, n=n: e.tensor_scalar(slot_i[:, n * PER_BANK:(n + 1) * PER_BANK, :, :].rearrange("p c e g -> p (c e g)"),
                                                      banks[n][:, :], float(NONE), None, ALU.add), t)
            banks.used(n, b)
        flat = lambda x: x[:, :, :, :].rearrange("p c e g -> p (c e g)")
        fi = f1[:, :].bitcast(I32)
        b = dve.do(lambda e: e.tensor_scalar(fi, flat(slot_i), P - 1, None, ALU.bitwise_and), b)
        b = dve.do(lambda e: e.tensor_copy(flat(slot_p), fi), b)
        b = dve.do(lambda e: e.tensor_scalar(fi, flat(slot_i), P.bit_length() - 1, None, ALU.logical_shift_right), b)
        slots_ready = dve.do(lambda e: e.tensor_copy(flat(slot_q), fi), b)

        def make_gates():
            probs, kept = f2, f1
            view = lambda x: x[:, :].rearrange("p (c e g) -> p c e g", e=E, g=G)
            over_e = lambda x: x[:, :].rearrange("p (c e g) -> p c g e", e=E, g=G)
            row = gate_row
            bc = lambda x: x[:, :, :].unsqueeze(2).to_broadcast([P, CH, E, G])
            for n in range(CH // PER_BANK):
                u = n % 2
                t = transpose_into(core, banks[u], PER_BANK, lambda c, n=n: L[:, (n * PER_BANK + c) * P:(n * PER_BANK + c + 1) * P],
                                   ident, [banks.idle(u)])
                b = dve.do(lambda e, n=n, u=u: e.tensor_copy(probs[:, n * BANK:(n + 1) * BANK], banks[u][:, :]), t)
                banks.used(u, b)
            b = dve.do(lambda e: e.tensor_reduce(row[:, :, :], over_e(probs), AX_X, ALU.max), b)
            b = dve.do(lambda e: e.tensor_tensor(view(probs), view(probs), bc(row), ALU.subtract), b)
            b = act.do(lambda e: e.activation(probs[:, :], probs[:, :], ACT.Exp), b)
            b = dve.do(lambda e: e.tensor_reduce(row[:, :, :], over_e(probs), AX_X, ALU.add), b)
            b = dve.do(lambda e: e.reciprocal(row[:, :, :], row[:, :, :]), b)
            b = dve.do(lambda e: e.tensor_tensor(view(probs), view(probs), bc(row), ALU.mult), b)
            b = dve.do(lambda e: e.tensor_scalar(kept[:, :], flat(slot_i), float(NONE), None, ALU.is_lt), b)
            b = dve.do(lambda e: e.tensor_tensor(probs[:, :], probs[:, :], kept[:, :], ALU.mult), b)
            b = dve.do(lambda e: e.tensor_reduce(row[:, :, :], over_e(probs), AX_X, ALU.add), b)
            b = dve.do(lambda e: e.scalar_tensor_tensor(out=row[:, :, :], in0=row[:, :, :], scalar=0.0, in1=row[:, :, :],
                                                        op0=ALU.is_le, op1=ALU.add), b)
            b = dve.do(lambda e: e.reciprocal(row[:, :, :], row[:, :, :]), b)
            order = kept[:, :].rearrange("p (g c e) -> p c e g", g=G, c=CH)
            b = dve.do(lambda e: e.tensor_tensor(order, view(probs), bc(row), ALU.mult), b)
            done["gates"] = core.lane("gates").send(sp, lambda e: e.dma_start(
                g["gate_dram"].rearrange("(n p) e -> p n e", p=P), kept[:, :].rearrange("p (n e) -> p n e", e=E)), b)

        gate_row = tile("gate_row", [P, CH, G])

        PIECES = CH // 2 // PC

        def mark(i, piece):
            x, n = i // 2, i * PIECES + piece
            c0 = (i % 2) * CH // 2 + piece * PC
            cs = slice(c0, c0 + PC)
            shape = [P, PC, G]
            of = lambda t, n: t[:, cs, x, :].unsqueeze(3).to_broadcast(shape + [n])
            b = dve.do(lambda e: e.tensor_tensor(eq_q[n][:, :, :, :], iota_q[:, :].unsqueeze(1).unsqueeze(1).to_broadcast(shape + [G]),
                                                 of(slot_q, G), ALU.is_equal), slots_ready, eq_q.idle(n))
            dve.do(lambda e: e.tensor_tensor(onehot_p[n][:, :, :, :], iota_p[:, :].unsqueeze(1).unsqueeze(1).to_broadcast(shape + [P]),
                                             of(slot_p, P), ALU.is_equal), onehot_p.idle(n))
            a = dve.do(lambda e: e.tensor_tensor(onehot_q[n][:, :, :, 0:G], eq_q[n][:, :, :, :],
                                                 token_high[:, cs, :].unsqueeze(3).to_broadcast(shape + [G]), ALU.mult), b, onehot_q.idle(n))
            a = dve.do(lambda e: e.tensor_scalar(onehot_q[n][:, :, :, G:2 * G], eq_q[n][:, :, :, :], token_low[:, 0:1], None, ALU.mult))
            eq_q.used(n, a)
            done["marked", n] = a

        def listing(i, piece):
            x, h, n = i // 2, i % 2, i * PIECES + piece
            u = 2 + x % 2
            opening, closing = h == 0 and piece == 0, h == 1 and piece == PIECES - 1
            for c in range(PC):
                for gr in range(G):
                    end = c == PC - 1 and gr == G - 1
                    step = (lambda e, c=c, gr=gr, first=opening and c == 0 and gr == 0, final=closing and end: e.matmul(
                        banks[u][:, 0:2 * G], onehot_p[n][:, c, gr, :], onehot_q[n][:, c, gr, :], start=first, stop=final))
                    if end:
                        m = pe.do(step)
                    else:
                        pe.quiet(step, done["marked", n], banks.idle(u) if opening else None)
            onehot_p.used(n, m)
            onehot_q.used(n, m)
            if closing:
                b = act.do(lambda e: e.copy(parts[x][:, :], banks[u][:, 0:2 * G]), m)
                banks.used(u, b)
                done["idx", x] = dve.do(lambda e: e.scalar_tensor_tensor(out=idx[x][:, :], in0=parts[x][:, 0:G], scalar=float(P),
                                                                         in1=parts[x][:, G:2 * G], op0=ALU.mult, op1=ALU.add), b, idx.idle(x))

        def fetch(i):
            x, h = i // 2, i % 2
            if i == 0:
                make_gates()
            pool.wait(done["idx", x], xg.idle(i))
            for c in range(C):
                col = idx[x][:, h * C + c:h * C + c + 1]
                done["xg", i] = core.lane(f"xg{i % 2}").send(pool, lambda e, c=c, col=col: e.indirect_dma_start(
                    xg[i][:, c, :], None, g["xn_dram"], bass.IndirectOffsetOnAxis(ap=col, axis=0)))

        def next_weights(i):
            if i % 2 == 0:
                if i > 0:
                    load_weights(i // 2)

        def take_w1(i, k):
            if i % 2 == 0:
                split_w1(i // 2, k)

        def take_w2(i, piece):
            if i % 2 == 0:
                split_w2(i // 2, piece)

        def fetch_gates(i):
            x, h = i // 2, i % 2
            pool.wait(done["gates"], gg.idle(i))
            for c in range(C):
                col = idx[x][:, h * C + c:h * C + c + 1]
                done["gg", i] = core.lane(f"gg{i % 4}").send(pool, lambda e, c=c, col=col: e.indirect_dma_start(
                    gg[i][:, c, :], None, g["gate_dram"], bass.IndirectOffsetOnAxis(ap=col, axis=0)))

        def turn(i):
            for k in range(KD):
                n = KD * i + k
                t = transpose_into(core, banks[k], C, lambda c, k=k: xg[i][:, c, k * P:(k + 1) * P], ident, [done["xg", i], banks.idle(k)])
                a = act.do(lambda e, k=k, n=n: e.copy(xg_full[n][:, :], banks[k][:, :]), t, xg_full.idle(n))
                banks.used(k, a)
                b = split(core, xg_full[n][:, :], xgT[i][:, k, :], dve, a, xgT.idle(i))
                xg_full.used(n, b)
            xg.used(i, t)
            done["xgT", i] = b

        def take_apart(i, f):
            n = KF * i + f
            done["hidden", i] = split(core, hidden_full[n][:, :], hidden[i][:, f, :], dve, done["h", n], hidden.idle(i))
            hidden_full.used(n, done["hidden", i])

        def expand(i, fs):
            x = i // 2
            for f in fs:
                u, n = 4 + f % 2, KF * i + f
                for k in range(KD):
                    for j, (w, h) in enumerate(w1[x][:, k, f * P:(f + 1) * P].pairs(xgT[i][:, k, :])):
                        m = pe.do(lambda e, w=w, h=h, u=u, first=k + j == 0, final=k == KD - 1 and j == 2: e.matmul(
                            banks[u][:, :], w, h, start=first, stop=final), done["xgT", i], done["w1", x], banks.idle(u))
                a = act.do(lambda e, f=f, u=u, n=n: e.activation(hidden_full[n][:, :], banks[u][:, :], ACT.Gelu, bias=b1[:, x, f:f + 1]),
                           m, hidden_full.idle(n))
                banks.used(u, a)
                done["h", n] = a
                if f > 0:
                    take_apart(i, f - 1)
            if f == KF - 1:
                take_apart(i, f)
                xgT.used(i, m)
                w1.used(x, m)

        def contract(i, c):
            x, h = i // 2, i % 2
            u = 6 + c % 2
            chunk = slice(c * P, (c + 1) * P)
            pe.wait(done["hidden", i], done["w2", x], banks.idle(u))
            for f in range(KF):
                for j, (h_, w) in enumerate(hidden[i][:, f, chunk].pairs(w2[x][:, f, :])):
                    final = f == KF - 1 and j == 2
                    step = (lambda e, h_=h_, w=w, first=f + j == 0, final=final: e.matmul(banks[u][:, 0:D], h_, w, start=first, stop=final))
                    if final:
                        m = pe.do(step)
                    else:
                        pe.quiet(step)
            a = act.do(lambda e: e.activation(ys[i][:, c, :], banks[u][:, 0:D], ACT.Copy, scale=gg[i][:, c, x:x + 1]), m, done["gg", i], ys.idle(i))
            banks.used(u, a)
            if c == C - 1:
                hidden.used(i, m)
                w2.used(x, m)
                done["gated", i] = a

        def add_bias(i):
            x = i // 2
            dve.wait(done["gated", i], done["b2", x], done["gg", i])
            for c in range(C):
                a = dve.do(lambda e, c=c: e.scalar_tensor_tensor(out=ys[i][:, c, :], in0=b2_row[x][:, :], scalar=gg[i][:, c, x:x + 1],
                                                                 in1=ys[i][:, c, :], op0=ALU.mult, op1=ALU.add))
            b2_row.used(x, a)
            gg.used(i, a)
            done["ys", i] = a

        def scatter(i):
            x, h = i // 2, i % 2
            pool.wait(done["ys", i], done.get(("sc", 2 * x - 1)), done.get(("sc", 2 * x - 2)))
            for c in range(C):
                col = idx[x][:, h * C + c:h * C + c + 1]
                done["sc", i] = core.lane(f"sc{i % 4}").send(pool, lambda e, c=c, col=col: e.indirect_dma_start(
                    g["moe_dram"], bass.IndirectOffsetOnAxis(ap=col, axis=0), ys[i][:, c, :], None, compute_op=ALU.add))
            ys.used(i, done["sc", i])
            if h == 1:
                idx.used(x, done["sc", i], done["sc", i - 1])

        pipeline(NI, [
            (next_weights, 3), (fetch_gates, 3), (turn, 4),
            (part_of(listing, 3), 1), (fetch, 2), (part_of(contract, 0), 5), (part_of(take_w1, 0), 4), (part_of(mark, 0), 0),
            (part_of(contract, 1), 5), (part_of(take_w1, 1), 4), (part_of(mark, 1), 0), (part_of(contract, 2), 5),
            (part_of(listing, 0), 0), (part_of(mark, 2), 0), (part_of(contract, 3), 5), (part_of(listing, 1), 0), (add_bias, 5),
            (part_of(expand, (0, 1)), 4), (part_of(take_w2, 0), 4), (part_of(mark, 3), 0), (part_of(expand, (2,)), 4), (scatter, 5),
            (part_of(listing, 2), 0), (part_of(expand, (3, 4, 5)), 4), (part_of(take_w2, 1), 4), (part_of(expand, (6, 7)), 4),
        ])
        core.everyone_waits_for_everyone()


def layer_one(core, A, g):
    pe, act, dve, pool, sp = core.engines
    banks, ident, cols = core.banks, g["ident"], g["cols"]
    B, S, D, T, KD, H, KW, TT, NT = (g[n] for n in ("B", "S", "D", "T", "KD", "HEADS", "KW", "TILE_T", "NT"))
    F = A["L1_ffn_W1"].shape[1]
    KF = F // P
    C = S // P
    HC = C // 2
    QC = HC // 2
    QT = QC * P
    HD = D // H
    PAD = P - TT
    HJ = P // HD
    BC = 4
    x1_dram = g["x1_dram"].rearrange("(b c p) d -> b p c d", c=C, p=P)
    moe_dram = g["moe_dram"].rearrange("(b c p) d -> b p c d", c=C, p=P)
    out_dram = g["out"].rearrange("b (c p) d -> b c p d", p=P)

    with ExitStack() as part:
        def tile(name, shape, dt=F32):
            return core.tile(part, name, shape, dt)

        def ring(name, n, shape):
            return core.ring(part, name, n, shape)

        w_fc = tile("w_fc", [P, KD, D])
        w1, w2 = core.split_tile(part, "l1_w1", [P, KD, F]), core.split_tile(part, "l1_w2", [P, KF, D])
        w_pe = tile("w_pe", [P, 2, HJ, KW])
        pe_bias, energy = tile("pe_bias", [P, 2, KW]), tile("energy", [P, H, KW])
        b1, per_count = tile("l1_b1", [P, KF]), tile("per_count", [P, S])
        x2, moe, v = (ring(n, k, [P, HC, D]) for n, k in (("x2_", 7), ("moe", 2), ("l1_v", 2)))
        xh = moe
        h4T, h_full = core.split_ring(part, "h4T", 1, [P, KD, BANK]), ring("l1_h_full", 1, [P, BANK])
        hidden, hidden_full = core.split_ring(part, "l1_hidden", 1, [P, KF, QT]), ring("l1_hidden_full", 3, [P, QT])
        row_in, row_mid, row_out = ring("row_in", 1, [P, D]), ring("row_mid", 1, [P, 2, D]), ring("row_out", 1, [P, 2, D])
        h3T, avgT = ring("h3T", 2, [P, KD, S]), ring("avgT", 2, [P, KD, PAD + S + PAD])
        CIRCLE = 3 * P
        assert CIRCLE == 4 * TT
        convT = tile("convT", [P, KD, CIRCLE])
        pc, w = ring("pc", 3, [P, 2, H, KW]), ring("w", 2, [P, KW, H])
        top, total = ring("top", 2, [P, H]), ring("total", 2, [P, H])
        band, bandT = ring("band", 2, [TT, P, H]), ring("bandT", 2, [P, H, TT])
        window, conv = ring("window", 2, [P, D]), ring("conv", 2, [TT, D])
        o = ring("o", 2, [P, D])
        stats, moments, scratch = tile("l1_stats", [P, HC, 6]), tile("l1_moments", [P, HC, 2]), tile("l1_scratch", [P, 4, HC])
        small_bank, expand_bank, contract_bank = (Ring([banks[u] for u in us]) for us in ((0, 1, 2, 3), (4, 5), (6, 7)))
        uses = [0]

        def take():
            uses[0] += 1
            return uses[0]

        a = pool.do(lambda e: e.memset(w_pe[:, :, :, :], 0.0))
        lane = core.lane("l1_weights")
        loads = [(w_fc[:, :, :], A["L1_attn_W_fcT"].rearrange("(k p) n -> p k n", p=P)),
                 (pe_bias[:, :, :].rearrange("p a k -> p (a k)"), A["L1_attn_b_pe"].rearrange("(a d) -> a d", a=1).to_broadcast([P, 2 * KW])),
                 (energy[:, :, :].rearrange("p h k -> p (h k)"), A["L1_attn_stt_energy"].rearrange("a h b k -> (a b) (h k)").to_broadcast([P, H * KW])),
                 (b1[:, :], A["L1_ffn_b1_c"]), (per_count[:, :], A["per_count"].to_broadcast([P, S]))]
        loads += [(w_pe[j * HD:(j + 1) * HD, :, j, :], A["L1_attn_W_pe"].rearrange("d (a k) -> d a k", a=2)) for j in range(HJ)]
        for dst, src in loads:
            weights = lane.send(sp, lambda e, dst=dst, src=src: e.dma_start(dst, src), a)
        w1_rows, w2_rows = (A[n].rearrange("(k p) n -> p k n", p=P) for n in ("L1_ffn_W1", "L1_ffn_W2"))
        quarters = [(w1[:, k:k + 1, :], w1_rows[:, k:k + 1, :], F) for k in range(KD)]
        quarters += [(w2[:, k:k + KF // 2, :], w2_rows[:, k:k + KF // 2, :], D) for k in (0, KF // 2)]
        for n, (parts, src, width) in enumerate(quarters):
            full = x2[n + 3][:, :, :].rearrange("p c d -> p (c d)").rearrange("p (k n) -> p k n", n=width)
            got = core.lane(f"l1_mlp{n}").send(sp, lambda e, full=full, src=src: e.dma_start(full, src))
            mlp_weights = split(core, full, parts, dve, got)
            x2.used(n + 3, mlp_weights)
        for i in range(2):
            pool.quiet(lambda e, i=i: e.memset(avgT[i][:, :, 0:PAD], 0.0))
            pads_ready = pool.do(lambda e, i=i: e.memset(avgT[i][:, :, PAD + S:], 0.0))
        done = {}

        def load(b, half):
            n = 2 * b + half
            cs = slice(half * HC, (half + 1) * HC)
            if half == 0:
                done["row_in", b] = core.lane("row_in").send(sp, lambda e: e.dma_start(
                    row_in[b][:, :], g["row1_dram"][b:b + 1, 0:D].to_broadcast([P, D])), row_in.idle(b))
            done["x1", n] = core.lane(f"l1_x{n % 7}").send(sp, lambda e: e.dma_start(x2[n][:, :, :], x1_dram[b][:, cs, :]), x2.idle(n))
            done["moe", n] = core.lane(f"l1_moe{n % 2}").send(sp, lambda e: e.dma_start(moe[n][:, :, :], moe_dram[b][:, cs, :]), moe.idle(n))

        def join(b, half):
            n = 2 * b + half
            bc = row_in[b][:, :].unsqueeze(1).to_broadcast([P, HC, D])
            done["gained", n] = pool.do(lambda e: e.tensor_tensor(moe[n][:, :, :], moe[n][:, :, :], bc, ALU.mult), done["moe", n], done["row_in", b])
            if half == 1:
                row_in.used(b, done["gained", n])

        def norm_in(b, half):
            n = 2 * b + half
            a = dve.do(lambda e: e.tensor_tensor(x2[n][:, :, :], x2[n][:, :, :], moe[n][:, :, :], ALU.add), done["gained", n], done["x1", n])
            y, a = statistics(core, stats, moments, lambda c: x2[n][:, c, :], HC, 1e-5, scratch, a)
            dve.wait(a)
            for c in range(HC):
                a = dve.do(lambda e, c=c: e.tensor_scalar(xh[n][:, c, :], x2[n][:, c, :], moments[:, c, 0:1], y[:, c:c + 1], ALU.subtract, ALU.mult))
            done["xh", n] = a

        def to_features(b, half, source, ready, target, scale, shift, free):
            for k in range(KD):
                u = take()
                t = transpose_into(core, small_bank[u], HC, lambda c, k=k: source[:, c, k * P:(k + 1) * P], ident, [ready, small_bank.idle(u)])
                a = act.do(lambda e, k=k, u=u: e.activation(target(k), small_bank[u][:, :], ACT.Identity, scale=cols[:, g[scale] + k, b:b + 1],
                                                            bias=cols[:, g[shift] + k, b:b + 1]), t, free)
                small_bank.used(u, a)
            return t, a

        def turn_in(b, half):
            n = 2 * b + half
            t, a = to_features(b, half, xh[n], done["xh", n], lambda k: h3T[b][:, k, half * BANK:(half + 1) * BANK], "SCALE1A", "SHIFT1A", h3T.idle(b))
            xh.used(n, t)
            done["h3T", b] = a

        def average(b, k):
            view = avgT[b][:, k, PAD:PAD + S]
            a = dve.do(lambda e: e.tensor_tensor_scan(view, h3T[b][:, k, :], g["zero"][:, 0:1].to_broadcast([P, S]), 0.0, ALU.add, ALU.add),
                       done["h3T", b], avgT.idle(b), weights)
            done["avgT", b] = dve.do(lambda e: e.tensor_tensor(view, view, per_count[:, :], ALU.mult), a)

        def kernel_product(b, c, j):
            n, u = b * C + c, take()
            m = pe.do(lambda e: e.matmul(small_bank[u][:, 0:2 * HJ * KW], avgT[b][:, j, PAD + c * P:PAD + (c + 1) * P],
                                         w_pe[:, :, :, :].rearrange("p a j k -> p (a j k)"), start=True, stop=True),
                      done["avgT", b], weights, small_bank.idle(u))
            a = act.do(lambda e: e.copy(pc[n][:, :, j * HJ:(j + 1) * HJ, :],
                                        small_bank[u][:, 0:2 * HJ * KW].rearrange("p (a j k) -> p a j k", a=2, j=HJ)), m, pc.idle(n))
            small_bank.used(u, a)
            done["product", n] = a

        def kernel_bias(b, c):
            n = b * C + c
            done["pc", n] = dve.do(lambda e: e.tensor_tensor(
                pc[n][:, :, :, :], pc[n][:, :, :, :], pe_bias[:, :, :].unsqueeze(2).to_broadcast([P, 2, H, KW]), ALU.add), done["product", n])

        def gate(b, c):
            n = b * C + c
            done["gate", n] = act.do(lambda e: e.activation(pc[n][:, 1, :, :], pc[n][:, 1, :, :], ACT.Tanh, scale=0.5), done["pc", n])

        def energies(b, c):
            n = b * C + c
            e1 = pc[n][:, 0, :, :]
            a = dve.do(lambda e: e.scalar_tensor_tensor(out=e1, in0=pc[n][:, 1, :, :], scalar=1.0, in1=e1,
                                                        op0=ALU.add, op1=ALU.mult), done["gate", n])
            a = dve.do(lambda e: e.scalar_tensor_tensor(out=e1, in0=e1, scalar=0.5, in1=energy[:, :, :],
                                                        op0=ALU.mult, op1=ALU.add), a)
            a = dve.do(lambda e: e.tensor_reduce(top[n][:, :], e1, AX_X, ALU.max), a, top.idle(n))
            a = dve.do(lambda e: e.tensor_tensor(e1, e1, top[n][:, :].unsqueeze(2).to_broadcast([P, H, KW]), ALU.subtract), a)
            top.used(n, a)
            done["energy", n] = a

        def exponentials(b, c):
            n = b * C + c
            done["exp", n] = act.do(lambda e: e.activation(pc[n][:, 0, :, :], pc[n][:, 0, :, :], ACT.Exp), done["energy", n])

        def softmax(b, c):
            n = b * C + c
            a = dve.do(lambda e: e.tensor_reduce(total[n][:, :], pc[n][:, 0, :, :], AX_X, ALU.add), done["exp", n])
            a = dve.do(lambda e: e.reciprocal(total[n][:, :], total[n][:, :]), a)
            a = dve.do(lambda e: e.tensor_tensor(w[n][:, :, :].rearrange("p k h -> p h k"), pc[n][:, 0, :, :],
                                                 total[n][:, :].unsqueeze(2).to_broadcast([P, H, KW]), ALU.mult), a, w.idle(n))
            pc.used(n, a)
            row = (P + 1) * H
            t = c * P
            while t < (c + 1) * P:
                i, tt = t // TT, t % TT
                rows = min(TT - tt, (c + 1) * P - t)
                off = tt * row + (PAD - KW + 1) * H
                dst = g["band_dram"][b % 2][i:i + 1, off:off + rows * row].rearrange("a (n r) -> (a n) r", r=row)[:, 0:KW * H]
                src = w[n][t - c * P:t - c * P + rows, :, :].rearrange("p k h -> p (k h)")
                sent = core.lane(f"w{n % 2}").send(sp, lambda e, dst=dst, src=src: e.dma_start(dst, src), a, done.get(("band", b - 2, i)))
                t += rows
            w.used(n, sent)
            done["w", b, c] = sent

        def load_band(n):
            b, i = divmod(n, NT)
            if b == B:
                return
            chunks = range(i * TT // P, min(C - 1, (i * TT + TT - 1) // P) + 1)
            done["band", b, i] = core.lane(f"band{n % 2}").send(sp, lambda e: e.dma_start(
                band[n][:, :, :].rearrange("t s h -> t (s h)"), g["band_dram"][b % 2][i:i + 1, 0:TT * P * H].rearrange("a (t r) -> (a t) r", t=TT)),
                band.idle(n), *[done["w", b, c] for c in chunks])

        def band_turn(b, i, qs):
            n = b * NT + i
            for q in qs:
                u = take()
                for j in range(BC):
                    h = q * BC + j
                    step = lambda e, h=h, j=j, u=u: e.transpose(small_bank[u][:, j * TT:(j + 1) * TT], band[n][:, :, h], ident[0:TT, 0:TT])
                    if j < BC - 1:
                        pe.quiet(step, done["band", b, i], small_bank.idle(u))
                    else:
                        t = pe.do(step)
                a = act.do(lambda e, q=q, u=u: e.copy(bandT[n][:, q * BC:(q + 1) * BC, :].rearrange("p h t -> p (h t)"), small_bank[u][:, 0:BC * TT]),
                           t, bandT.idle(n))
                small_bank.used(u, a)
            done["bandT", n] = a
            if qs[-1] == H // BC - 1:
                band.used(n, t)
                load_band(n + 2)

        def window_turn(b, i):
            n, u = b * NT + i, take()
            for k in range(KD):
                t = pe.do(lambda e, k=k: e.transpose(small_bank[u][:, k * P:(k + 1) * P], avgT[b][:, k, i * TT:i * TT + P], ident[:, :]),
                          small_bank.idle(u), pads_ready)
            if i == NT - 1:
                avgT.used(b, t)
            a = act.do(lambda e: e.copy(window[n][:, :], small_bank[u][:, 0:D]), t, window.idle(n))
            small_bank.used(u, a)
            done["window", n] = a

        def band_product(b, i):
            n, u = b * NT + i, take()
            for h in range(H):
                step = lambda e, h=h: e.matmul(small_bank[u][0:TT, h * HD:(h + 1) * HD], bandT[n][:, h, :], window[n][:, h * HD:(h + 1) * HD],
                                               start=True, stop=True)
                if h < H - 1:
                    pe.quiet(step, done["bandT", n], done["window", n], small_bank.idle(u))
                else:
                    m = pe.do(step)
            bandT.used(n, m)
            window.used(n, m)
            a = act.do(lambda e: e.copy(conv[n][:, :], small_bank[u][0:TT, 0:D]), m, conv.idle(n))
            small_bank.used(u, a)
            done["conv", n] = a

        def conv_turn(b, i):
            n, u = b * NT + i, take()
            size = min(TT, S - i * TT)
            for k in range(KD):
                t = pe.do(lambda e, k=k: e.transpose(small_bank[u][:, k * TT:(k + 1) * TT], conv[n][:, k * P:(k + 1) * P], ident[0:TT, 0:TT]),
                          done["conv", n], small_bank.idle(u))
            conv.used(n, t)
            before = done.get(("mixed", b, ((i - 4) * TT + TT - 1) // P) if i >= 4 else ("mixed", b - 1, C - 1))
            place = i * TT % CIRCLE
            a = act.do(lambda e: e.copy(convT[:, :, place:place + size],
                                        small_bank[u][:, 0:KD * TT].rearrange("p (k t) -> p k t", k=KD)[:, :, 0:size]), t, before)
            small_bank.used(u, a)
            done["convT", b] = a

        def mix(b, c):
            n, u = 2 * b + c // HC, take()
            for k in range(KD):
                pe.quiet(lambda e, k=k: e.matmul(small_bank[u][:, 0:D], convT[:, k, c * P % CIRCLE:c * P % CIRCLE + P], w_fc[:, k, :], start=k == 0, stop=False),
                         done["convT", b], small_bank.idle(u))
            for k in range(KD):
                m = pe.do(lambda e, k=k: e.matmul(small_bank[u][:, k * P:(k + 1) * P], h3T[b][:, k, c * P:(c + 1) * P], ident[:, :],
                                                  start=False, stop=k == KD - 1))
            a = act.do(lambda e: e.copy(v[n][:, c % HC, :], small_bank[u][:, 0:D]), m, v.idle(n))
            small_bank.used(u, a)
            done["v", n] = a
            done["mixed", b, c] = m
            if c == C - 1:
                h3T.used(b, m)

        def load_rows(b):
            done["row_mid", b] = core.lane("row_mid").send(sp, lambda e: e.dma_start(
                row_mid[b][:, :, :].rearrange("p a d -> p (a d)"), g["row1_dram"][b:b + 1, D:3 * D].to_broadcast([P, 2 * D])), row_mid.idle(b))

        def load_out_rows(b):
            done["row_out", b] = core.lane("row_out").send(sp, lambda e: e.dma_start(
                row_out[b][:, :, :].rearrange("p a d -> p (a d)"), g["row1_dram"][b:b + 1, 3 * D:5 * D].to_broadcast([P, 2 * D])), row_out.idle(b))

        def norm_mid_a(b, half):
            n = 2 * b + half
            y, a = statistics(core, stats, moments, lambda c: v[n][:, c, :], HC, 1e-6, scratch, done["v", n])
            dve.wait(a)
            for c in range(HC):
                a = dve.do(lambda e, c=c: e.tensor_scalar(v[n][:, c, :], v[n][:, c, :], moments[:, c, 0:1], y[:, c:c + 1], ALU.subtract, ALU.mult))
            bc = lambda r: row_mid[b][:, r:r + 1, :].to_broadcast([P, HC, D])
            pool.do(lambda e: e.tensor_tensor(x2[n][:, :, :], x2[n][:, :, :], bc(1), ALU.add), done["row_mid", b], done["xh", n])
            a = pool.do(lambda e: e.tensor_tensor(v[n][:, :, :], v[n][:, :, :], bc(0), ALU.mult), a)
            if half == 1:
                row_mid.used(b, a)
            done["mid", n] = a

        def norm_mid_b(b, half):
            n = 2 * b + half
            a = dve.do(lambda e: e.tensor_tensor(x2[n][:, :, :], x2[n][:, :, :], v[n][:, :, :], ALU.add), done["mid", n])
            y, a = statistics(core, stats, moments, lambda c: x2[n][:, c, :], HC, 1e-5, scratch, a)
            dve.wait(a)
            for c in range(HC):
                a = dve.do(lambda e, c=c: e.tensor_scalar(v[n][:, c, :], x2[n][:, c, :], moments[:, c, 0:1], y[:, c:c + 1], ALU.subtract, ALU.mult))
            done["h4", n] = a

        def turn_mid(b, half):
            n = 2 * b + half
            for k in range(KD):
                u, m = take(), KD * n + k
                t = transpose_into(core, small_bank[u], HC, lambda c, k=k: v[n][:, c, k * P:(k + 1) * P], ident, [done["h4", n], small_bank.idle(u)])
                a = act.do(lambda e, k=k, u=u, m=m: e.activation(h_full[m][:, :], small_bank[u][:, :], ACT.Identity, scale=cols[:, g["SCALE1B"] + k, b:b + 1],
                                                                 bias=cols[:, g["SHIFT1B"] + k, b:b + 1]), t, h_full.idle(m))
                small_bank.used(u, a)
                a = split(core, h_full[m][:, :], h4T[n][:, k, :], dve, a, h4T.idle(n))
                h_full.used(m, a)
            v.used(n, t)
            done["h4T", n] = a

        def take_apart(b, quarter, f):
            q = 4 * b + quarter
            n = KF * q + f
            done["hidden", q] = split(core, hidden_full[n][:, :], hidden[q][:, f, :], pool, done["relu", n], hidden.idle(q))
            hidden_full.used(n, done["hidden", q])

        def expand(b, quarter, f):
            q, h, u = 4 * b + quarter, 2 * b + quarter // 2, f
            n = KF * q + f
            tokens = slice(quarter % 2 * QT, (quarter % 2 + 1) * QT)
            pe.wait(done["h4T", h], mlp_weights, expand_bank.idle(u))
            for k in range(KD):
                for j, (w_, x_) in enumerate(w1[:, k, f * P:(f + 1) * P].pairs(h4T[h][:, k, tokens])):
                    m = pe.do(lambda e, w_=w_, x_=x_, first=k + j == 0, final=k == KD - 1 and j == 2: e.matmul(
                        expand_bank[u][:, 0:QT], w_, x_, start=first, stop=final))
            a = act.do(lambda e: e.activation(hidden_full[n][:, :], expand_bank[u][:, 0:QT], ACT.Relu, bias=b1[:, f:f + 1]), m, hidden_full.idle(n))
            expand_bank.used(u, a)
            done["relu", n] = a
            if f > 0:
                take_apart(b, quarter, f - 1)
            if f == KF - 1:
                take_apart(b, quarter, f)
                if quarter % 2 == 1:
                    h4T.used(h, m)

        def row_gain(b, half):
            n = 2 * b + half
            bc = row_out[b][:, 1:2, :].to_broadcast([P, HC, D])
            done["x3", n] = pool.do(lambda e: e.tensor_tensor(x2[n][:, :, :], x2[n][:, :, :], bc, ALU.add), done["row_out", b], done["h4", n])

        def contract(b, quarter, c):
            q, n, u = 4 * b + quarter, 2 * b + quarter // 2, c
            place = quarter % 2 * QC + c
            pe.wait(done["hidden", q], contract_bank.idle(u))
            for f in range(KF):
                for j, (x_, w_) in enumerate(hidden[q][:, f, c * P:(c + 1) * P].pairs(w2[:, f, :])):
                    m = pe.do(lambda e, x_=x_, w_=w_, first=f + j == 0, final=f == KF - 1 and j == 2: e.matmul(
                        contract_bank[u][:, 0:D], x_, w_, start=first, stop=final))
            if c == QC - 1:
                hidden.used(q, m)
            a = dve.do(lambda e: e.tensor_tensor(o[c][:, :], contract_bank[u][:, 0:D], row_out[b][:, 0, :], ALU.mult), m, done["row_out", b], o.idle(c))
            contract_bank.used(u, a)
            a = dve.do(lambda e: e.tensor_tensor(o[c][:, :], o[c][:, :], x2[n][:, place, :], ALU.add), a, done["x3", n])
            o.used(c, core.lane(f"out{c % 2}").send(sp, lambda e: e.dma_start(out_dram[b, quarter * QC + c], o[c][:, :]), a))
            if place == HC - 1:
                x2.used(n, a)
                if quarter == 3:
                    row_out.used(b, a)

        plan = []

        def at(place, lag, stage, *args):
            plan.append((place, len(plan), lambda b: stage(b, *args), lag))

        at(0.0, 3, load_out_rows)
        at(2.0, 2, load_rows)
        at(0.3, 0, load, 0)
        at(3.5, 0, join, 0)
        at(4.5, 0, norm_in, 0)
        at(6.9, 0, load, 1)
        at(8.5, 0, join, 1)
        at(10.0, 0, norm_in, 1)
        at(0.0, 1, turn_in, 0)
        at(0.15, 1, turn_in, 1)
        at(0.4, 1, average, 0)
        at(0.6, 1, average, 1)
        for c in range(C):
            start = 1.7 + 1.25 * c
            for j in range(KD):
                at(start + 0.4 * j, 1, kernel_product, c, j)
            at(start + 0.7, 1, kernel_bias, c)
            at(start + 1.3, 1, gate, c)
            at(start + 1.6, 1, energies, c)
            at(start + 2.1, 1, exponentials, c)
            at(start + 2.45, 1, softmax, c)
        at(6.0, 1, lambda b: [load_band(n) for n in range(2)] if b == 0 else None)
        mixed = 0
        for i in range(NT):
            at(i + 0.1, 2, band_turn, i, (0, 1))
            at(i + 0.4, 2, window_turn, i)
            at(i + 0.6, 2, band_turn, i, (2, 3))
            at(i + 1.2, 2, band_product, i)
            at(i + 1.7, 2, conv_turn, i)
            while mixed < C and (mixed + 1) * P <= (i + 1) * TT:
                at(i + 2.05, 2, mix, mixed)
                mixed += 1
        while mixed < C:
            at(NT + 1.3, 2, mix, mixed)
            mixed += 1
        at(7.4, 2, norm_mid_a, 0)
        at(8.8, 2, norm_mid_b, 0)
        at(11.7, 2, turn_mid, 0)
        at(0.2, 3, norm_mid_a, 1)
        at(1.7, 3, norm_mid_b, 1)
        at(5.1, 3, turn_mid, 1)
        at(0.9, 3, row_gain, 0)
        at(4.3, 3, row_gain, 1)
        for quarter in range(4):
            start = 3.25 * quarter + 0.2
            for f in range(KF):
                at(start + 0.2 * f, 3, expand, quarter, f)
            for c in range(QC):
                at(start + 2.0 + 0.6 * c, 3, contract, quarter, c)
        pipeline(B, [(stage, lag) for _, _, stage, lag in sorted(plan, key=lambda z: z[:2])])
        core.everyone_waits_for_everyone()


def columns(vector):
    return vector.reshape(-1, P).T


def kernel(**inputs):
    import numpy as np
    import concourse.bacc as bacc
    from concourse.bass_utils import run_bass_kernel_spmd

    x = {name: np.asarray(a) for name, a in inputs.items()}
    B, S, D = x["L0_attn_x"].shape
    E = x["L0_ffn_router_weight"].shape[0]
    keep = ["L0_attn_x", "L0_attn_W_ret", "L0_attn_W1", "L0_attn_W2", "L0_attn_b2", "L0_attn_ln2_scale", "L0_attn_ln2_bias",
            "L0_ffn_norm_weight", "L0_ffn_router_bias", "L0_ffn_router_weight", "L0_ffn_fc2_bias", "L0_wmod", "L1_wmod",
            "L1_attn_W_pe", "L1_attn_b_pe", "L1_attn_stt_energy", "L1_attn_gamma", "L1_attn_beta", "L1_ffn_W1", "L1_ffn_W2", "L1_ffn_b2"]
    arrays = {n: x[n] for n in keep}
    arrays["L0_cT"], arrays["L1_cT"] = x["L0_c"].T, x["L1_c"].T
    arrays["L0_ffn_router_wT"] = x["L0_ffn_router_weight"].T
    arrays["L0_ffn_fc1_wT"] = x["L0_ffn_fc1_weight"].transpose(0, 2, 1)
    arrays["L0_ffn_fc2_wT"] = x["L0_ffn_fc2_weight"].transpose(0, 2, 1)
    arrays["L1_attn_W_fcT"] = x["L1_attn_W_fc"].T
    for n in ("L0_attn_b_ret", "L0_attn_ln1_scale", "L0_attn_ln1_bias", "L0_attn_b1", "L0_ffn_fc1_bias", "L1_ffn_b1"):
        arrays[n + "_c"] = columns(x[n])
    p = np.arange(P)
    G = P // E
    same = p[:, None] // G == p[None, :] // G
    arrays["block_ones"] = same.astype(np.float32)
    arrays["block_below"] = (same & (p[:, None] < p[None, :])).astype(np.float32)
    arrays["iota_row"] = np.tile(p.astype(np.float32), (P, 1))
    arrays["iota_column"] = p.astype(np.float32).reshape(P, 1)
    c, gr = np.divmod(np.arange(P), G)
    arrays["chunk_ids"] = np.tile((gr * (B * S // G // P) + c).astype(np.float32), (P, 1))
    arrays["per_count"] = (np.float32(1) / np.arange(1, S + 1, dtype=np.float32)).reshape(1, S)

    nc = bacc.Bacc("TRN2", target_bir_lowering=False, num_devices=1)
    feed, A = {}, {}
    for name, a in arrays.items():
        a = np.ascontiguousarray(a)
        feed[f"in_{name}"] = a
        A[name] = nc.dram_tensor(f"in_{name}", a.shape, mybir.dt.from_np(a.dtype), kind="ExternalInput").ap()
    out = nc.dram_tensor("out", (B, S, D), F32, kind="ExternalOutput").ap()
    build(nc, A, out)
    r = run_bass_kernel_spmd(nc, [feed], core_ids=[0])
    return r.results[0]["out"]
```
